# Optimizing a Trainium2 kernel written in Bass

```python
import numpy as np
import jax
import jax.numpy as jnp

def _softmax(x, axis=-1):
    return jax.nn.softmax(x, axis=axis)

def _gelu(x):
    return jax.nn.gelu(x, approximate=True)

def _silu(x):
    return jax.nn.silu(x)

def _sigmoid(x):
    return jax.nn.sigmoid(x)

def _layernorm(x, axis=-1, eps=1e-05):
    m = jnp.mean(x, axis=axis, keepdims=True)
    v = jnp.var(x, axis=axis, keepdims=True)
    return (x - m) / jnp.sqrt(v + eps)

def _scatter_add(tgt, idx, src, axis=0):
    return tgt.at[idx].add(src)

def _segment_sum(src, seg, n):
    return jax.ops.segment_sum(src, seg, n)
kernel_name = 'mk_hybrid_d1_jaxref_r8_3297d6'

def setup_inputs(seed: int=0):
    np.random.seed(seed)
    _w = jnp.asarray

    def _L0_attn_a_setup():
        import jax, jax.numpy as jnp
        import numpy as np
        D_MODEL = 128
        N_HEADS = 16
        D_HEAD = D_MODEL // N_HEADS
        BATCH = 2
        SEQ = 256
        key = jax.random.key(seed)
        ks = jax.random.split(key, 5)
        s = 1.0 / np.sqrt(D_MODEL)
        return {'x': jax.random.normal(ks[0], (BATCH, SEQ, D_MODEL), dtype=jnp.float32), 'W_qkv': jax.random.normal(ks[1], (3 * D_MODEL, D_MODEL), dtype=jnp.float32) * s, 'b_qkv': jax.random.normal(ks[2], (3 * D_MODEL,), dtype=jnp.float32) * 0.01, 'W_out': jax.random.normal(ks[3], (D_MODEL, D_MODEL), dtype=jnp.float32) * s, 'b_out': jax.random.normal(ks[4], (D_MODEL,), dtype=jnp.float32) * 0.01}
    _L0_attn_a_in = _L0_attn_a_setup()

    def _L0_attn_b_setup():
        import jax, jax.numpy as jnp
        import numpy as np
        N_HEADS = 16
        BUCKETS = 32
        MAX_REL = 64
        ATT_SPAN = BUCKETS
        LN_EPS = 1e-07

        def make_log_bucket_position(relative_pos, bucket_size, max_position):
            sign = jnp.sign(relative_pos)
            mid = bucket_size // 2
            abs_pos = jnp.where((relative_pos < mid) & (relative_pos > -mid), mid - 1, jnp.abs(relative_pos))
            log_pos = jnp.ceil(jnp.log(abs_pos / mid) / jnp.log((max_position - 1) / mid) * (mid - 1)) + mid
            bucket_pos = jnp.where(abs_pos <= mid, abs_pos, log_pos * sign)
            return bucket_pos.astype(jnp.int32)

        def build_relative_position(q_size, k_size, bucket_size, max_position):
            rel = jnp.arange(q_size)[:, None] - jnp.arange(k_size)[None, :]
            rel = make_log_bucket_position(rel, bucket_size, max_position)
            return rel.astype(jnp.int32)
        key = jax.random.key(seed)
        ks = jax.random.split(key, 16)
        B, S, H = (4, 128, 128)
        std = 0.02
        inp = {'hidden_states': jax.random.normal(ks[0], (B, S, H), jnp.float32), 'attention_mask': jnp.ones((B, S), jnp.float32), 'rel_embeddings': jax.random.normal(ks[1], (2 * ATT_SPAN, H), jnp.float32) * std, 'Wq': jax.random.normal(ks[2], (H, H), jnp.float32) * std, 'bq': jnp.zeros((H,), jnp.float32), 'Wk': jax.random.normal(ks[3], (H, H), jnp.float32) * std, 'bk': jnp.zeros((H,), jnp.float32), 'Wv': jax.random.normal(ks[4], (H, H), jnp.float32) * std, 'bv': jnp.zeros((H,), jnp.float32), 'Wo': jax.random.normal(ks[5], (H, H), jnp.float32) * std, 'bo': jnp.zeros((H,), jnp.float32), 'ln_scale': jnp.ones((H,), jnp.float32), 'ln_bias': jnp.zeros((H,), jnp.float32)}
        return inp
    _L0_attn_b_in = _L0_attn_b_setup()

    def _L0_ffn_setup():
        import jax, jax.numpy as jnp
        import numpy as np
        E = 8
        D = 128
        DO = 128
        R = 64
        H = 32
        B, T = (8, 256)
        key = jax.random.key(seed)
        ks = jax.random.split(key, 12)
        s = lambda k, shape, fan: jax.random.normal(k, shape, jnp.float32) / np.sqrt(fan)
        return {'x': jax.random.normal(ks[0], (B, T, D), jnp.float32), 'W_base': s(ks[1], (D, DO), D), 'b_base': jnp.zeros((DO,), jnp.float32), 'Wd1': s(ks[2], (E, D, H), D), 'bd1': jnp.zeros((E, H), jnp.float32), 'Wd2': s(ks[3], (E, H, D), H), 'bd2': jnp.zeros((E, D), jnp.float32), 'Wa_down': s(ks[4], (E, D, R), D), 'ba_down': jnp.zeros((E, R), jnp.float32), 'Wa_up': s(ks[5], (E, R, DO), R), 'ba_up': jnp.zeros((E, DO), jnp.float32)}
    _L0_ffn_in = _L0_ffn_setup()
    _d = {'L0_attn_a_x': _L0_attn_a_in['x'], 'L0_attn_a_W_qkv': _L0_attn_a_in['W_qkv'], 'L0_attn_a_b_qkv': _L0_attn_a_in['b_qkv'], 'L0_attn_a_W_out': _L0_attn_a_in['W_out'], 'L0_attn_a_b_out': _L0_attn_a_in['b_out'], 'L0_attn_b_attention_mask': _L0_attn_b_in['attention_mask'], 'L0_attn_b_rel_embeddings': _L0_attn_b_in['rel_embeddings'], 'L0_attn_b_Wq': _L0_attn_b_in['Wq'], 'L0_attn_b_bq': _L0_attn_b_in['bq'], 'L0_attn_b_Wk': _L0_attn_b_in['Wk'], 'L0_attn_b_bk': _L0_attn_b_in['bk'], 'L0_attn_b_Wv': _L0_attn_b_in['Wv'], 'L0_attn_b_bv': _L0_attn_b_in['bv'], 'L0_attn_b_Wo': _L0_attn_b_in['Wo'], 'L0_attn_b_bo': _L0_attn_b_in['bo'], 'L0_attn_b_ln_scale': _L0_attn_b_in['ln_scale'], 'L0_attn_b_ln_bias': _L0_attn_b_in['ln_bias'], 'L0_ffn_W_base': _L0_ffn_in['W_base'], 'L0_ffn_b_base': _L0_ffn_in['b_base'], 'L0_ffn_Wd1': _L0_ffn_in['Wd1'], 'L0_ffn_bd1': _L0_ffn_in['bd1'], 'L0_ffn_Wd2': _L0_ffn_in['Wd2'], 'L0_ffn_bd2': _L0_ffn_in['bd2'], 'L0_ffn_Wa_down': _L0_ffn_in['Wa_down'], 'L0_ffn_ba_down': _L0_ffn_in['ba_down'], 'L0_ffn_Wa_up': _L0_ffn_in['Wa_up'], 'L0_ffn_ba_up': _L0_ffn_in['ba_up']}
    _x0 = _d['L0_attn_a_x']
    _d['L0_attn_a_x'] = jax.random.normal(jax.random.fold_in(jax.random.key(seed), 1), (8, 256, 128), dtype=_x0.dtype)
    del _x0
    return _d

def reference(L0_attn_a_x, L0_attn_a_W_qkv, L0_attn_a_b_qkv, L0_attn_a_W_out, L0_attn_a_b_out, L0_attn_b_attention_mask, L0_attn_b_rel_embeddings, L0_attn_b_Wq, L0_attn_b_bq, L0_attn_b_Wk, L0_attn_b_bk, L0_attn_b_Wv, L0_attn_b_bv, L0_attn_b_Wo, L0_attn_b_bo, L0_attn_b_ln_scale, L0_attn_b_ln_bias, L0_ffn_W_base, L0_ffn_b_base, L0_ffn_Wd1, L0_ffn_bd1, L0_ffn_Wd2, L0_ffn_bd2, L0_ffn_Wa_down, L0_ffn_ba_down, L0_ffn_Wa_up, L0_ffn_ba_up):

    def _L0_attn_a_ref(x, W_qkv, b_qkv, W_out, b_out):
        import jax, jax.numpy as jnp
        import numpy as np
        D_MODEL = 128
        N_HEADS = 16
        D_HEAD = D_MODEL // N_HEADS
        BATCH = 2
        SEQ = 256
        b, s, d = x.shape
        qkv = x @ W_qkv.T + b_qkv
        qkv = qkv.reshape(b, s, N_HEADS, 3 * D_HEAD)
        q = qkv[..., :D_HEAD]
        k = qkv[..., D_HEAD:2 * D_HEAD]
        v = qkv[..., 2 * D_HEAD:]
        scale = np.sqrt(D_HEAD).astype(np.float32)
        scores = jnp.einsum('bqhd,bkhd->bhqk', q, k) / scale
        attn = jax.nn.softmax(scores, axis=-1)
        out = jnp.einsum('bhqk,bkhd->bqhd', attn, v)
        out = out.reshape(b, s, d)
        return out @ W_out.T + b_out

    def _L0_attn_b_ref(hidden_states, attention_mask, rel_embeddings, Wq, bq, Wk, bk, Wv, bv, Wo, bo, ln_scale, ln_bias):
        import jax, jax.numpy as jnp
        import numpy as np
        N_HEADS = 16
        BUCKETS = 32
        MAX_REL = 64
        ATT_SPAN = BUCKETS
        LN_EPS = 1e-07

        def make_log_bucket_position(relative_pos, bucket_size, max_position):
            sign = jnp.sign(relative_pos)
            mid = bucket_size // 2
            abs_pos = jnp.where((relative_pos < mid) & (relative_pos > -mid), mid - 1, jnp.abs(relative_pos))
            log_pos = jnp.ceil(jnp.log(abs_pos / mid) / jnp.log((max_position - 1) / mid) * (mid - 1)) + mid
            bucket_pos = jnp.where(abs_pos <= mid, abs_pos, log_pos * sign)
            return bucket_pos.astype(jnp.int32)

        def build_relative_position(q_size, k_size, bucket_size, max_position):
            rel = jnp.arange(q_size)[:, None] - jnp.arange(k_size)[None, :]
            rel = make_log_bucket_position(rel, bucket_size, max_position)
            return rel.astype(jnp.int32)
        B, S, H = hidden_states.shape
        nH = N_HEADS
        d = H // nH

        def split_heads(x):
            return jnp.transpose(x.reshape(B, S, nH, d), (0, 2, 1, 3))
        q = split_heads(hidden_states @ Wq + bq)
        k = split_heads(hidden_states @ Wk + bk)
        v = split_heads(hidden_states @ Wv + bv)
        scale_factor = 3
        scale = jnp.sqrt(jnp.asarray(d * scale_factor, hidden_states.dtype))
        scores = jnp.einsum('bhqd,bhkd->bhqk', q, k) / scale
        rel = build_relative_position(S, S, BUCKETS, MAX_REL)
        pos_k = (rel_embeddings @ Wk + bk).reshape(2 * ATT_SPAN, nH, d)
        pos_k = jnp.transpose(pos_k, (1, 0, 2))
        c2p_att = jnp.einsum('bhqd,hpd->bhqp', q, pos_k)
        c2p_pos = jnp.clip(rel + ATT_SPAN, 0, 2 * ATT_SPAN - 1)
        c2p = jnp.take_along_axis(c2p_att, jnp.broadcast_to(c2p_pos[None, None], (B, nH, S, S)), axis=-1)
        p2c_pos = jnp.clip(-rel + ATT_SPAN, 0, 2 * ATT_SPAN - 1)
        p2c_att = jnp.einsum('bhkd,hpd->bhkp', k, pos_k)
        p2c = jnp.take_along_axis(p2c_att, jnp.broadcast_to(p2c_pos[None, None], (B, nH, S, S)), axis=-1)
        p2c = jnp.swapaxes(p2c, -1, -2)
        scores = scores + (c2p + p2c) / scale
        probs = jax.nn.softmax(scores, axis=-1)
        ctx = jnp.einsum('bhqk,bhkd->bhqd', probs, v)
        ctx = jnp.transpose(ctx, (0, 2, 1, 3)).reshape(B, S, H)
        out = ctx @ Wo + bo + hidden_states
        mu = jnp.mean(out, axis=-1, keepdims=True)
        var = jnp.mean(jnp.square(out - mu), axis=-1, keepdims=True)
        out = (out - mu) * jax.lax.rsqrt(var + LN_EPS) * ln_scale + ln_bias
        return out

    def _L0_ffn_ref(x, W_base, b_base, Wd1, bd1, Wd2, bd2, Wa_down, ba_down, Wa_up, ba_up):
        import jax, jax.numpy as jnp
        import numpy as np
        E = 8
        D = 128
        DO = 128
        R = 64
        H = 32
        B, T = (8, 256)
        base = jnp.einsum('btd,do->bto', x, W_base) + b_base
        h = jax.nn.relu(jnp.einsum('btd,edh->ebth', x, Wd1) + bd1[:, None, None, :])
        recon = jnp.einsum('ebth,ehd->ebtd', h, Wd2) + bd2[:, None, None, :]
        losses = jnp.mean((recon - x[None]) ** 2, axis=(2, 3))
        idx = jnp.argmin(losses, axis=0)
        a = jax.nn.relu(jnp.einsum('btd,bdr->btr', x, Wa_down[idx]) + ba_down[idx][:, None, :])
        adapter_out = jnp.einsum('btr,bro->bto', a, Wa_up[idx]) + ba_up[idx][:, None, :]
        return base + adapter_out
    x = L0_attn_a_x
    x = x + _L0_attn_a_ref(_layernorm(x, axis=-1), L0_attn_a_W_qkv, L0_attn_a_b_qkv, L0_attn_a_W_out, L0_attn_a_b_out)
    x = x + _L0_ffn_ref(_layernorm(x, axis=-1), L0_ffn_W_base, L0_ffn_b_base, L0_ffn_Wd1, L0_ffn_bd1, L0_ffn_Wd2, L0_ffn_bd2, L0_ffn_Wa_down, L0_ffn_ba_down, L0_ffn_Wa_up, L0_ffn_ba_up)
    x = x + _L0_attn_b_ref(_layernorm(x, axis=-1), L0_attn_b_attention_mask, L0_attn_b_rel_embeddings, L0_attn_b_Wq, L0_attn_b_bq, L0_attn_b_Wk, L0_attn_b_bk, L0_attn_b_Wv, L0_attn_b_bv, L0_attn_b_Wo, L0_attn_b_bo, L0_attn_b_ln_scale, L0_attn_b_ln_bias)
    x = x + _L0_ffn_ref(_layernorm(x, axis=-1), L0_ffn_W_base, L0_ffn_b_base, L0_ffn_Wd1, L0_ffn_bd1, L0_ffn_Wd2, L0_ffn_bd2, L0_ffn_Wa_down, L0_ffn_ba_down, L0_ffn_Wa_up, L0_ffn_ba_up)
    return x

_drawn_inputs = setup_inputs


def setup_inputs(seed=0):
    import zlib

    import numpy as np

    out = dict(_drawn_inputs(seed))
    spreads = {'L0_attn_b_bq': (0.0, 0.8),
     'L0_attn_b_bk': (0.0, 0.8),
     'L0_attn_b_bv': (0.0, 0.8),
     'L0_attn_b_bo': (0.0, 0.1),
     'L0_attn_b_ln_scale': (1.0, 0.2),
     'L0_attn_b_ln_bias': (0.0, 0.1),
     'L0_ffn_b_base': (0.0, 0.1),
     'L0_ffn_bd1': (0.0, 0.1),
     'L0_ffn_bd2': (0.0, 0.1),
     'L0_ffn_ba_down': (0.0, 0.1),
     'L0_ffn_ba_up': (0.0, 0.1)}
    factors = {'L0_attn_b_rel_embeddings': 8.0,
     'L0_attn_b_Wq': 64.0,
     'L0_attn_b_Wk': 64.0,
     'L0_attn_a_b_qkv': 6.675,
     'L0_attn_a_b_out': 5.696,
     'L0_attn_b_Wv': 7.159,
     'L0_attn_b_Wo': 4.778}
    for name, (base, spread) in spreads.items():
        noise = np.random.default_rng([zlib.crc32(name.encode()), seed]).standard_normal(out[name].shape)
        drawn = base * np.exp(spread * noise) if base else spread * noise
        out[name] = jnp.asarray(drawn.astype(out[name].dtype))
    for name, factor in factors.items():
        out[name] = (out[name] * factor).astype(out[name].dtype)
    return out
```

```python
from contextlib import ExitStack

import numpy as np

import concourse.bass as bass
from concourse import mybir
from concourse.alu_op_type import AluOpType as ALU

F32 = mybir.dt.float32
BF16 = mybir.dt.bfloat16
ACT = mybir.ActivationFunctionType
AX = mybir.AxisListType

P = 128
D = 128
NH = 16
DH = D // NH
SEQ = 256
NB = 2
NT = NB * SEQ // P
TOK = NB * SEQ
HC = 4
NG = NB * 2
NCH = NG * NH // HC
BH = NB * NH
VC = 32
PARTS = 3
KS = PARTS * PARTS * DH
NE, HE, R = 8, 32, 64
SELW = R + D + 1
SPAN, MAX_REL = 32, 64
NIDX = 32
CEN_C, CEN_P = SPAN + SPAN // 2 - 1, SPAN - SPAN // 2 + 1
EPS_LN, EPS_B = 1e-5, 1e-7
SCALE_A = 1.0 / float(np.sqrt(np.float32(DH)))
SCALE_B = 1.0 / float(np.sqrt(np.float32(3 * DH)))
RELW = 2 * SEQ


def relative_buckets():
    rel = np.arange(-(SEQ - 1), SEQ)
    mid = SPAN // 2
    a = np.where((rel < mid) & (rel > -mid), mid - 1, np.abs(rel)).astype(np.float32)
    steps = np.log(a / np.float32(mid)) / np.log(np.float32((MAX_REL - 1) / mid)) * np.float32(mid - 1)
    log_pos = np.ceil(steps.astype(np.float32)) + mid
    return np.where(a <= mid, a, log_pos * np.sign(rel)).astype(np.int32)


def constant_table():
    bucket = dict(zip(range(-(SEQ - 1), SEQ), relative_buckets()))
    order_c = list(range(0, 16)) + list(range(48, 64))
    order_p = list(range(0, 17)) + list(range(49, 64))
    ohc = np.zeros((P, RELW), np.float32)
    ohp = np.zeros((P, RELW), np.float32)
    for r, _ in bucket.items():
        c = int(np.clip(bucket[r] + SPAN, 0, 2 * SPAN - 1))
        p = int(np.clip(-bucket[-r] + SPAN, 0, 2 * SPAN - 1))
        for part in range(PARTS):
            if c != CEN_C:
                ohc[part * NIDX + order_c.index(c), SEQ - 1 - r] = 1.0
            if p != CEN_P:
                ohp[part * NIDX + order_p.index(p), SEQ - 1 + r] = 1.0
    mask = np.zeros((P, NH), np.float32)
    for p in range(P):
        h = p % NH
        mask[p, (h % 4) * 4 + h // 4] = 1.0
    iota = np.broadcast_to(np.arange(NE, dtype=np.float32), (P, NE))
    return np.ascontiguousarray(np.concatenate([np.eye(P, dtype=np.float32), mask, iota, ohc, ohp], axis=1))


C_ID, C_MASK = 0, P
C_IOTA = C_MASK + NH
CW = C_IOTA + NE


class Signal:

    def __init__(self, sem, keys, step=1):
        self.sem, self.step = sem, step
        self.place = {k: n + 1 for n, k in enumerate(keys)}
        assert len(self.place) == len(keys)

    def at(self, key):
        return self.place[key] * self.step


def attention_steps(layer):
    steps = []
    for i in range(NCH + 2):
        refill = layer == "b" and i in (0, NCH // 2)
        if refill and i:
            steps += [("T", i - 1), ("PV", i - 2)]
        if refill:
            steps += [("D", i * 2 // NCH)]
        if i < NCH:
            steps += [("S", i)]
        if 1 <= i <= NCH and not (refill and i):
            steps += [("T", i - 1)]
        if i >= 2:
            c = i - 2
            if not (refill and i):
                steps += [("PV", c)]
            if c >= HC and c % HC < 3:
                steps += [(("OB", "OT", "OP")[c % HC], c // HC - 1)]
    return steps + [("OB", NG - 1), ("OT", NG - 1), ("OP", NG - 1)]


def group(layer, n):
    return (n // 2, n % 2) if layer == "a" else (n % 2, n // 2)


def build(nc, t):
    with ExitStack() as ctx:
        def sb(name, shape, dt=F32):
            return ctx.enter_context(nc.sbuf_tensor(name, shape, dt))

        def sem(name):
            return ctx.enter_context(nc.semaphore(name))

        cst = sb("cst", [P, CW])
        ident = cst[:, C_ID:C_ID + P]
        iota = cst[:, C_IOTA:C_IOTA + NE]
        oh_c = sb("oh_c", [P, RELW], BF16)
        oh_p = sb("oh_p", [P, RELW], BF16)
        ones = sb("ones", [P, P])
        neg_half = sb("neg_half", [P, NT])
        wq, wk, wv, wo = ({L: sb(f"{n}_{L}", [P, D]) for L in "ab"} for n in ("wq", "wk", "wv", "wo"))
        bq, bk = ({L: sb(f"{n}_{L}", [P, 1]) for L in "ab"} for n in ("bq", "bk"))
        bv, bo = ({L: sb(f"{n}_{L}", [P, D]) for L in "ab"} for n in ("bv", "bo"))
        bq_pos, bk_pos = sb("bq_pos", [P, 1]), sb("bk_pos", [P, 1])
        ln_s, ln_b = sb("ln_s", [P, D]), sb("ln_b", [P, D])
        pos_w = {y: sb(f"pos_w_{y}", [P, 4, NIDX, 4]) for y in "cp"}
        w_base = sb("w_base", [P, D])
        wd1 = sb("wd1", [P, NE, HE])
        bd1 = sb("bd1", [P, 2])
        wd2 = sb("wd2", [P, NE, D])
        bd2 = sb("bd2", [P, NE])
        w_all = sb("w_all", [P, NE, SELW])

        x = sb("x", [P, NT, D])
        xn = sb("xn", [P, NT, D])
        xnT = sb("xnT", [P, TOK])
        xb = sb("xb", [P, NT, D])
        stats = sb("stats", [P, NT, 6])
        mv = sb("mv", [P, NT, 2])
        ve = sb("ve", [P, NT])
        rstd = sb("rstd", [P, NT])
        qk_parts = sb("qk_parts", [P, PARTS, 2, TOK], BF16)
        v = sb("v", [P, NT, NH, VC])
        q_stack = sb("q_stack", [KS, NB, NH, SEQ], BF16)
        k_stack = sb("k_stack", [KS, NB, NH, SEQ], BF16)
        prob = sb("prob", [P, 2, HC, SEQ])
        probT = sb("probT", [P, 2, HC, 2, P])
        rest, qk = (prob[:, n].rearrange("p a b -> p (a b)").rearrange("p (a b) -> p a b", a=2) for n in range(2))
        pos_rest = probT[:].rearrange("p n a b c -> p n (a b c)").rearrange("p n (g t) -> p n g t", g=4)
        nmax = sb("nmax", [P, 2, HC])
        nbias = sb("nbias", [P, 2, HC])
        rsum = sb("rsum", [P, 2, NH])
        rinv = sb("rinv", [P, 2, NH])
        o_sb = sb("o_sb", [P, 2, NH, DH])
        oT = sb("oT", [P, 2, P])
        o_turned = sb("o_turned", [P, 2, HC, P])
        plain = sb("plain", [P, 2, TOK])
        att = {y: sb(f"att_{y}", [PARTS * NIDX, NB, NH, SEQ], BF16) for y in "cp"}
        c2p = sb("c2p", [P, 2, BH, P])
        p2c = sb("p2c", [P, BH, SEQ])
        hT = c2p[:, 0, 0:8, :].rearrange("p a b -> p (a b)").rearrange("p (a b) -> p a b", a=2)
        diff = c2p[:, 0, 8:24, :].rearrange("p a b -> p (a b)").rearrange("p (k e t) -> p k e t", k=2, e=2)
        picked = p2c[:, :, :].rearrange("p a b -> p (a b)")[:, 0:NB * NE * SELW].rearrange(
            "p (b e c) -> p b e c", b=NB, e=NE)
        att_parts = p2c[:].rearrange("p a b -> p (a b)").bitcast(BF16)[:, 0:2 * PARTS * 4 * SEQ].rearrange(
            "p (n s g t) -> p n s g t", n=2, s=PARTS, g=4)
        tables = c2p[:].rearrange("p a b c -> p (a b c)")[:, 0:2 * RELW]
        aT = sb("aT", [R + 1, TOK])
        w_sel = sb("w_sel", [P, NB, SELW])
        loss_p = sb("loss_p", [P, NB, NE])
        lmin, lkey, kmin, onehot = (sb(n, s) for n, s in (
            ("lmin", [P, NB]), ("lkey", [P, NB, NE]), ("kmin", [P, NB]), ("onehot", [P, NB, NE])))
        y = plain[:, 0, :].rearrange("p (t n) -> p t n", t=NT)
        rel_sb = sb("rel_sb", [2 * SPAN, D])
        relT = sb("relT", [P, 2 * SPAN])
        posT = sb("posT", [P, 2 * SPAN])
        dpos = {c: sb(f"dpos_{c}", [P, NIDX]) for c in "cp"}

        ps_s = [ctx.enter_context(nc.psum_tensor(f"ps_s{n}", [P, 2, 512], F32)) for n in range(2)]
        ps_t = [ctx.enter_context(nc.psum_tensor(f"ps_t{n}", [P, 512], F32)) for n in range(2)]
        ps_m = [ctx.enter_context(nc.psum_tensor(f"ps_m{n}", [P, 512], F32)) for n in range(2)]

        q_dram = nc.dram_tensor("q_scratch", (NB, PARTS, PARTS, P, SEQ), BF16, kind="Internal").ap()
        k_dram = nc.dram_tensor("k_scratch", (NB, PARTS, P, SEQ), BF16, kind="Internal").ap()
        att_dram = nc.dram_tensor("att_scratch", (2, NB, PARTS, P, 4 * SEQ), BF16, kind="Internal").ap()

        s_cst, s_load, s_rows, s_wd2 = sem("s_cst"), sem("s_load"), sem("s_rows"), sem("s_wd2")
        s_zero, s_tr, s_trc, s_cast, s_pos, s_perm, s_bb = (
            sem(n) for n in ("s_zero", "s_tr", "s_trc", "s_cast", "s_pos", "s_perm", "s_bb"))
        rows = {n: xn[:, k, :] for k, n in enumerate(("q", "k", "v", "o"))}
        raw = {"q": x[:, 0, :], "k": x[:, 1, :]}
        qkv_c = t["L0_attn_a_W_qkv"].rearrange("(h c) i -> c h i", c=3 * DH)
        qkv_h = t["L0_attn_a_W_qkv"].rearrange("(h c) i -> h c i", c=3 * DH)
        bqkv_c = t["L0_attn_a_b_qkv"].rearrange("(h c u) -> c h u", c=3 * DH, u=1)
        bqkv_h = t["L0_attn_a_b_qkv"].rearrange("(h c) -> h c", c=3 * DH)

        def column(name):
            return t[name].rearrange("(h d u) -> d h u", d=DH, u=1)

        def everywhere(name):
            return t[name].rearrange("(u n) -> u n", u=1).to_broadcast([P, D])

        loads = [
            (w_base[:], t["L0_ffn_W_base"]),
            (wv["b"][:], t["L0_attn_b_Wv"]), (wo["b"][:], t["L0_attn_b_Wo"]),
            (raw["q"], t["L0_attn_b_Wq"]), (raw["k"], t["L0_attn_b_Wk"]),
            (rel_sb[:], t["L0_attn_b_rel_embeddings"]),
            (bq["a"][:], bqkv_c[0:DH]), (bk["a"][:], bqkv_c[DH:2 * DH]),
            (bv["a"][:].rearrange("p (h d) -> p h d", d=DH),
             bqkv_h[:, 2 * DH:].rearrange("(u h) d -> u h d", u=1).to_broadcast([P, NH, DH])),
            (bo["a"][:], everywhere("L0_attn_a_b_out")),
            (bq["b"][:], column("L0_attn_b_bq")), (bk["b"][:], column("L0_attn_b_bk")),
            (bv["b"][:], everywhere("L0_attn_b_bv")), (bo["b"][:], everywhere("L0_attn_b_bo")),
            (ln_s[:], everywhere("L0_attn_b_ln_scale")), (ln_b[:], everywhere("L0_attn_b_ln_bias")),
            (wd1[:], t["L0_ffn_Wd1"].rearrange("e d h -> d e h")),
            (bd1[:], t["L0_ffn_bd1"].rearrange("(j e) h -> (e h) j", j=2)),
            (bd2[:], t["L0_ffn_bd2"].rearrange("e d -> d e")),
        ]
        loads_zeroed = [
            (w_all[:, :, 0:R], t["L0_ffn_Wa_down"].rearrange("e d r -> d e r")),
            (w_all[0:R, :, R:R + D], t["L0_ffn_Wa_up"].rearrange("e r o -> r e o")),
            (w_all[R:R + 1, :, R:R + D], t["L0_ffn_ba_up"].rearrange("(u e) o -> u e o", u=1)),
            (w_all[0:R, :, R + D:SELW], t["L0_ffn_ba_down"].rearrange("e (r u) -> r e u", u=1)),
            (aT[R:R + 1, 0:D], t["L0_ffn_b_base"].rearrange("(u n) -> u n", u=1)),
        ] + [(wd2[HE * (e % 4):HE * (e % 4 + 1), e, :], t["L0_ffn_Wd2"][e]) for e in range(NE)]

        ctx.enter_context(nc.allow_non_contiguous_dma(reason="bias vectors laid out one element per partition"))
        with nc.Block() as block:
            @block.sync
            def _(sp):
                sp.dma_start(cst[:], t["constants"][:, 0:CW]).then_inc(s_cst, 16)
                sp.dma_start(tables, t["constants"][:, CW:]).then_inc(s_cst, 16)
                sp.dma_start(rows["q"], qkv_c[0:DH]).then_inc(s_rows, 16)
                sp.dma_start(rows["k"], qkv_c[DH:2 * DH]).then_inc(s_rows, 16)
                sp.dma_start(rows["v"], qkv_h[:, 2 * DH:]).then_inc(s_rows, 16)
                sp.dma_start(rows["o"], t["L0_attn_a_W_out"]).then_inc(s_rows, 16)
                for dst, src in loads:
                    sp.dma_start(dst, src).then_inc(s_load, 16)
                sp.wait_ge(s_zero, 3)
                for dst, src in loads_zeroed:
                    sp.dma_start(dst, src).then_inc(s_wd2, 16)
                sp.wait_ge(s_load, 16 * len(loads))
                sp.wait_ge(s_wd2, 16 * len(loads_zeroed))

            @block.gpsimd
            def _(pool):
                nc.gpsimd.memset(wd2[:], 0.0).then_inc(s_zero, 1)
                nc.gpsimd.memset(w_all[:], 0.0).then_inc(s_zero, 1)
                nc.gpsimd.memset(neg_half[:], -0.5).then_inc(s_zero, 1)
                nc.gpsimd.memset(ones[:], 1.0).then_inc(s_zero, 1)
                nc.gpsimd.memset(v[:], 0.0).then_inc(s_zero, 1)
                pool.wait_ge(s_zero, 5)
                pool.wait_ge(s_wd2, 16 * len(loads_zeroed))
                nc.gpsimd.tensor_tensor(
                    w_all[R:R + 1, :, R:R + D], w_all[R:R + 1, :, R:R + D],
                    aT[R:R + 1, 0:D].rearrange("u (e n) -> u e n", e=1).to_broadcast([1, NE, D]),
                    ALU.add).then_inc(s_bb, 1)
                pool.wait_ge(s_bb, 1)
                nc.gpsimd.memset(aT[R:R + 1, :], 1.0).then_inc(s_bb, 1)
                pool.wait_ge(s_bb, 2)

            @block.tensor
            def _(pe):
                pe.wait_ge(s_cst, 32)
                pe.wait_ge(s_rows, 16 * 4)
                for k, n in enumerate("qkvo"):
                    ins = nc.tensor.transpose(ps_m[0][:, k * P:(k + 1) * P], rows[n], ident)
                ins.then_inc(s_tr, 1)
                pe.wait_ge(s_load, 16 * len(loads))
                nc.tensor.transpose(ps_m[1][:, 0:2 * SPAN], rel_sb[:], ident[0:2 * SPAN, 0:2 * SPAN]).then_inc(s_tr, 1)
                pe.wait_ge(s_trc, 5)
                pe.wait_ge(s_perm, 2)
                nc.tensor.matmul(ps_t[0][:, 0:2 * SPAN], wk["b"][:], relT[:], start=True, stop=True).then_inc(s_tr, 1)

            @block.vector
            def _(dve):
                dve.wait_ge(s_cst, 32)
                nc.vector.tensor_copy(oh_c[:], tables[:, 0:RELW])
                nc.vector.tensor_copy(oh_p[:], tables[:, RELW:])
                dve.wait_ge(s_tr, 1)
                for k, w in enumerate((wq["a"], wk["a"], wv["a"], wo["a"])):
                    nc.vector.tensor_copy(w[:], ps_m[0][:, k * P:(k + 1) * P]).then_inc(s_trc, 1)
                dve.wait_ge(s_load, 16 * len(loads))
                for n, w in (("q", wq["b"]), ("k", wk["b"])):
                    nc.vector.tensor_copy(w[:].rearrange("p (d h) -> p d h", d=DH),
                                          raw[n].rearrange("p (h d) -> p d h", d=DH)).then_inc(s_perm, 1)
                dve.wait_ge(s_tr, 2)
                nc.vector.tensor_copy(relT[:], ps_m[1][:, 0:2 * SPAN]).then_inc(s_trc, 1)
                dve.wait_ge(s_tr, 3)
                nc.vector.tensor_scalar(posT[:], ps_t[0][:, 0:2 * SPAN], bk["b"][:], None, ALU.add).then_inc(s_pos, 1)
                dve.wait_ge(s_pos, 1)
                nc.vector.tensor_tensor(bq_pos[:], bq["b"][:], posT[:, CEN_P:CEN_P + 1], ALU.add)
                nc.vector.tensor_tensor(bk_pos[:], bk["b"][:], posT[:, CEN_C:CEN_C + 1], ALU.add)
                for c, cen, cut, nxt in (("c", CEN_C, 16, 48), ("p", CEN_P, 17, 49)):
                    nc.vector.tensor_scalar(dpos[c][:, 0:cut], posT[:, 0:cut], posT[:, cen:cen + 1], None,
                                            ALU.subtract).then_inc(s_pos, 1)
                    nc.vector.tensor_scalar(dpos[c][:, cut:], posT[:, nxt:], posT[:, cen:cen + 1], None,
                                            ALU.subtract).then_inc(s_pos, 1)
                dve.wait_ge(s_pos, 5)
                for c in "cp":
                    for g in range(4):
                        m = cst[:, C_MASK + 4 * g:C_MASK + 4 * g + 4].rearrange("p (u h) -> p u h", u=1)
                        nc.vector.tensor_tensor(
                            pos_w[c][:, g], dpos[c][:].rearrange("p (i u) -> p i u", u=1).to_broadcast([P, NIDX, 4]),
                            m.to_broadcast([P, NIDX, 4]), ALU.mult)

        nc.all_engine_barrier()

        turn_sems = []

        def signal(name, keys, step=1):
            s = sem(name)
            turn_sems.append(s)
            return Signal(s, list(keys), step)

        norms = ["a", "f", "b", "n", "g"]
        with_xt = ["a", "f", "b", "g"]
        steps = {L: attention_steps(L) for L in "ab"}
        chunks = [(L, i) for L in "ab" for i in range(NCH)]
        groups = [(L, n) for L in "ab" for n in range(NG)]

        DJ = 8
        s_jobs, m_jobs = [], []

        def attention_jobs(L):
            m_jobs.append((("xt", L), 0))
            s_jobs.extend([("qk", L), ("v", L)])
            if L == "b":
                s_jobs.extend([("att", c, b) for c in "cp" for b in range(NB)])
            for kind, k in steps[L]:
                if kind == "S":
                    s_jobs.append(("S", L, k))
                elif kind == "D":
                    s_jobs.extend([("D", k, c, j) for c in "cp" for j in range(DJ)])
                elif kind in ("OB", "OT", "OP"):
                    m_jobs.append(((kind, L, k), k % 2))

        def ffn_jobs(s):
            m_jobs.append((("xt", s), 0))
            s_jobs.append(("h", s))
            s_jobs.extend([("rec", s, k) for k in range(NE // 2)])
            m_jobs.append((("loss", s), 1))
            s_jobs.extend([("act", s), ("ffo", s)])

        attention_jobs("a")
        ffn_jobs("f")
        attention_jobs("b")
        ffn_jobs("g")

        x_loaded, out_stored = signal("x_loaded", ["x"], 16), signal("out_stored", ["x"], 16)
        LB = [(L, b) for L in "ab" for b in range(NB)]
        parts_stored = {b: signal(f"parts_stored{b}", [(L, n) for L in "ab" for n in range(1 + PARTS)], 16) for b in range(NB)}
        stack_loaded = {b: signal(f"stack_loaded{b}", [(L, n) for L in "ab" for n in range(1 + PARTS)], 16) for b in range(NB)}
        pos_parts_stored = {n: signal(f"pos_parts_stored{n}", [(c, b) for c in "cp" for b in range(NB)][n::2], 16) for n in range(2)}
        pos_stack_loaded = {c: signal(f"pos_stack_loaded_{c}", range(NB), 16) for c in "cp"}

        score_slot_filled = signal("score_slot_filled", s_jobs)
        small_bank_filled = signal("small_bank_filled", [k for k, _ in m_jobs])
        probs_turned = signal("probs_turned", [(L, i, hh) for L, i in chunks for hh in range(2)])
        values_weighed = signal("values_weighed", chunks)

        normed = signal("normed", [(s, k) for s in norms for k in range(NT)])
        stats_done = signal("stats_done", [(s, k) for s in norms for k in range(2 * NT)])
        variance_done = signal("variance_done", norms)
        root_done = signal("root_done", norms)
        bias_added = signal("bias_added", ["a", "b", "n"])
        xnT_ready = signal("xnT_ready", with_xt)
        qk_ready = signal("qk_ready", [(L, n) for L in "ab" for n in range(2)])
        plain_qk_ready = signal("plain_qk_ready", [0, 1])
        v_ready = signal("v_ready", "ab")
        part1_ready = signal("part1_ready", LB)
        part2_ready = signal("part2_ready", LB)
        rest_ready = signal("rest_ready", LB)
        part3_ready = signal("part3_ready", LB)
        AK = [(c, b) for c in "cp" for b in range(NB)]
        pos_part1_ready, pos_part2_ready = signal("pos_part1_ready", AK), signal("pos_part2_ready", AK)
        pos_rest_ready, pos_part3_ready = signal("pos_rest_ready", AK), signal("pos_part3_ready", AK)
        DK = [(q, c, j) for q in range(2) for c in "cp" for j in range(DJ)]
        d_engine = {k: ("act" if k[2] % 2 else "dve") for k in DK}
        spread_by_act = signal("spread_by_act", [k for k in DK if d_engine[k] == "act"])
        spread_by_dve = signal("spread_by_dve", [k for k in DK if d_engine[k] == "dve"])
        scores_summed = signal("scores_summed", range(NCH))
        max_ready = signal("max_ready", chunks)
        exp_bias_ready = signal("exp_bias_ready", chunks)
        probs_ready = signal("probs_ready", chunks)

        def t_engine(L, i, hh):
            if hh == 0:
                return "dve"
            return "act" if L == "b" or i % 2 == 0 else "dve"

        halves = [(L, i, hh) for L, i in chunks for hh in range(2)]
        probT_by_act = signal("probT_by_act", [k for k in halves if t_engine(*k) == "act"])
        probT_by_dve = signal("probT_by_dve", [k for k in halves if t_engine(*k) == "dve"])
        moved_by = {"act": probT_by_act, "dve": probT_by_dve}
        inverse_ready = signal("inverse_ready", groups)
        out_moved = signal("out_moved", groups)
        heads_out_ready = signal("heads_out_ready", groups)
        outT_ready = signal("outT_ready", groups)
        residual_added = signal("residual_added", groups)
        hidden_ready = signal("hidden_ready", [(s, j) for s in "fg" for j in range(2)])
        diff_ready = signal("diff_ready", [(s, k) for s in "fg" for k in range(NE // 2)])
        losses_ready = signal("losses_ready", [(s, k) for s in "fg" for k in range(NE // 2)])
        choice_step = signal("choice_step", [(s, k) for s in "fg" for k in range(5)])
        picked_by_dve = signal("picked_by_dve", "fg")
        picked_by_pool = signal("picked_by_pool", "fg")
        adapter_ready = signal("adapter_ready", [(s, b) for s in "fg" for b in range(NB)])
        adapter_hidden_ready = signal("adapter_hidden_ready", [(s, b) for s in "fg" for b in range(NB)])
        ffn_added = signal("ffn_added", "fg")
        inner_norm_step = signal("inner_norm_step", ["s", "x"])

        def freed_s(job):
            kind = job[0]
            if kind == "qk":
                return (qk_ready, ("a", 1)) if job[1] == "a" else (plain_qk_ready, 1)
            if kind == "v":
                return v_ready, job[1]
            if kind == "att":
                return pos_rest_ready, job[1:]
            if kind == "D":
                return (spread_by_act if d_engine[job[1:]] == "act" else spread_by_dve), job[1:]
            if kind == "S":
                return (probs_ready, job[1:]) if job[1] == "a" else (scores_summed, job[2])
            if kind == "h":
                return hidden_ready, (job[1], 1)
            if kind == "rec":
                return diff_ready, job[1:]
            if kind == "act":
                return adapter_hidden_ready, (job[1], NB - 1)
            return ffn_added, job[1]

        def slot_s(job):
            return s_jobs.index(job) % 2

        def take_s(pe, job):
            n = s_jobs.index(job)
            if n >= 2:
                read_out, key = freed_s(s_jobs[n - 2])
                pe.wait_ge(read_out.sem, read_out.at(key))
            return ps_s[n % 2]

        def spread_views(k):
            qt, c, j = k
            src = ps_s[slot_s(("D", *k))].rearrange("p a (n b) -> p b (a n)", b=BH)
            if c == "c":
                return c2p[:, j // 4, :, (j % 4) * 32:(j % 4 + 1) * 32], src
            return p2c[:, :, j * 32:(j + 1) * 32], src

        def one_hot_wide(b):
            return onehot[:, b, :].rearrange("p (e u) -> p e u", u=1).to_broadcast([P, NE, SELW])

        x_rows = t["L0_attn_a_x"].rearrange("b (t p) d -> (b t) p d", p=P)
        out_rows = t["out"].rearrange("b (t p) d -> (b t) p d", p=P)
        n_turns = x_rows.shape[0] // NT

        with nc.Fori(0, n_turns) as turn:
            with nc.Block() as block:

                @block.sync
                def _(sp):
                    sp.dma_start(x[:], x_rows[bass.ts(turn, NT)].rearrange("t p d -> p t d")).then_inc(x_loaded.sem, 16)

                    def store_qk(L, b):
                        sp.wait_ge(part3_ready.sem, part3_ready.at((L, b)))
                        sp.wait_ge(part2_ready.sem, part2_ready.at((L, b)))
                        parts = [qk_parts[:, :, n, b * SEQ:(b + 1) * SEQ] for n in range(2)]
                        sp.dma_start(k_dram[b].rearrange("j p t -> p j t"), parts[1]).then_inc(parts_stored[b].sem, 16)
                        for j in range(PARTS):
                            sp.dma_start(q_dram[b, :, j].rearrange("i p t -> p i t"), parts[0]).then_inc(parts_stored[b].sem, 16)

                    def load_qk(L, b):
                        sp.wait_ge(parts_stored[b].sem, parts_stored[b].at((L, PARTS)))
                        if L == "b" and b == 0:
                            sp.wait_ge(score_slot_filled.sem, score_slot_filled.at(("S", "a", NCH - 1)))
                        for i in range(PARTS):
                            sp.dma_start(
                                k_stack[i * PARTS * DH:(i + 1) * PARTS * DH, b].rearrange("r h t -> r (h t)"),
                                k_dram[b].rearrange("j (d h) t -> (j d) (h t)", d=DH)).then_inc(stack_loaded[b].sem, 16)
                        sp.dma_start(
                            q_stack[:, b].rearrange("r h t -> r (h t)"),
                            q_dram[b].rearrange("i j (d h) t -> (i j d) (h t)", d=DH)).then_inc(stack_loaded[b].sem, 16)

                    def store_positions(n):
                        c, b = AK[n]
                        sp.wait_ge(pos_part3_ready.sem, pos_part3_ready.at((c, b)))
                        sp.wait_ge(pos_part2_ready.sem, pos_part2_ready.at((c, b)))
                        sp.dma_start(att_dram["cp".index(c), b].rearrange("s p t -> p s t"),
                                     att_parts[:, n % 2].rearrange("p s g t -> p s (g t)")).then_inc(
                                         pos_parts_stored[n % 2].sem, 16)

                    def load_positions(n):
                        c, b = AK[n]
                        sp.wait_ge(pos_parts_stored[n % 2].sem, pos_parts_stored[n % 2].at((c, b)))
                        sp.dma_start(att[c][:, b].rearrange("r h t -> r (h t)"),
                                     att_dram["cp".index(c), b].rearrange("s (i a) t -> (s i) (a t)", a=4)).then_inc(
                                         pos_stack_loaded[c].sem, 16)

                    for b in range(NB):
                        store_qk("a", b)
                    for b in range(NB):
                        load_qk("a", b)
                    for n in range(len(AK)):
                        store_positions(n)
                        if n:
                            load_positions(n - 1)
                    store_qk("b", 0)
                    load_positions(len(AK) - 1)
                    store_qk("b", 1)
                    for b in range(NB):
                        load_qk("b", b)
                    sp.wait_ge(ffn_added.sem, ffn_added.at("g"))
                    sp.dma_start(out_rows[bass.ts(turn, NT)].rearrange("t p d -> p t d"), x[:]).then_inc(out_stored.sem, 16)
                    sp.wait_ge(out_stored.sem, out_stored.at("x"))

                @block.tensor
                def _(pe):
                    def turn_xn(s):
                        pe.wait_ge(normed.sem, normed.at((s, NT - 1)))
                        for k in range(NT):
                            ins = nc.tensor.transpose(ps_m[0][:, k * P:(k + 1) * P], xn[:, k, :], ident)
                        ins.then_inc(small_bank_filled.sem, 1)

                    def project(L):
                        pe.wait_ge(xnT_ready.sem, xnT_ready.at(L))
                        slot = take_s(pe, ("qk", L))
                        nc.tensor.matmul(slot[:, 0, :], wq[L][:], xnT[:], start=True, stop=True)
                        nc.tensor.matmul(slot[:, 1, :], wk[L][:], xnT[:], start=True, stop=True).then_inc(score_slot_filled.sem, 1)
                        slot = take_s(pe, ("v", L))
                        for k in range(NT):
                            ins = nc.tensor.matmul(slot[:, 0, k * P:(k + 1) * P], xnT[:, k * P:(k + 1) * P],
                                                   wv[L][:], start=True, stop=True)
                        ins.then_inc(score_slot_filled.sem, 1)

                    def position_terms():
                        for c, b in AK:
                            pe.wait_ge(plain_qk_ready.sem, plain_qk_ready.at("cp".index(c)))
                            slot = take_s(pe, ("att", c, b)).rearrange("p a (g t) -> p (a g) t", g=2)
                            for g in range(4):
                                ins = nc.tensor.matmul(slot[:, g, :], pos_w[c][:, g].rearrange("p i h -> p (i h)"),
                                                       plain[:, "cp".index(c), b * SEQ:(b + 1) * SEQ],
                                                       start=True, stop=True)
                            ins.then_inc(score_slot_filled.sem, 1)

                    def spread_positions(qt):
                        for c in "cp":
                            pe.wait_ge(pos_stack_loaded[c].sem, pos_stack_loaded[c].at(NB - 1))
                            for j in range(DJ):
                                job = ("D", qt, c, j)
                                slot = take_s(pe, job).rearrange("p a (n b) -> p (a n) b", b=BH)
                                for u in range(P // 4):
                                    if c == "c":
                                        kt, fixed = j // 4, qt * P + (j % 4) * 32 + u
                                        start = SEQ - 1 - fixed + kt * P
                                        table = oh_c
                                    else:
                                        fixed = j * 32 + u
                                        start = SEQ - 1 - fixed + qt * P
                                        table = oh_p
                                    ins = nc.tensor.matmul(
                                        slot[:, u, :], table[0:PARTS * NIDX, start:start + P],
                                        att[c][:, :, :, fixed:fixed + 1].rearrange("r b h u -> r (b h u)"),
                                        start=True, stop=True)
                                ins.then_inc(score_slot_filled.sem, 1)

                    def scores(L, i):
                        b, qt = group(L, i // HC)
                        if i % HC == 0:
                            pe.wait_ge(stack_loaded[b].sem, stack_loaded[b].at((L, PARTS)))
                        if L == "b" and i % (NCH // 2) == 0:
                            pe.wait_ge(spread_by_act.sem, spread_by_act.at((qt, "c", DJ - 1)))
                            pe.wait_ge(spread_by_dve.sem, spread_by_dve.at((qt, "c", DJ - 2)))
                        slot = take_s(pe, ("S", L, i)).rearrange("p a (g t) -> p (a g) t", g=2)
                        for k in range(HC):
                            h = (i % HC) * HC + k
                            if L == "b":
                                for kt in range(2):
                                    nc.tensor.matmul(slot[:, k, kt * P:(kt + 1) * P], c2p[:, kt, b * NH + h, :], ident,
                                                     start=(k % 2 == 0 and kt == 0), stop=False, is_transpose=True,
                                                     skip_group_check=True)
                            ins = nc.tensor.matmul(slot[:, k, :], q_stack[:, b, h, qt * P:(qt + 1) * P],
                                                   k_stack[:, b, h, :], start=(L == "a"), stop=True,
                                                   skip_group_check=True)
                        ins.then_inc(score_slot_filled.sem, 1)

                    def turn_probs(L, i):
                        pe.wait_ge(probs_ready.sem, probs_ready.at((L, i)))
                        for hh in range(2):
                            if (L, i) != ("a", 0):
                                before = (L, i - 1, hh) if i else ("a", NCH - 1, hh)
                                moved = moved_by[t_engine(*before)]
                                pe.wait_ge(moved.sem, moved.at(before))
                            for k in range(2):
                                for kt in range(2):
                                    ins = nc.tensor.transpose(
                                        ps_t[hh][:, (2 * k + kt) * P:(2 * k + kt + 1) * P],
                                        prob[:, i % 2, 2 * hh + k, kt * P:(kt + 1) * P], ident)
                            ins.then_inc(probs_turned.sem, 1)

                    def weigh_values(L, i):
                        n = i // HC
                        b, qt = group(L, n)
                        if i == 0:
                            pe.wait_ge(v_ready.sem, v_ready.at(L))
                        if i % HC == 0 and n >= 2:
                            pe.wait_ge(residual_added.sem, residual_added.at((L, n - 2)))
                        for hh in range(2):
                            key = (L, i, hh)
                            moved = moved_by[t_engine(*key)]
                            pe.wait_ge(moved.sem, moved.at(key))
                        c = i % HC
                        for kt in range(2):
                            for k in range(HC):
                                ins = nc.tensor.matmul(ps_m[n % 2][VC * k:VC * (k + 1), c * P:(c + 1) * P],
                                                       v[:, 2 * b + kt, c * HC + k, :], probT[:, i % 2, k, kt, :],
                                                       start=(kt == 0), stop=(kt == 1), skip_group_check=True)
                        ins.then_inc(values_weighed.sem, 1)

                    def turn_back(L, n):
                        pe.wait_ge(out_moved.sem, out_moved.at((L, n)))
                        for c in range(HC):
                            ins = nc.tensor.transpose(ps_m[n % 2][:, c * P:(c + 1) * P], o_turned[:, n % 2, c, :], ident)
                        ins.then_inc(small_bank_filled.sem, 1)

                    def turn_out(L, n):
                        pe.wait_ge(heads_out_ready.sem, heads_out_ready.at((L, n)))
                        nc.tensor.transpose(ps_m[n % 2][:, 0:P], o_sb[:, n % 2].rearrange("p h d -> p (h d)"),
                                                 ident).then_inc(small_bank_filled.sem, 1)

                    def project_out(L, n):
                        pe.wait_ge(outT_ready.sem, outT_ready.at((L, n)))
                        nc.tensor.matmul(ps_m[n % 2][:, 0:P], oT[:, n % 2, :], wo[L][:], start=True, stop=True).then_inc(small_bank_filled.sem, 1)

                    def attend(L):
                        turn_xn(L)
                        project(L)
                        if L == "b":
                            position_terms()
                        do = {"S": scores, "T": turn_probs, "PV": weigh_values, "OB": turn_back, "OT": turn_out, "OP": project_out}
                        for kind, k in steps[L]:
                            if kind == "D":
                                spread_positions(k)
                            else:
                                do[kind](L, k)

                    def ffn(s):
                        turn_xn(s)
                        pe.wait_ge(xnT_ready.sem, xnT_ready.at(s))
                        slot = take_s(pe, ("h", s))
                        for j in range(2):
                            ins = nc.tensor.matmul(slot[:, j, :], wd1[:, 4 * j:4 * j + 4, :].rearrange("p e h -> p (e h)"),
                                                   xnT[:], start=True, stop=True)
                        ins.then_inc(score_slot_filled.sem, 1)
                        pe.wait_ge(hidden_ready.sem, hidden_ready.at((s, 1)))
                        for k in range(NE // 2):
                            slot = take_s(pe, ("rec", s, k))
                            for j in range(2):
                                e = 2 * k + j
                                ins = nc.tensor.matmul(slot[:, j, :], wd2[:, e, :], hT[:, e // 4, :],
                                                       start=True, stop=True)
                            ins.then_inc(score_slot_filled.sem, 1)
                        pe.wait_ge(losses_ready.sem, losses_ready.at((s, NE // 2 - 1)))
                        nc.tensor.matmul(ps_m[1][:, 0:NB * NE], ones[:], loss_p[:].rearrange("p b e -> p (b e)"),
                                              start=True, stop=True).then_inc(small_bank_filled.sem, 1)
                        slot = take_s(pe, ("act", s))
                        for b in range(NB):
                            pe.wait_ge(adapter_ready.sem, adapter_ready.at((s, b)))
                            ins = nc.tensor.matmul(slot[0:R, 0, b * SEQ:(b + 1) * SEQ], w_sel[:, b, 0:R],
                                                   xnT[:, b * SEQ:(b + 1) * SEQ], start=True, stop=True)
                        ins.then_inc(score_slot_filled.sem, 1)
                        slot = take_s(pe, ("ffo", s))
                        pe.wait_ge(adapter_hidden_ready.sem, adapter_hidden_ready.at((s, NB - 1)))
                        for k in range(NT):
                            nc.tensor.matmul(slot[:, 0, k * P:(k + 1) * P], xnT[:, k * P:(k + 1) * P], w_base[:],
                                             start=True, stop=False)
                            ins = nc.tensor.matmul(slot[:, 0, k * P:(k + 1) * P], aT[:, k * P:(k + 1) * P],
                                                   w_sel[0:R + 1, k // 2, R:R + D], start=False, stop=True)
                        ins.then_inc(score_slot_filled.sem, 1)

                    attend("a")
                    ffn("f")
                    attend("b")
                    ffn("g")

                @block.scalar
                def _(act):
                    def copy_xt(s):
                        act.wait_ge(small_bank_filled.sem, small_bank_filled.at(("xt", s)))
                        nc.scalar.copy(xnT[:], ps_m[0][:]).then_inc(xnT_ready.sem, 1)

                    def split(L):
                        if L == "b":
                            for n, bias in enumerate((bq["b"], bk["b"])):
                                act.wait_ge(qk_ready.sem, qk_ready.at(("b", n)))
                                nc.scalar.activation(plain[:, n, :], ps_s[slot_s(("qk", "b"))][:, n, :],
                                                          ACT.Identity, bias=bias[:]).then_inc(plain_qk_ready.sem, 1)
                            split_positions()
                        for b in range(NB):
                            cols = slice(b * SEQ, (b + 1) * SEQ)
                            act.wait_ge(qk_ready.sem, qk_ready.at((L, 1)))
                            if L == "b":
                                act.wait_ge(parts_stored[b].sem, parts_stored[b].at(("a", PARTS)))
                            nc.scalar.copy(qk_parts[:, 0, :, cols], qk[:, :, cols]).then_inc(part1_ready.sem, 1)
                        for b in range(NB):
                            cols = slice(b * SEQ, (b + 1) * SEQ)
                            act.wait_ge(rest_ready.sem, rest_ready.at((L, b)))
                            nc.scalar.copy(qk_parts[:, 1, :, cols], rest[:, :, cols]).then_inc(part2_ready.sem, 1)

                    def split_positions():
                        for n, (c, b) in enumerate(AK):
                            slot = ps_s[slot_s(("att", c, b))].rearrange("p a (g t) -> p (a g) t", g=2)
                            act.wait_ge(score_slot_filled.sem, score_slot_filled.at(("att", c, b)))
                            if n >= 2:
                                act.wait_ge(pos_parts_stored[n % 2].sem, pos_parts_stored[n % 2].at(AK[n - 2]))
                            nc.scalar.copy(att_parts[:, n % 2, 0], slot).then_inc(pos_part1_ready.sem, 1)
                            act.wait_ge(pos_rest_ready.sem, pos_rest_ready.at((c, b)))
                            nc.scalar.copy(att_parts[:, n % 2, 1], pos_rest[:, n % 2]).then_inc(pos_part2_ready.sem, 1)

                    def spread_out(qt):
                        for k in DK:
                            if k[0] == qt and d_engine[k] == "act":
                                if qt:
                                    act.wait_ge(score_slot_filled.sem, score_slot_filled.at(("S", "b", NCH // 2 - 1)))
                                    act.wait_ge(scores_summed.sem, scores_summed.at(NCH // 2 - 1))
                                act.wait_ge(score_slot_filled.sem, score_slot_filled.at(("D", *k)))
                                nc.scalar.copy(*spread_views(k)).then_inc(spread_by_act.sem, 1)

                    def exps(L, i):
                        scale = SCALE_A if L == "a" else SCALE_B
                        src = ps_s[slot_s(("S", L, i))].rearrange("p a (g t) -> p (a g) t", g=2)
                        n = i // HC
                        act.wait_ge(exp_bias_ready.sem, exp_bias_ready.at((L, i)))
                        if L == "b":
                            src = prob[:, i % 2]
                        elif i >= 2:
                            act.wait_ge(probs_turned.sem, probs_turned.at((L, i - 2, 1)))
                        for k in range(HC):
                            h = (i % HC) * HC + k
                            ins = nc.scalar.activation(prob[:, i % 2, k, :], src[:, k, :], ACT.Exp,
                                                       bias=nbias[:, i % 2, k:k + 1], scale=scale,
                                                       accum_out=rsum[:, n % 2, h:h + 1])
                        ins.then_inc(probs_ready.sem, 1)

                    def move_probs(L, i):
                        for hh in range(2):
                            if t_engine(L, i, hh) == "act":
                                act.wait_ge(probs_turned.sem, probs_turned.at((L, i, hh)))
                                if i >= 2:
                                    act.wait_ge(values_weighed.sem, values_weighed.at((L, i - 2)))
                                nc.scalar.copy(probT[:, i % 2, 2 * hh:2 * hh + 2],
                                                    ps_t[hh][:].rearrange("p (a b c) -> p a b c", a=2, b=2)).then_inc(probT_by_act.sem, 1)

                    def move_out(L, n):
                        act.wait_ge(values_weighed.sem, values_weighed.at((L, HC * n + HC - 1)))
                        nc.scalar.copy(o_turned[:, n % 2].rearrange("p c t -> p (c t)"),
                                       ps_m[n % 2][:]).then_inc(out_moved.sem, 1)

                    def copy_out(L, n):
                        act.wait_ge(small_bank_filled.sem, small_bank_filled.at(("OT", L, n)))
                        nc.scalar.copy(oT[:, n % 2, :], ps_m[n % 2][:, 0:P]).then_inc(outT_ready.sem, 1)

                    def attend(L):
                        copy_xt(L)
                        split(L)
                        for kind, k in steps[L]:
                            if kind == "S":
                                exps(L, k)
                            elif kind == "T":
                                move_probs(L, k)
                            elif kind == "OB":
                                move_out(L, k)
                            elif kind == "OT":
                                copy_out(L, k)
                            elif kind == "D":
                                spread_out(k)

                    def ffn(s):
                        copy_xt(s)
                        for j in range(2):
                            act.wait_ge(score_slot_filled.sem, score_slot_filled.at(("h", s)))
                            nc.scalar.activation(hT[:, j, :], ps_s[slot_s(("h", s))][:, j, :], ACT.Relu,
                                                      bias=bd1[:, j:j + 1]).then_inc(hidden_ready.sem, 1)
                        for k in range(NE // 2):
                            act.wait_ge(diff_ready.sem, diff_ready.at((s, k)))
                            for j in range(2):
                                for b in range(NB):
                                    e = 2 * k + j
                                    d = diff[:, k % 2, j, b * SEQ:(b + 1) * SEQ]
                                    ins = nc.scalar.activation(d, d, ACT.Square, bias=bd2[:, e:e + 1],
                                                               accum_out=loss_p[:, b, e:e + 1])
                            ins.then_inc(losses_ready.sem, 1)
                        for b in range(NB):
                            act.wait_ge(score_slot_filled.sem, score_slot_filled.at(("act", s)))
                            cols = slice(b * SEQ, (b + 1) * SEQ)
                            nc.scalar.activation(aT[0:R, cols], ps_s[slot_s(("act", s))][0:R, 0, cols], ACT.Relu,
                                                      bias=w_sel[0:R, b, R + D:SELW]).then_inc(adapter_hidden_ready.sem, 1)

                    attend("a")
                    ffn("f")
                    attend("b")
                    ffn("g")

                @block.vector
                def _(dve):
                    def norm(s, src, eps):
                        for k in range(NT):
                            nc.vector.bn_stats(stats[:, k, :], src[:, k, :]).then_inc(stats_done.sem, 1)
                        for k in range(NT):
                            dve.wait_ge(stats_done.sem, stats_done.at((s, k)))
                            nc.vector.bn_aggr(mv[:, k, :], stats[:, k, :]).then_inc(stats_done.sem, 1)
                        dve.wait_ge(stats_done.sem, stats_done.at((s, 2 * NT - 1)))
                        nc.vector.tensor_scalar(ve[:], mv[:, :, 1], eps, None, ALU.add).then_inc(variance_done.sem, 1)
                        dve.wait_ge(root_done.sem, root_done.at(s))
                        for k in range(NT):
                            nc.vector.tensor_scalar(xn[:, k, :], src[:, k, :], mv[:, k, 0:1], rstd[:, k:k + 1],
                                                         ALU.subtract, ALU.mult).then_inc(normed.sem, 1)

                    def split(L):
                        slot = ps_s[slot_s(("qk", L))]
                        dve.wait_ge(score_slot_filled.sem, score_slot_filled.at(("qk", L)))
                        for n, bias in enumerate((bq[L], bk[L]) if L == "a" else (bq_pos, bk_pos)):
                            nc.vector.tensor_scalar(qk[:, n, :], slot[:, n, :], bias[:], None, ALU.add).then_inc(qk_ready.sem, 1)
                        dve.wait_ge(score_slot_filled.sem, score_slot_filled.at(("v", L)))
                        nc.vector.tensor_tensor(
                            v[:, :, :, 0:DH],
                            ps_s[slot_s(("v", L))][:, 0, :].rearrange("p (t h d) -> p t h d", t=NT, h=NH),
                            bv[L][:].rearrange("p (u h d) -> p u h d", u=1, h=NH).to_broadcast([P, NT, NH, DH]),
                            ALU.add).then_inc(v_ready.sem, 1)
                        if L == "b":
                            split_positions()
                        for b in range(NB):
                            cols = slice(b * SEQ, (b + 1) * SEQ)
                            dve.wait_ge(part1_ready.sem, part1_ready.at((L, b)))
                            nc.vector.tensor_tensor(rest[:, :, cols], qk[:, :, cols], qk_parts[:, 0, :, cols],
                                                         ALU.subtract).then_inc(rest_ready.sem, 1)
                        for b in range(NB):
                            cols = slice(b * SEQ, (b + 1) * SEQ)
                            dve.wait_ge(part2_ready.sem, part2_ready.at((L, b)))
                            nc.vector.tensor_tensor(qk_parts[:, 2, :, cols], rest[:, :, cols],
                                                         qk_parts[:, 1, :, cols], ALU.subtract).then_inc(part3_ready.sem, 1)

                    def split_positions():
                        for n, (c, b) in enumerate(AK):
                            slot = ps_s[slot_s(("att", c, b))].rearrange("p a (g t) -> p (a g) t", g=2)
                            dve.wait_ge(pos_part1_ready.sem, pos_part1_ready.at((c, b)))
                            if n >= 2:
                                dve.wait_ge(pos_part3_ready.sem, pos_part3_ready.at(AK[n - 2]))
                            nc.vector.tensor_tensor(pos_rest[:, n % 2], slot, att_parts[:, n % 2, 0], ALU.subtract).then_inc(pos_rest_ready.sem, 1)
                            dve.wait_ge(pos_part2_ready.sem, pos_part2_ready.at((c, b)))
                            nc.vector.tensor_tensor(att_parts[:, n % 2, 2], pos_rest[:, n % 2], att_parts[:, n % 2, 1],
                                                         ALU.subtract).then_inc(pos_part3_ready.sem, 1)

                    def spread_out(qt):
                        for k in DK:
                            if k[0] == qt and d_engine[k] == "dve":
                                if qt:
                                    dve.wait_ge(score_slot_filled.sem, score_slot_filled.at(("S", "b", NCH // 2 - 1)))
                                dve.wait_ge(score_slot_filled.sem, score_slot_filled.at(("D", *k)))
                                nc.vector.tensor_copy(*spread_views(k)).then_inc(spread_by_dve.sem, 1)

                    def maxima(L, i):
                        b, qt = group(L, i // HC)
                        slot = ps_s[slot_s(("S", L, i))].rearrange("p a (g t) -> p (a g) t", g=2)
                        dve.wait_ge(score_slot_filled.sem, score_slot_filled.at(("S", L, i)))
                        if L == "a":
                            nc.vector.tensor_reduce(nmax[:, i % 2, :], slot, AX.X, ALU.max).then_inc(max_ready.sem, 1)
                        else:
                            if i % (NCH // 2) == 0:
                                dve.wait_ge(spread_by_act.sem, spread_by_act.at((qt, "p", DJ - 1)))
                                dve.wait_ge(spread_by_dve.sem, spread_by_dve.at((qt, "p", DJ - 2)))
                            if i >= 2:
                                dve.wait_ge(probs_turned.sem, probs_turned.at((L, i - 2, 1)))
                            for k in range(HC):
                                h = (i % HC) * HC + k
                                ins = nc.vector.tensor_tensor_reduce(
                                    out=prob[:, i % 2, k, :], in0=slot[:, k, :], in1=p2c[:, b * NH + h, :],
                                    scale=1.0, scalar=-3.4e38, op0=ALU.add, op1=ALU.max,
                                    accum_out=nmax[:, i % 2, k:k + 1])
                            ins.then_inc(scores_summed.sem, 1)
                            dve.wait_ge(scores_summed.sem, scores_summed.at(i))
                        scale = SCALE_A if L == "a" else SCALE_B
                        if L == "a":
                            dve.wait_ge(max_ready.sem, max_ready.at((L, i)))
                        nc.vector.tensor_scalar(nbias[:, i % 2, :], nmax[:, i % 2, :], -scale, None, ALU.mult).then_inc(exp_bias_ready.sem, 1)

                    def move_probs(L, i):
                        for hh in range(2):
                            if t_engine(L, i, hh) == "dve":
                                dve.wait_ge(probs_turned.sem, probs_turned.at((L, i, hh)))
                                if i >= 2:
                                    dve.wait_ge(values_weighed.sem, values_weighed.at((L, i - 2)))
                                nc.vector.tensor_copy(probT[:, i % 2, 2 * hh:2 * hh + 2],
                                                           ps_t[hh][:].rearrange("p (a b c) -> p a b c", a=2, b=2)).then_inc(probT_by_dve.sem, 1)

                    def normalize(L, n):
                        dve.wait_ge(probs_ready.sem, probs_ready.at((L, HC * n + HC - 1)))
                        nc.vector.reciprocal(rinv[:, n % 2, :], rsum[:, n % 2, :]).then_inc(inverse_ready.sem, 1)
                        dve.wait_ge(small_bank_filled.sem, small_bank_filled.at(("OB", L, n)))
                        dve.wait_ge(inverse_ready.sem, inverse_ready.at((L, n)))
                        nc.vector.tensor_tensor(
                            o_sb[:, n % 2], ps_m[n % 2][:].rearrange("p (h e) -> p h e", e=VC)[:, :, 0:DH],
                            rinv[:, n % 2, :].rearrange("p (h u) -> p h u", u=1).to_broadcast([P, NH, DH]),
                            ALU.mult).then_inc(heads_out_ready.sem, 1)

                    def add_out(L, n):
                        b, qt = group(L, n)
                        k = 2 * b + qt
                        if n == 0:
                            dve.wait_ge(bias_added.sem, bias_added.at(L))
                        dve.wait_ge(small_bank_filled.sem, small_bank_filled.at(("OP", L, n)))
                        nc.vector.tensor_tensor((x if L == "a" else y)[:, k, :], ps_m[n % 2][:, 0:P], xb[:, k, :],
                                                     ALU.add).then_inc(residual_added.sem, 1)

                    def attend(L):
                        split(L)
                        for kind, k in steps[L]:
                            if kind == "S":
                                maxima(L, k)
                            elif kind == "T":
                                move_probs(L, k)
                            elif kind == "D":
                                spread_out(k)
                            elif kind == "OT":
                                normalize(L, k)
                            elif kind == "OP":
                                add_out(L, k)

                    def ffn(s):
                        xT = xnT[:].rearrange("p (u n) -> p u n", u=1).to_broadcast([P, 2, TOK])
                        for k in range(NE // 2):
                            dve.wait_ge(score_slot_filled.sem, score_slot_filled.at(("rec", s, k)))
                            if k == 0:
                                dve.wait_ge(xnT_ready.sem, xnT_ready.at(s))
                            if k >= 2:
                                dve.wait_ge(losses_ready.sem, losses_ready.at((s, k - 2)))
                            nc.vector.tensor_tensor(diff[:, k % 2], ps_s[slot_s(("rec", s, k))][:], xT,
                                                         ALU.subtract).then_inc(diff_ready.sem, 1)
                        loss = ps_m[1][:, 0:NB * NE].rearrange("p (b e) -> p b e", b=NB)
                        numbers = iota.rearrange("p (u e) -> p u e", u=1).to_broadcast([P, NB, NE])

                        def wide(a):
                            return a[:].rearrange("p (b u) -> p b u", u=1).to_broadcast([P, NB, NE])

                        dve.wait_ge(small_bank_filled.sem, small_bank_filled.at(("loss", s)))
                        nc.vector.tensor_reduce(lmin[:], loss, AX.X, ALU.min).then_inc(choice_step.sem, 1)
                        dve.wait_ge(choice_step.sem, choice_step.at((s, 0)))
                        nc.vector.tensor_tensor(lkey[:], loss, wide(lmin), ALU.is_gt).then_inc(choice_step.sem, 1)
                        dve.wait_ge(choice_step.sem, choice_step.at((s, 1)))
                        nc.vector.scalar_tensor_tensor(out=lkey[:], in0=lkey[:], scalar=float(NE), in1=numbers,
                                                            op0=ALU.mult, op1=ALU.add).then_inc(choice_step.sem, 1)
                        dve.wait_ge(choice_step.sem, choice_step.at((s, 2)))
                        nc.vector.tensor_reduce(kmin[:], lkey[:], AX.X, ALU.min).then_inc(choice_step.sem, 1)
                        dve.wait_ge(choice_step.sem, choice_step.at((s, 3)))
                        nc.vector.tensor_tensor(onehot[:], numbers, wide(kmin), ALU.is_equal).then_inc(choice_step.sem, 1)
                        dve.wait_ge(choice_step.sem, choice_step.at((s, 4)))
                        nc.vector.tensor_tensor(picked[:, 0], w_all[:], one_hot_wide(0), ALU.mult).then_inc(picked_by_dve.sem, 1)
                        for b in range(NB):
                            if b == 0:
                                dve.wait_ge(picked_by_dve.sem, picked_by_dve.at(s))
                            else:
                                dve.wait_ge(picked_by_pool.sem, picked_by_pool.at(s))
                            nc.vector.tensor_reduce(w_sel[:, b, :], picked[:, b].rearrange("p e c -> p c e"),
                                                         AX.X, ALU.add).then_inc(adapter_ready.sem, 1)
                        dve.wait_ge(score_slot_filled.sem, score_slot_filled.at(("ffo", s)))
                        nc.vector.tensor_tensor(
                            x[:], x[:], ps_s[slot_s(("ffo", s))][:, 0, :].rearrange("p (t n) -> p t n", t=NT), ALU.add).then_inc(ffn_added.sem, 1)

                    dve.wait_ge(x_loaded.sem, x_loaded.at("x"))
                    norm("a", x, EPS_LN)
                    attend("a")
                    dve.wait_ge(residual_added.sem, residual_added.at(("a", NG - 1)))
                    norm("f", x, EPS_LN)
                    ffn("f")
                    dve.wait_ge(ffn_added.sem, ffn_added.at("f"))
                    norm("b", x, EPS_LN)
                    attend("b")
                    dve.wait_ge(residual_added.sem, residual_added.at(("b", NG - 1)))
                    norm("n", y, EPS_B)
                    dve.wait_ge(normed.sem, normed.at(("n", NT - 1)))
                    nc.vector.tensor_tensor(
                        y, xn[:], ln_s[:].rearrange("p (u n) -> p u n", u=1).to_broadcast([P, NT, D]), ALU.mult).then_inc(inner_norm_step.sem, 1)
                    dve.wait_ge(inner_norm_step.sem, inner_norm_step.at("s"))
                    dve.wait_ge(bias_added.sem, bias_added.at("n"))
                    nc.vector.tensor_tensor(x[:], y, xb[:], ALU.add).then_inc(inner_norm_step.sem, 1)
                    dve.wait_ge(inner_norm_step.sem, inner_norm_step.at("x"))
                    norm("g", x, EPS_LN)
                    ffn("g")

                @block.gpsimd
                def _(pool):
                    def root(s):
                        pool.wait_ge(variance_done.sem, variance_done.at(s))
                        nc.gpsimd.tensor_tensor(rstd[:], ve[:], neg_half[:], ALU.pow).then_inc(root_done.sem, 1)

                    def add_bias(key, src, bias):
                        nc.gpsimd.tensor_tensor(
                            xb[:], src[:], bias[:].rearrange("p (u n) -> p u n", u=1).to_broadcast([P, NT, D]),
                            ALU.add).then_inc(bias_added.sem, 1)

                    def pick(s):
                        pool.wait_ge(choice_step.sem, choice_step.at((s, 4)))
                        nc.gpsimd.tensor_tensor(picked[:, 1], w_all[:], one_hot_wide(1), ALU.mult).then_inc(picked_by_pool.sem, 1)

                    pool.wait_ge(x_loaded.sem, x_loaded.at("x"))
                    root("a")
                    add_bias("a", x, bo["a"])
                    root("f")
                    pick("f")
                    root("b")
                    pool.wait_ge(normed.sem, normed.at(("b", NT - 1)))
                    add_bias("b", xn, bo["b"])
                    root("n")
                    add_bias("n", x, ln_b)
                    root("g")
                    pick("g")

            nc.all_engine_barrier()
            for s in turn_sems:
                nc.gpsimd.sem_clear(s)
            nc.all_engine_barrier()


def kernel(**inputs):
    import numpy as _np
    import concourse.bacc as _bacc
    from concourse import mybir as _mybir
    from concourse.bass_utils import run_bass_kernel_spmd as _run

    nc = _bacc.Bacc("TRN2", target_bir_lowering=False, num_devices=1)
    arrays = {name: _np.ascontiguousarray(a) for name, a in inputs.items() if name != "L0_attn_b_attention_mask"}
    arrays["constants"] = constant_table()
    aps = {n: nc.dram_tensor(n, a.shape, _mybir.dt.from_np(a.dtype), kind="ExternalInput").ap()
           for n, a in arrays.items()}
    aps["out"] = nc.dram_tensor("out", inputs["L0_attn_a_x"].shape, _mybir.dt.float32, kind="ExternalOutput").ap()
    build(nc, aps)
    return _run(nc, [arrays], core_ids=[0]).results[0]["out"]
```

```python
from contextlib import ExitStack

import numpy as np

import concourse.bass as bass
from concourse import mybir
from concourse.alu_op_type import AluOpType as ALU

F32 = mybir.dt.float32
BF16 = mybir.dt.bfloat16
ACT = mybir.ActivationFunctionType
AX = mybir.AxisListType

P = 128
D = 128
NH = 16
DH = D // NH
SEQ = 256
NB = 2
NT = NB * SEQ // P
TOK = NB * SEQ
HC = 4
NG = NB * 2
NCH = NG * NH // HC
BH = NB * NH
VC = 32
PARTS = 3
KS = PARTS * PARTS * DH
NE, HE, R = 8, 32, 64
SELW = R + D + 1
SPAN, MAX_REL = 32, 64
NIDX = 32
CEN_C, CEN_P = SPAN + SPAN // 2 - 1, SPAN - SPAN // 2 + 1
EPS_LN, EPS_B = 1e-5, 1e-7
SCALE_A = 1.0 / float(np.sqrt(np.float32(DH)))
SCALE_B = 1.0 / float(np.sqrt(np.float32(3 * DH)))
RELW = 2 * SEQ


def relative_buckets():
    rel = np.arange(-(SEQ - 1), SEQ)
    mid = SPAN // 2
    a = np.where((rel < mid) & (rel > -mid), mid - 1, np.abs(rel)).astype(np.float32)
    steps = np.log(a / np.float32(mid)) / np.log(np.float32((MAX_REL - 1) / mid)) * np.float32(mid - 1)
    log_pos = np.ceil(steps.astype(np.float32)) + mid
    return np.where(a <= mid, a, log_pos * np.sign(rel)).astype(np.int32)


def constant_table():
    bucket = dict(zip(range(-(SEQ - 1), SEQ), relative_buckets()))
    order_c = list(range(0, 16)) + list(range(48, 64))
    order_p = list(range(0, 17)) + list(range(49, 64))
    ohc = np.zeros((P, RELW), np.float32)
    ohp = np.zeros((P, RELW), np.float32)
    for r, _ in bucket.items():
        c = int(np.clip(bucket[r] + SPAN, 0, 2 * SPAN - 1))
        p = int(np.clip(-bucket[-r] + SPAN, 0, 2 * SPAN - 1))
        for part in range(PARTS):
            if c != CEN_C:
                ohc[part * NIDX + order_c.index(c), SEQ - 1 - r] = 1.0
            if p != CEN_P:
                ohp[part * NIDX + order_p.index(p), SEQ - 1 + r] = 1.0
    mask = np.zeros((P, NH), np.float32)
    for p in range(P):
        h = p % NH
        mask[p, (h % 4) * 4 + h // 4] = 1.0
    iota = np.broadcast_to(np.arange(NE, dtype=np.float32), (P, NE))
    return np.ascontiguousarray(np.concatenate([np.eye(P, dtype=np.float32), mask, iota, ohc, ohp], axis=1))


C_ID, C_MASK = 0, P
C_IOTA = C_MASK + NH
CW = C_IOTA + NE


class Signal:

    def __init__(self, sem, keys, step=1):
        self.sem, self.step = sem, step
        self.place = {k: n + 1 for n, k in enumerate(keys)}
        assert len(self.place) == len(keys)

    def at(self, key):
        return self.place[key] * self.step


PAIRS = 8 // NB
CHUNKS = [(L, p, i) for L in "ab" for p in range(PAIRS) for i in range(NCH)]
NUMBER = {c: g for g, c in enumerate(CHUNKS)}
POS = 8
DJ = 8


def group(n):
    L, p, i = CHUNKS[HC * n]
    m = i // HC
    return (L, p, m // 2, m % 2) if L == "a" else (L, p, m % 2, m // 2)


def front_steps(L, p):
    slots = [[("norm1", L, p)], [], [("norm2", L, p)], [("xt", L, p)], [],
             [("q", L, p)], [("k", L, p)]]
    if L == "b":
        for n in range(POS + 1):
            slots.append(([("att", p, n)] if n < POS else []) + ([("att_late", p, n - 1)] if n else []))
    return slots + [[("split1", L, p)], [("v", L, p)], [("split2", L, p), ("load_qk", L, p)]]


def ffn_steps(s, p):
    slots = [[("norm1", s, p)], [], [("norm2", s, p)], [("xt", s, p)], [], [("h", s, p, 0)], [("h", s, p, 1)], []]
    slots += [[("rec", s, p, e)] + ([("square", s, p, e - 1)] if e else []) for e in range(NE)]
    slots += [[("square", s, p, NE - 1)], [("loss", s, p)]] + [[("pick", s, p, n)] for n in range(4)]
    slots += [[("act", s, p)], [], [("ffo", s, p)]]
    if s == "g":
        slots.append([("store", p)])
    return slots


def inner_steps(p):
    return [[("norm1", "n", p)], [], [("norm2", "n", p), ("inner", p)], []]


BANK_JOBS = ("xt", "q", "k", "att", "v", "h", "rec", "loss", "act", "ffo", "OB", "OT", "OP")
JOB_GAP, ATT_GAP = 2, 2


def make_plan():
    last = PAIRS - 1
    assert PAIRS == 4
    sides = {
        ("a", 0): [(0, front_steps("a", 1))],
        ("a", 1): [(0, front_steps("a", 2)), (20, ffn_steps("f", 0))],
        ("a", 2): [(0, front_steps("a", 3))],
        ("a", 3): [(0, front_steps("b", 0)), (0, ffn_steps("f", 1))],
        ("b", 0): [(6, front_steps("b", 1)), (0, ffn_steps("f", 2))],
        ("b", 1): [(22, inner_steps(0)), (0, front_steps("b", 2)), (0, ffn_steps("f", 3))],
        ("b", 2): [(22, inner_steps(1)), (0, front_steps("b", 3)), (0, ffn_steps("g", 0))],
        ("b", 3): [(22, inner_steps(2)), (0, ffn_steps("g", 1)), (0, ffn_steps("g", 2))],
    }
    plan = [s for slot in front_steps("a", 0) for s in slot] + [("v_copy", "a", 0)]
    due = []
    done = set()
    count = start = last_job = 0
    side = []

    def emit(steps, side):
        nonlocal count, due, last_job
        plan.extend(steps)
        count += 1
        steps_due = [s for when, s in sorted(d for d in due if d[0] <= count)]
        plan.extend(steps_due)
        due = [d for d in due if d[0] > count]
        for s in steps:
            if s[0] == "PV" and s[3] % HC == HC - 1:
                n = NUMBER[s[1:]] // HC
                plan.append(("OM", n))
                due += [(count + 3, ("OB", n)), (count + 6, ("OT", n)), (count + 9, ("OP", n))]
        for step in steps_due:
            if step[0] in BANK_JOBS:
                last_job = count
        if side:
            jobs = [s[0] for s in side[0][1] if s[0] in BANK_JOBS]
            gap = ATT_GAP if jobs == ["att"] else JOB_GAP
            if count - start >= side[0][0] and (not jobs or count - last_job >= gap):
                plan.extend(side.pop(0)[1])
                if jobs:
                    last_job = count

    def weigh(g):
        if g < 0 or g in done:
            return []
        done.add(g)
        nxt = [("v_copy",) + CHUNKS[g + 1][:2]] if g % NCH == NCH - 1 and g + 1 < len(CHUNKS) else []
        return [("PV",) + CHUNKS[g]] + nxt

    turned = set()

    def turn(g):
        if g < 0 or g in turned:
            return []
        turned.add(g)
        return [("T",) + CHUNKS[g]]

    for L in "ab":
        for p in range(PAIRS):
            start = count
            side = [(0, slot) for _, slot in side]
            side += [(first, slot) for first, slots in sides[L, p] for slot in slots]
            for i in range(NCH):
                g = NUMBER[L, p, i]
                if L == "b" and i % (NCH // 2) == 0:
                    jobs = [(p, i * 2 // NCH, c, j) for c in "cp" for j in range(DJ)]
                    for m, key in enumerate(jobs):
                        emit([("D",) + key], side)
                        if m == 1:
                            emit(turn(g - 1), side)
                        if m == 3:
                            emit(weigh(g - 2), side)
                        if m == 6:
                            emit(weigh(g - 1), side)
                emit([("S", L, p, i)], side)
                for steps in (turn(g - 1), weigh(g - 2)):
                    if steps:
                        emit(steps, side)
    emit(turn(len(CHUNKS) - 1), side)
    emit(weigh(len(CHUNKS) - 2), side)
    emit(weigh(len(CHUNKS) - 1), side)
    while due:
        emit([], side)
    for _, slot in side:
        plan.extend(slot)
    for slot in inner_steps(last) + ffn_steps("g", last):
        plan.extend(slot)
    return plan


def build(nc, t):
    with ExitStack() as ctx:
        def sb(name, shape, dt=F32):
            return ctx.enter_context(nc.sbuf_tensor(name, shape, dt))

        def sem(name):
            return ctx.enter_context(nc.semaphore(name))

        cst = sb("cst", [P, CW])
        ident = cst[:, C_ID:C_ID + P]
        iota = cst[:, C_IOTA:C_IOTA + NE]
        oh_c = sb("oh_c", [P, RELW], BF16)
        oh_p = sb("oh_p", [P, RELW], BF16)
        ones = sb("ones", [P, P])
        neg_half = sb("neg_half", [P, NT])
        wq, wk, wv, wo = ({L: sb(f"{n}_{L}", [P, D]) for L in "ab"} for n in ("wq", "wk", "wv", "wo"))
        bq, bk = ({L: sb(f"{n}_{L}", [P, 1]) for L in "ab"} for n in ("bq", "bk"))
        bv, bo = ({L: sb(f"{n}_{L}", [P, D]) for L in "ab"} for n in ("bv", "bo"))
        centre = sb("centre", [P, 2])
        ln_s, ln_b = sb("ln_s", [P, D]), sb("ln_b", [P, D])
        pos_w = {y: sb(f"pos_w_{y}", [P, 4, NIDX, 4]) for y in "cp"}
        w_base = sb("w_base", [P, D])
        wd1 = sb("wd1", [P, NE, HE])
        bd1 = sb("bd1", [P, 2])
        wd2 = sb("wd2", [P, NE, D])
        bd2 = sb("bd2", [P, NE])
        w_all = sb("w_all", [P, NE, SELW])

        x = sb("x", [P, PAIRS, NT, D])
        xn = sb("xn", [P, 2, NT, D])
        xnT = sb("xnT", [P, TOK])
        stats = sb("stats", [P, NT, 6])
        mv = sb("mv", [P, NT, 2])
        ve = sb("ve", [P, NT])
        rstd = sb("rstd", [P, NT])
        parts = sb("parts", [P, PARTS * 2 * TOK], BF16)
        qk_parts = parts[:].rearrange("p (s n t) -> p s n t", s=PARTS, n=2)
        att_parts = parts[:].rearrange("p (n s g t) -> p n s g t", n=2, s=PARTS, g=2)
        v = sb("v", [P, NT, NH, VC])
        stack_0 = sb("stack_0", [KS, 2, NB, NH, SEQ], BF16)
        prob = sb("prob", [P, 2, HC, SEQ])
        probT = sb("probT", [P, 2, HC, 2, P])
        qk = sb("qk", [P, 2, TOK])
        rest = sb("rest", [P, 2, TOK])
        pos_rest = rest[:].rearrange("p n (g t) -> p n g t", g=2)
        hT, diff = qk, rest
        nmax = sb("nmax", [P, 2, HC])
        nbias = sb("nbias", [P, 2, HC])
        rsum = sb("rsum", [P, 2, NH])
        rinv = sb("rinv", [P, 2, NH])
        o_sb = sb("o_sb", [P, NH, DH])
        oT = sb("oT", [P, P])
        o_turned = sb("o_turned", [P, HC, P])
        plain = sb("plain", [P, 2, TOK])
        new_v = plain[:, 0, :].rearrange("p (t h d) -> p t h d", t=NT, h=NH)
        ffn_xn = plain[:, 1, :].rearrange("p (t n) -> p t n", t=NT)
        att = {y: sb(f"att_{y}", [PARTS * NIDX, NB, NH, SEQ], BF16) for y in "cp"}
        c2p = sb("c2p", [P, 2, BH, P])
        p2c = sb("p2c", [P, BH, SEQ])
        stack_1 = c2p[:].rearrange("p a b c -> p (a b c)").bitcast(BF16).rearrange(
            "p (n b h t) -> p n b h t", n=2, b=NB, h=NH)[0:KS]
        stacks = [stack_0[:], stack_1]
        tables = c2p[:].rearrange("p a b c -> p (a b c)")[:, 0:2 * RELW]
        aT = sb("aT", [R + 1, TOK])
        w_sel = sb("w_sel", [P, NB, SELW])
        loss_p = sb("loss_p", [P, NB, NE])
        lmin, lkey, kmin, onehot = (sb(n, s) for n, s in (
            ("lmin", [P, NB]), ("lkey", [P, NB, NE]), ("kmin", [P, NB]), ("onehot", [P, NB, NE])))
        spare = p2c[:].rearrange("p a b -> p (a b)")
        rel_sb = spare[0:2 * SPAN, 0:D]
        relT = spare[:, D:D + 2 * SPAN]
        posT = spare[:, 2 * D:2 * D + 2 * SPAN]
        dpos = {c: spare[:, (3 + k) * D:(3 + k) * D + NIDX] for k, c in enumerate("cp")}
        rows = {n: spare[:, (5 + k) * D:(6 + k) * D] for k, n in enumerate(("q", "k", "v", "o"))}
        raw = {n: spare[:, (9 + k) * D:(10 + k) * D] for k, n in enumerate("qk")}

        ps_s = [ctx.enter_context(nc.psum_tensor(f"ps_s{n}", [P, 2, 512], F32)) for n in range(2)]
        ps_t = [ctx.enter_context(nc.psum_tensor(f"ps_t{n}", [P, 512], F32)) for n in range(2)]
        ps_o = ctx.enter_context(nc.psum_tensor("ps_o", [P, 512], F32))
        ps_m = ctx.enter_context(nc.psum_tensor("ps_m", [P, 512], F32))

        q_dram = nc.dram_tensor("q_scratch", (NB, PARTS, PARTS, P, SEQ), BF16, kind="Internal").ap()
        k_dram = nc.dram_tensor("k_scratch", (NB, PARTS, P, SEQ), BF16, kind="Internal").ap()
        att_dram = nc.dram_tensor("att_scratch", (2, NB, PARTS, P, 4 * SEQ), BF16, kind="Internal").ap()

        s_cst, s_x, s_load, s_rows, s_wd2 = sem("s_cst"), sem("s_x"), sem("s_load"), sem("s_rows"), sem("s_wd2")
        s_zero, s_tr, s_trc, s_cast, s_pos, s_perm, s_bb = (
            sem(n) for n in ("s_zero", "s_tr", "s_trc", "s_cast", "s_pos", "s_perm", "s_bb"))
        qkv_c = t["L0_attn_a_W_qkv"].rearrange("(h c) i -> c h i", c=3 * DH)
        qkv_h = t["L0_attn_a_W_qkv"].rearrange("(h c) i -> h c i", c=3 * DH)
        bqkv_c = t["L0_attn_a_b_qkv"].rearrange("(h c u) -> c h u", c=3 * DH, u=1)
        bqkv_h = t["L0_attn_a_b_qkv"].rearrange("(h c) -> h c", c=3 * DH)

        def column(name):
            return t[name].rearrange("(h d u) -> d h u", d=DH, u=1)

        def everywhere(name):
            return t[name].rearrange("(u n) -> u n", u=1).to_broadcast([P, D])

        loads = [
            (w_base[:], t["L0_ffn_W_base"]),
            (wv["b"][:], t["L0_attn_b_Wv"]), (wo["b"][:], t["L0_attn_b_Wo"]),
            (raw["q"], t["L0_attn_b_Wq"]), (raw["k"], t["L0_attn_b_Wk"]),
            (rel_sb, t["L0_attn_b_rel_embeddings"]),
            (bq["a"][:], bqkv_c[0:DH]), (bk["a"][:], bqkv_c[DH:2 * DH]),
            (bv["a"][:].rearrange("p (h d) -> p h d", d=DH),
             bqkv_h[:, 2 * DH:].rearrange("(u h) d -> u h d", u=1).to_broadcast([P, NH, DH])),
            (bo["a"][:], everywhere("L0_attn_a_b_out")),
            (bq["b"][:], column("L0_attn_b_bq")), (bk["b"][:], column("L0_attn_b_bk")),
            (bv["b"][:], everywhere("L0_attn_b_bv")), (bo["b"][:], everywhere("L0_attn_b_bo")),
            (ln_s[:], everywhere("L0_attn_b_ln_scale")), (ln_b[:], everywhere("L0_attn_b_ln_bias")),
            (wd1[:], t["L0_ffn_Wd1"].rearrange("e d h -> d e h")),
            (bd1[:], t["L0_ffn_bd1"].rearrange("(j e) h -> (e h) j", j=2)),
            (bd2[:], t["L0_ffn_bd2"].rearrange("e d -> d e")),
        ]
        loads_zeroed = [
            (w_all[:, :, 0:R], t["L0_ffn_Wa_down"].rearrange("e d r -> d e r")),
            (w_all[0:R, :, R:R + D], t["L0_ffn_Wa_up"].rearrange("e r o -> r e o")),
            (w_all[R:R + 1, :, R:R + D], t["L0_ffn_ba_up"].rearrange("(u e) o -> u e o", u=1)),
            (w_all[0:R, :, R + D:SELW], t["L0_ffn_ba_down"].rearrange("e (r u) -> r e u", u=1)),
            (aT[R:R + 1, 0:D], t["L0_ffn_b_base"].rearrange("(u n) -> u n", u=1)),
        ] + [(wd2[HE * (e % 4):HE * (e % 4 + 1), e, :], t["L0_ffn_Wd2"][e]) for e in range(NE)]

        ctx.enter_context(nc.allow_non_contiguous_dma(reason="bias vectors laid out one element per partition"))
        with nc.Block() as block:
            @block.sync
            def _(sp):
                sp.dma_start(cst[:], t["constants"][:, 0:CW]).then_inc(s_cst, 16)
                sp.dma_start(tables, t["constants"][:, CW:]).then_inc(s_cst, 16)
                sp.dma_start(rows["q"], qkv_c[0:DH]).then_inc(s_rows, 16)
                sp.dma_start(rows["k"], qkv_c[DH:2 * DH]).then_inc(s_rows, 16)
                sp.dma_start(rows["v"], qkv_h[:, 2 * DH:]).then_inc(s_rows, 16)
                sp.dma_start(rows["o"], t["L0_attn_a_W_out"]).then_inc(s_rows, 16)
                sp.dma_start(x[:].rearrange("p a t d -> p (a t) d"),
                             t["L0_attn_a_x"].rearrange("b (t p) d -> p (b t) d", p=P)).then_inc(s_x, 16)
                for dst, src in loads:
                    sp.dma_start(dst, src).then_inc(s_load, 16)
                sp.wait_ge(s_zero, 3)
                for dst, src in loads_zeroed:
                    sp.dma_start(dst, src).then_inc(s_wd2, 16)
                sp.wait_ge(s_x, 16)
                sp.wait_ge(s_load, 16 * len(loads))
                sp.wait_ge(s_wd2, 16 * len(loads_zeroed))

            @block.gpsimd
            def _(pool):
                nc.gpsimd.memset(wd2[:], 0.0).then_inc(s_zero, 1)
                nc.gpsimd.memset(w_all[:], 0.0).then_inc(s_zero, 1)
                nc.gpsimd.memset(neg_half[:], -0.5).then_inc(s_zero, 1)
                nc.gpsimd.memset(ones[:], 1.0).then_inc(s_zero, 1)
                nc.gpsimd.memset(v[:], 0.0).then_inc(s_zero, 1)
                pool.wait_ge(s_zero, 5)
                pool.wait_ge(s_wd2, 16 * len(loads_zeroed))
                nc.gpsimd.tensor_tensor(
                    w_all[R:R + 1, :, R:R + D], w_all[R:R + 1, :, R:R + D],
                    aT[R:R + 1, 0:D].rearrange("u (e n) -> u e n", e=1).to_broadcast([1, NE, D]),
                    ALU.add).then_inc(s_bb, 1)
                pool.wait_ge(s_bb, 1)
                nc.gpsimd.memset(aT[R:R + 1, :], 1.0).then_inc(s_bb, 1)
                pool.wait_ge(s_bb, 2)

            @block.tensor
            def _(pe):
                pe.wait_ge(s_cst, 32)
                pe.wait_ge(s_rows, 16 * 4)
                for k, n in enumerate("qkvo"):
                    ins = nc.tensor.transpose(ps_m[:, k * P:(k + 1) * P], rows[n], ident)
                ins.then_inc(s_tr, 1)
                pe.wait_ge(s_load, 16 * len(loads))
                nc.tensor.transpose(ps_o[:, 0:2 * SPAN], rel_sb, ident[0:2 * SPAN, 0:2 * SPAN]).then_inc(s_tr, 1)
                pe.wait_ge(s_trc, 5)
                pe.wait_ge(s_perm, 2)
                nc.tensor.matmul(ps_t[0][:, 0:2 * SPAN], wk["b"][:], relT, start=True, stop=True).then_inc(s_tr, 1)

            @block.vector
            def _(dve):
                dve.wait_ge(s_cst, 32)
                nc.vector.tensor_copy(oh_c[:], tables[:, 0:RELW])
                nc.vector.tensor_copy(oh_p[:], tables[:, RELW:])
                dve.wait_ge(s_tr, 1)
                for k, w in enumerate((wq["a"], wk["a"], wv["a"], wo["a"])):
                    nc.vector.tensor_copy(w[:], ps_m[:, k * P:(k + 1) * P]).then_inc(s_trc, 1)
                dve.wait_ge(s_load, 16 * len(loads))
                for n, w in (("q", wq["b"]), ("k", wk["b"])):
                    nc.vector.tensor_copy(w[:].rearrange("p (d h) -> p d h", d=DH),
                                          raw[n].rearrange("p (h d) -> p d h", d=DH)).then_inc(s_perm, 1)
                dve.wait_ge(s_tr, 2)
                nc.vector.tensor_copy(relT, ps_o[:, 0:2 * SPAN]).then_inc(s_trc, 1)
                dve.wait_ge(s_tr, 3)
                nc.vector.tensor_scalar(posT, ps_t[0][:, 0:2 * SPAN], bk["b"][:], None, ALU.add).then_inc(s_pos, 1)
                dve.wait_ge(s_pos, 1)
                nc.vector.tensor_copy(centre[:, 0:1], posT[:, CEN_P:CEN_P + 1])
                nc.vector.tensor_copy(centre[:, 1:2], posT[:, CEN_C:CEN_C + 1])
                for c, cen, cut, nxt in (("c", CEN_C, 16, 48), ("p", CEN_P, 17, 49)):
                    nc.vector.tensor_scalar(dpos[c][:, 0:cut], posT[:, 0:cut], posT[:, cen:cen + 1], None,
                                            ALU.subtract).then_inc(s_pos, 1)
                    nc.vector.tensor_scalar(dpos[c][:, cut:], posT[:, nxt:], posT[:, cen:cen + 1], None,
                                            ALU.subtract).then_inc(s_pos, 1)
                dve.wait_ge(s_pos, 5)
                for c in "cp":
                    for g in range(4):
                        m = cst[:, C_MASK + 4 * g:C_MASK + 4 * g + 4].rearrange("p (u h) -> p u h", u=1)
                        nc.vector.tensor_tensor(
                            pos_w[c][:, g], dpos[c].rearrange("p (i u) -> p i u", u=1).to_broadcast([P, NIDX, 4]),
                            m.to_broadcast([P, NIDX, 4]), ALU.mult)

        nc.all_engine_barrier()

        plan = make_plan()

        def order(*kinds):
            return [s[1:] for s in plan if s[0] in kinds]

        def signal(name, keys, step=1):
            return Signal(sem(name), list(keys), step)

        s_jobs = [s for s in plan if s[0] in ("S", "D")]
        m_jobs = [s for s in plan if s[0] in ("xt", "q", "k", "att", "v", "h", "rec", "loss", "act", "ffo", "OB", "OT", "OP")
                  and not (s[0] == "att" and s[2] >= POS)]
        s_place = {s: n for n, s in enumerate(s_jobs)}
        m_place = {s: n for n, s in enumerate(m_jobs)}
        fronts = order("q")
        norms, turns = order("norm2"), order("xt")
        ffns = order("loss")
        n_groups = len(CHUNKS) // HC

        parts_stored = {b: signal(f"parts_stored{b}", [k + (n,) for k in fronts for n in range(1 + PARTS)], 16) for b in range(NB)}
        stack_loaded = {b: signal(f"stack_loaded{b}", [k + (n,) for k in fronts for n in range(1 + PARTS)], 16) for b in range(NB)}
        pos_parts_stored = {m: signal(f"pos_parts_stored{m}", [k for k in order("att_late") if k[1] % 2 == m], 16) for m in range(2)}
        pos_stack_loaded = {c: signal(f"pos_stack_loaded_{c}", [(p, b) for p in range(PAIRS) for b in range(NB)], 16) for c in "cp"}
        out_stored = signal("out_stored", order("store"), 16)

        score_slot_filled = signal("score_slot_filled", s_jobs)
        small_bank_filled = signal("small_bank_filled", m_jobs)
        probs_turned = signal("probs_turned", [c + (hh,) for c in CHUNKS for hh in range(2)])
        values_weighed = signal("values_weighed", CHUNKS)

        stats_done = signal("stats_done", [k + (n,) for k in order("norm1") for n in range(2 * NT)])
        variance_done = signal("variance_done", order("norm1"))
        root_done = signal("root_done", order("norm1"))
        normed = signal("normed", [k + (n,) for k in norms for n in range(NT)])
        bias_added = signal("bias_added", [s[1:] for s in plan if (s[0] == "xt" and s[1] in "ab") or (s[0] == "norm1" and s[1] == "n")])
        xnT_ready = signal("xnT_ready", turns)
        plain_ready = signal("plain_ready", [(p, n) for L, p in fronts if L == "b" for n in range(2)])
        qk_ready_a = signal("qk_ready_a", [(p, n) for L, p in fronts if L == "a" for n in range(2)])
        qk_ready_b = signal("qk_ready_b", [(p, n) for L, p in fronts if L == "b" for n in range(2)])
        new_v_ready = signal("new_v_ready", order("v"))
        v_ready = signal("v_ready", order("v_copy"))
        split_keys = [k + (b,) for k in fronts for b in range(NB)]
        part1_ready, part2_ready = signal("part1_ready", split_keys), signal("part2_ready", split_keys)
        rest_ready, part3_ready = signal("rest_ready", split_keys), signal("part3_ready", split_keys)
        pos_keys = order("att_late")
        pos_part1_ready, pos_part2_ready = signal("pos_part1_ready", pos_keys), signal("pos_part2_ready", pos_keys)
        pos_rest_ready, pos_part3_ready = signal("pos_rest_ready", pos_keys), signal("pos_part3_ready", pos_keys)
        spread_by_act = signal("spread_by_act", [k for k in order("D") if k[3] % 2 == 1])
        spread_by_dve = signal("spread_by_dve", [k for k in order("D") if k[3] % 2 == 0])
        scores_summed = signal("scores_summed", [c for c in CHUNKS if c[0] == "b"])
        max_ready = signal("max_ready", [c for c in CHUNKS if c[0] == "a"])
        exp_bias_ready = signal("exp_bias_ready", CHUNKS)
        probs_ready = signal("probs_ready", CHUNKS)

        def t_engine(chunk, hh):
            if hh == 0:
                return "dve"
            return "act" if chunk[0] == "b" or chunk[2] % 2 == 0 else "dve"

        halves = [(c, hh) for c in CHUNKS for hh in range(2)]
        moved_by = {e: signal(f"probT_by_{e}", [k for k in halves if t_engine(*k) == e]) for e in ("act", "dve")}
        inverse_ready = signal("inverse_ready", range(n_groups))
        out_moved = signal("out_moved", range(n_groups))
        heads_out_ready = signal("heads_out_ready", range(n_groups))
        outT_ready = signal("outT_ready", range(n_groups))
        residual_added = signal("residual_added", range(n_groups))
        hidden_ready = signal("hidden_ready", order("h"))
        diff_ready = signal("diff_ready", order("rec"))
        losses_ready = signal("losses_ready", order("square"))
        choice_step = signal("choice_step", [k + (n,) for k in ffns for n in range(5)])
        expert_added = signal("expert_added", [k + (b, e) for k in ffns for e in range(NE) for b in range(NB)])
        adapter_hidden_ready = signal("adapter_hidden_ready", [k + (b,) for k in ffns for b in range(NB)])
        ffn_added = signal("ffn_added", ffns)
        inner_norm_step = signal("inner_norm_step", [(p, n) for p in range(PAIRS) for n in range(2)])

        def before(keys, key):
            n = keys.index(key)
            return keys[n - 1] if n else None

        last_ffn_before, last_front_before = {}, {}
        seen_ffn = seen_front = None
        for kind, *key in plan:
            if kind == "norm1" and key[0] != "n":
                last_ffn_before[tuple(key)], last_front_before[tuple(key)] = seen_ffn, seen_front
                if key[0] in "fg":
                    seen_ffn = tuple(key)
                else:
                    seen_front = tuple(key)

        def last_chunk_of_group(n):
            return CHUNKS[HC * n + HC - 1]

        def take_s(pe, job):
            n = s_place[job]
            if n >= 2:
                kind, *key = s_jobs[n - 2]
                key = tuple(key)
                if kind == "S":
                    read_out = probs_ready if key[0] == "a" else scores_summed
                else:
                    read_out = spread_by_act if key[3] % 2 else spread_by_dve
                pe.wait_ge(read_out.sem, read_out.at(key))
            return ps_s[n % 2]

        def slot_s(job):
            return ps_s[s_place[job] % 2]

        def take_m(pe, job):
            n = m_place[job]
            if n:
                kind, *key = m_jobs[n - 1]
                key = tuple(key)
                if kind in ("q", "k"):
                    read_out = qk_ready_a if key[0] == "a" else plain_ready
                    key = (key[1], "qk".index(kind))
                elif kind == "loss":
                    read_out, key = choice_step, key + (1,)
                elif kind == "act":
                    read_out, key = adapter_hidden_ready, key + (NB - 1,)
                elif kind in ("OB", "OT", "OP"):
                    read_out = {"OB": heads_out_ready, "OT": outT_ready, "OP": residual_added}[kind]
                    key = key[0]
                else:
                    read_out = {"xt": xnT_ready, "att": pos_rest_ready, "v": new_v_ready, "h": hidden_ready,
                                "rec": diff_ready, "ffo": ffn_added}[kind]
                pe.wait_ge(read_out.sem, read_out.at(key))

        def spread_views(k):
            p, qt, c, j = k
            src = slot_s(("D",) + k).rearrange("p a (n b) -> p b (a n)", b=BH)
            if c == "c":
                return c2p[:, j // 4, :, (j % 4) * 32:(j % 4 + 1) * 32], src
            return p2c[:, :, j * 32:(j + 1) * 32], src

        def stack(L, p):
            return stacks[p % 2 if L == "a" else 0]

        def last_reader_of_stack(L, p):
            if L == "a":
                return ("a", p - 2, NCH - 1) if p >= 2 else None
            return ("b", p - 1, NCH - 1) if p else ("a", PAIRS - 2 + PAIRS % 2, NCH - 1)

        x_rows = t["L0_attn_a_x"].rearrange("b (t p) d -> (b t) p d", p=P)
        out_rows = t["out"].rearrange("b (t p) d -> (b t) p d", p=P)
        chunk_before_half = {}
        for p in range(PAIRS):
            for qt in range(2):
                chunk_before_half[p, qt] = CHUNKS[NUMBER["b", p, qt * NCH // 2] - 1]

        with nc.Block() as block:

            @block.sync
            def _(sp):
                def store_qk(L, p, b):
                    sp.wait_ge(part3_ready.sem, part3_ready.at((L, p, b)))
                    sp.wait_ge(part2_ready.sem, part2_ready.at((L, p, b)))
                    if before(fronts, (L, p)):
                        sp.wait_ge(stack_loaded[b].sem, stack_loaded[b].at(before(fronts, (L, p)) + (PARTS,)))
                    parts_of = [qk_parts[:, :, n, b * SEQ:(b + 1) * SEQ] for n in range(2)]
                    sp.dma_start(k_dram[b].rearrange("j p t -> p j t"), parts_of[1]).then_inc(parts_stored[b].sem, 16)
                    for j in range(PARTS):
                        sp.dma_start(q_dram[b, :, j].rearrange("i p t -> p i t"), parts_of[0]).then_inc(parts_stored[b].sem, 16)

                def load_qk(L, p, b):
                    q_stack, k_stack = (stack(L, p)[:, n] for n in range(2))
                    sp.wait_ge(parts_stored[b].sem, parts_stored[b].at((L, p, PARTS)))
                    if b == 0 and last_reader_of_stack(L, p):
                        sp.wait_ge(score_slot_filled.sem, score_slot_filled.at(("S",) + last_reader_of_stack(L, p)))
                    for i in range(PARTS):
                        sp.dma_start(
                            k_stack[i * PARTS * DH:(i + 1) * PARTS * DH, b].rearrange("r h t -> r (h t)"),
                            k_dram[b].rearrange("j (d h) t -> (j d) (h t)", d=DH)).then_inc(stack_loaded[b].sem, 16)
                    sp.dma_start(
                        q_stack[:, b].rearrange("r h t -> r (h t)"),
                        q_dram[b].rearrange("i j (d h) t -> (i j d) (h t)", d=DH)).then_inc(stack_loaded[b].sem, 16)

                def store_positions(p, n):
                    c, b, half = n // 4, n // 2 % 2, n % 2
                    sp.wait_ge(pos_part3_ready.sem, pos_part3_ready.at((p, n)))
                    sp.wait_ge(pos_part2_ready.sem, pos_part2_ready.at((p, n)))
                    if p and n == 0:
                        sp.wait_ge(pos_stack_loaded["c"].sem, pos_stack_loaded["c"].at((p - 1, NB - 1)))
                        sp.wait_ge(pos_stack_loaded["p"].sem, pos_stack_loaded["p"].at((p - 1, NB - 1)))
                    sp.dma_start(att_dram[c, b].rearrange("s p t -> p s t")[:, :, half * 2 * SEQ:(half + 1) * 2 * SEQ],
                                 att_parts[:, n % 2].rearrange("p s g t -> p s (g t)")).then_inc(
                                     pos_parts_stored[n % 2].sem, 16)

                def load_positions(p):
                    if p:
                        sp.wait_ge(score_slot_filled.sem, score_slot_filled.at(("D", p - 1, 1, "p", DJ - 1)))
                    for c in "cp":
                        for b in range(NB):
                            n = 4 * "cp".index(c) + 2 * b
                            for half in range(2):
                                sp.wait_ge(pos_parts_stored[half].sem, pos_parts_stored[half].at((p, n + half)))
                            sp.dma_start(att[c][:, b].rearrange("r h t -> r (h t)"),
                                         att_dram["cp".index(c), b].rearrange("s (i a) t -> (s i) (a t)", a=4)).then_inc(
                                             pos_stack_loaded[c].sem, 16)

                for kind, *key in plan:
                    if kind == "att_late":
                        store_positions(*key)
                    elif kind == "split2":
                        for b in range(NB):
                            store_qk(*key, b)
                        if key[0] == "b":
                            load_positions(key[1])
                    elif kind == "load_qk":
                        for b in range(NB):
                            load_qk(*key, b)
                    elif kind == "store":
                        (p,) = key
                        sp.wait_ge(ffn_added.sem, ffn_added.at(("g", p)))
                        sp.dma_start(out_rows[p * NT:(p + 1) * NT].rearrange("t p d -> p t d"), x[:, p]).then_inc(out_stored.sem, 16)
                sp.wait_ge(out_stored.sem, out_stored.at((PAIRS - 1,)))

            @block.tensor
            def _(pe):
                def turn_xn(s, p):
                    src = ffn_xn if s in "fg" else xn[:, p % 2]
                    pe.wait_ge(normed.sem, normed.at((s, p, NT - 1)))
                    take_m(pe, ("xt", s, p))
                    for k in range(NT):
                        ins = nc.tensor.transpose(ps_m[:, k * P:(k + 1) * P], src[:, k, :], ident)
                    ins.then_inc(small_bank_filled.sem, 1)

                def project(which, L, p):
                    pe.wait_ge(xnT_ready.sem, xnT_ready.at((L, p)))
                    take_m(pe, (which, L, p))
                    w = wq[L] if which == "q" else wk[L]
                    nc.tensor.matmul(ps_m[:], w[:], xnT[:], start=True, stop=True).then_inc(small_bank_filled.sem, 1)

                def project_v(L, p):
                    take_m(pe, ("v", L, p))
                    for k in range(NT):
                        ins = nc.tensor.matmul(ps_m[:, k * P:(k + 1) * P], xnT[:, k * P:(k + 1) * P],
                                               wv[L][:], start=True, stop=True)
                    ins.then_inc(small_bank_filled.sem, 1)

                def position_terms(p, n):
                    c, b, half = n // 4, n // 2 % 2, n % 2
                    pe.wait_ge(plain_ready.sem, plain_ready.at((p, c)))
                    take_m(pe, ("att", p, n))
                    for g in range(2):
                        ins = nc.tensor.matmul(ps_m[:, g * SEQ:(g + 1) * SEQ],
                                               pos_w["cp"[c]][:, 2 * half + g].rearrange("p i h -> p (i h)"),
                                               plain[:, c, b * SEQ:(b + 1) * SEQ], start=True, stop=True)
                    ins.then_inc(small_bank_filled.sem, 1)

                def spread_positions(p, qt, c, j):
                    if j == 0:
                        pe.wait_ge(pos_stack_loaded[c].sem, pos_stack_loaded[c].at((p, NB - 1)))
                    slot = take_s(pe, ("D", p, qt, c, j)).rearrange("p a (n b) -> p (a n) b", b=BH)
                    for u in range(P // 4):
                        if c == "c":
                            fixed = qt * P + (j % 4) * 32 + u
                            start = SEQ - 1 - fixed + j // 4 * P
                            table = oh_c
                        else:
                            fixed = j * 32 + u
                            start = SEQ - 1 - fixed + qt * P
                            table = oh_p
                        ins = nc.tensor.matmul(
                            slot[:, u, :], table[0:PARTS * NIDX, start:start + P],
                            att[c][:, :, :, fixed:fixed + 1].rearrange("r b h u -> r (b h u)"),
                            start=True, stop=True)
                    ins.then_inc(score_slot_filled.sem, 1)

                def scores(L, p, i):
                    _, _, b, qt = group(NUMBER[L, p, i] // HC)
                    q_stack, k_stack = (stack(L, p)[:, n] for n in range(2))
                    if i % HC == 0:
                        pe.wait_ge(stack_loaded[b].sem, stack_loaded[b].at((L, p, PARTS)))
                    if L == "b" and i % (NCH // 2) == 0:
                        pe.wait_ge(spread_by_act.sem, spread_by_act.at((p, qt, "c", DJ - 1)))
                        pe.wait_ge(spread_by_dve.sem, spread_by_dve.at((p, qt, "c", DJ - 2)))
                    slot = take_s(pe, ("S", L, p, i)).rearrange("p a (g t) -> p (a g) t", g=2)
                    for k in range(HC):
                        h = (i % HC) * HC + k
                        if L == "b":
                            for kt in range(2):
                                nc.tensor.matmul(slot[:, k, kt * P:(kt + 1) * P], c2p[:, kt, b * NH + h, :], ident,
                                                 start=(k % 2 == 0 and kt == 0), stop=False, is_transpose=True,
                                                 skip_group_check=True)
                        ins = nc.tensor.matmul(slot[:, k, :], q_stack[:, b, h, qt * P:(qt + 1) * P],
                                               k_stack[:, b, h, :], start=(L == "a"), stop=True,
                                               skip_group_check=True)
                    ins.then_inc(score_slot_filled.sem, 1)

                def turn_probs(L, p, i):
                    g = NUMBER[L, p, i]
                    pe.wait_ge(probs_ready.sem, probs_ready.at((L, p, i)))
                    for hh in range(2):
                        if g:
                            key = (CHUNKS[g - 1], hh)
                            moved = moved_by[t_engine(*key)]
                            pe.wait_ge(moved.sem, moved.at(key))
                        for k in range(2):
                            for kt in range(2):
                                ins = nc.tensor.transpose(
                                    ps_t[hh][:, (2 * k + kt) * P:(2 * k + kt + 1) * P],
                                    prob[:, g % 2, 2 * hh + k, kt * P:(kt + 1) * P], ident)
                        ins.then_inc(probs_turned.sem, 1)

                def weigh_values(L, p, i):
                    g = NUMBER[L, p, i]
                    b = group(g // HC)[2]
                    if i == 0:
                        pe.wait_ge(v_ready.sem, v_ready.at((L, p)))
                    if i % HC == 0 and g:
                        pe.wait_ge(out_moved.sem, out_moved.at(g // HC - 1))
                    for hh in range(2):
                        key = ((L, p, i), hh)
                        moved = moved_by[t_engine(*key)]
                        pe.wait_ge(moved.sem, moved.at(key))
                    c = i % HC
                    for kt in range(2):
                        for k in range(HC):
                            ins = nc.tensor.matmul(ps_o[VC * k:VC * (k + 1), c * P:(c + 1) * P],
                                                   v[:, 2 * b + kt, c * HC + k, :], probT[:, g % 2, k, kt, :],
                                                   start=(kt == 0), stop=(kt == 1), skip_group_check=True)
                    ins.then_inc(values_weighed.sem, 1)

                def turn_back(n):
                    pe.wait_ge(out_moved.sem, out_moved.at(n))
                    take_m(pe, ("OB", n))
                    for c in range(HC):
                        ins = nc.tensor.transpose(ps_m[:, c * P:(c + 1) * P], o_turned[:, c, :], ident)
                    ins.then_inc(small_bank_filled.sem, 1)

                def turn_out(n):
                    pe.wait_ge(heads_out_ready.sem, heads_out_ready.at(n))
                    take_m(pe, ("OT", n))
                    nc.tensor.transpose(ps_m[:, 0:P], o_sb[:].rearrange("p h d -> p (h d)"),
                                        ident).then_inc(small_bank_filled.sem, 1)

                def project_out(n):
                    pe.wait_ge(outT_ready.sem, outT_ready.at(n))
                    take_m(pe, ("OP", n))
                    nc.tensor.matmul(ps_m[:, 0:P], oT[:], wo[group(n)[0]][:], start=True, stop=True).then_inc(small_bank_filled.sem, 1)

                def hidden(s, p, j):
                    pe.wait_ge(xnT_ready.sem, xnT_ready.at((s, p)))
                    take_m(pe, ("h", s, p, j))
                    nc.tensor.matmul(ps_m[:], wd1[:, 4 * j:4 * j + 4, :].rearrange("p e h -> p (e h)"),
                                     xnT[:], start=True, stop=True).then_inc(small_bank_filled.sem, 1)

                def reconstruct(s, p, e):
                    pe.wait_ge(hidden_ready.sem, hidden_ready.at((s, p, e // 4)))
                    take_m(pe, ("rec", s, p, e))
                    nc.tensor.matmul(ps_m[:], wd2[:, e, :], hT[:, e // 4, :],
                                     start=True, stop=True).then_inc(small_bank_filled.sem, 1)

                def sum_losses(s, p):
                    pe.wait_ge(losses_ready.sem, losses_ready.at((s, p, NE - 1)))
                    take_m(pe, ("loss", s, p))
                    nc.tensor.matmul(ps_m[:, 0:NB * NE], ones[:], loss_p[:].rearrange("p b e -> p (b e)"),
                                     start=True, stop=True).then_inc(small_bank_filled.sem, 1)

                def adapter_down(s, p):
                    take_m(pe, ("act", s, p))
                    for b in range(NB):
                        pe.wait_ge(expert_added.sem, expert_added.at((s, p, b, NE - 1)))
                        ins = nc.tensor.matmul(ps_m[0:R, b * SEQ:(b + 1) * SEQ], w_sel[:, b, 0:R],
                                               xnT[:, b * SEQ:(b + 1) * SEQ], start=True, stop=True)
                    ins.then_inc(small_bank_filled.sem, 1)

                def ffn_out(s, p):
                    take_m(pe, ("ffo", s, p))
                    pe.wait_ge(adapter_hidden_ready.sem, adapter_hidden_ready.at((s, p, NB - 1)))
                    for k in range(NT):
                        nc.tensor.matmul(ps_m[:, k * P:(k + 1) * P], xnT[:, k * P:(k + 1) * P], w_base[:],
                                         start=True, stop=False)
                        ins = nc.tensor.matmul(ps_m[:, k * P:(k + 1) * P], aT[:, k * P:(k + 1) * P],
                                               w_sel[0:R + 1, k // 2, R:R + D], start=False, stop=True)
                    ins.then_inc(small_bank_filled.sem, 1)

                do = {"S": scores, "T": turn_probs, "PV": weigh_values, "D": spread_positions, "OB": turn_back,
                      "OT": turn_out, "OP": project_out, "xt": turn_xn, "v": project_v, "h": hidden,
                      "rec": reconstruct, "loss": sum_losses, "act": adapter_down, "ffo": ffn_out}
                for kind, *key in plan:
                    if kind in ("q", "k"):
                        project(kind, *key)
                    elif kind == "att":
                        if key[1] < POS:
                            position_terms(*key)
                    elif kind in do:
                        do[kind](*key)

            @block.scalar
            def _(act):
                def copy_xt(s, p):
                    act.wait_ge(small_bank_filled.sem, small_bank_filled.at(("xt", s, p)))
                    last = before(turns, (s, p))
                    if last:
                        job = ("v",) + last if last[0] in "ab" else ("ffo",) + last
                        act.wait_ge(small_bank_filled.sem, small_bank_filled.at(job))
                    nc.scalar.copy(xnT[:], ps_m[:]).then_inc(xnT_ready.sem, 1)

                def copy_qk(which, L, p):
                    n = "qk".index(which)
                    act.wait_ge(small_bank_filled.sem, small_bank_filled.at((which, L, p)))
                    last = before(fronts, (L, p))
                    if L == "a":
                        if last:
                            act.wait_ge(rest_ready.sem, rest_ready.at(last + (NB - 1,)))
                        if last_ffn_before[L, p]:
                            act.wait_ge(small_bank_filled.sem, small_bank_filled.at(("rec",) + last_ffn_before[L, p] + (NE - 1,)))
                        nc.scalar.activation(qk[:, n, :], ps_m[:], ACT.Identity,
                                             bias=(bq, bk)[n]["a"][:]).then_inc(qk_ready_a.sem, 1)
                    else:
                        if n == 0:
                            act.wait_ge(v_ready.sem, v_ready.at(last))
                        elif last_ffn_before[L, p]:
                            act.wait_ge(small_bank_filled.sem, small_bank_filled.at(("xt",) + last_ffn_before[L, p]))
                        nc.scalar.activation(plain[:, n, :], ps_m[:], ACT.Identity,
                                             bias=(bq, bk)[n]["b"][:]).then_inc(plain_ready.sem, 1)

                def split1(L, p):
                    for b in range(NB):
                        cols = slice(b * SEQ, (b + 1) * SEQ)
                        ready = qk_ready_a if L == "a" else qk_ready_b
                        act.wait_ge(ready.sem, ready.at((p, 1)))
                        if before(fronts, (L, p)):
                            act.wait_ge(parts_stored[b].sem, parts_stored[b].at(before(fronts, (L, p)) + (PARTS,)))
                        if L == "b" and b == 0:
                            for m in range(2):
                                act.wait_ge(pos_parts_stored[m].sem, pos_parts_stored[m].at((p, POS - 2 + m)))
                        nc.scalar.copy(qk_parts[:, 0, :, cols], qk[:, :, cols]).then_inc(part1_ready.sem, 1)

                def split2(L, p):
                    for b in range(NB):
                        cols = slice(b * SEQ, (b + 1) * SEQ)
                        act.wait_ge(rest_ready.sem, rest_ready.at((L, p, b)))
                        nc.scalar.copy(qk_parts[:, 1, :, cols], rest[:, :, cols]).then_inc(part2_ready.sem, 1)

                def position_part1(p, n):
                    act.wait_ge(small_bank_filled.sem, small_bank_filled.at(("att", p, n)))
                    if n >= 2:
                        act.wait_ge(pos_parts_stored[n % 2].sem, pos_parts_stored[n % 2].at((p, n - 2)))
                    elif n == 0:
                        for b in range(NB):
                            act.wait_ge(parts_stored[b].sem, parts_stored[b].at(before(fronts, ("b", p)) + (PARTS,)))
                    nc.scalar.copy(att_parts[:, n % 2, 0], ps_m[:].rearrange("p (g t) -> p g t", g=2)).then_inc(pos_part1_ready.sem, 1)

                def position_part2(p, n):
                    act.wait_ge(pos_rest_ready.sem, pos_rest_ready.at((p, n)))
                    nc.scalar.copy(att_parts[:, n % 2, 1], pos_rest[:, n % 2]).then_inc(pos_part2_ready.sem, 1)

                def spread_out(p, qt, c, j):
                    if j % 2 == 1:
                        earlier = chunk_before_half[p, qt]
                        act.wait_ge(score_slot_filled.sem, score_slot_filled.at(("S",) + earlier))
                        if earlier[0] == "b":
                            act.wait_ge(scores_summed.sem, scores_summed.at(earlier))
                        act.wait_ge(score_slot_filled.sem, score_slot_filled.at(("D", p, qt, c, j)))
                        nc.scalar.copy(*spread_views((p, qt, c, j))).then_inc(spread_by_act.sem, 1)

                def exps(L, p, i):
                    g = NUMBER[L, p, i]
                    n = g // HC
                    scale = SCALE_A if L == "a" else SCALE_B
                    src = slot_s(("S", L, p, i)).rearrange("p a (g t) -> p (a g) t", g=2)
                    act.wait_ge(exp_bias_ready.sem, exp_bias_ready.at((L, p, i)))
                    if L == "b":
                        src = prob[:, g % 2]
                    elif g >= 2:
                        act.wait_ge(probs_turned.sem, probs_turned.at(CHUNKS[g - 2] + (1,)))
                    if i % HC == 0 and n >= 2:
                        act.wait_ge(inverse_ready.sem, inverse_ready.at(n - 2))
                    for k in range(HC):
                        h = (i % HC) * HC + k
                        ins = nc.scalar.activation(prob[:, g % 2, k, :], src[:, k, :], ACT.Exp,
                                                   bias=nbias[:, g % 2, k:k + 1], scale=scale,
                                                   accum_out=rsum[:, n % 2, h:h + 1])
                    ins.then_inc(probs_ready.sem, 1)

                def move_probs(L, p, i):
                    g = NUMBER[L, p, i]
                    for hh in range(2):
                        if t_engine((L, p, i), hh) == "act":
                            act.wait_ge(probs_turned.sem, probs_turned.at((L, p, i, hh)))
                            if g >= 2:
                                act.wait_ge(values_weighed.sem, values_weighed.at(CHUNKS[g - 2]))
                            nc.scalar.copy(probT[:, g % 2, 2 * hh:2 * hh + 2],
                                           ps_t[hh][:].rearrange("p (a b c) -> p a b c", a=2, b=2)).then_inc(moved_by["act"].sem, 1)

                def move_out(n):
                    act.wait_ge(values_weighed.sem, values_weighed.at(last_chunk_of_group(n)))
                    if n:
                        act.wait_ge(small_bank_filled.sem, small_bank_filled.at(("OB", n - 1)))
                    nc.scalar.copy(o_turned[:].rearrange("p c t -> p (c t)"), ps_o[:]).then_inc(out_moved.sem, 1)

                def copy_out(n):
                    act.wait_ge(small_bank_filled.sem, small_bank_filled.at(("OT", n)))
                    if n:
                        act.wait_ge(small_bank_filled.sem, small_bank_filled.at(("OP", n - 1)))
                    nc.scalar.copy(oT[:], ps_m[:, 0:P]).then_inc(outT_ready.sem, 1)

                def hidden(s, p, j):
                    if j == 0:
                        act.wait_ge(rest_ready.sem, rest_ready.at(last_front_before[s, p] + (NB - 1,)))
                        if last_ffn_before[s, p]:
                            act.wait_ge(small_bank_filled.sem, small_bank_filled.at(("rec",) + last_ffn_before[s, p] + (NE - 1,)))
                    act.wait_ge(small_bank_filled.sem, small_bank_filled.at(("h", s, p, j)))
                    nc.scalar.activation(hT[:, j, :], ps_m[:], ACT.Relu, bias=bd1[:, j:j + 1]).then_inc(hidden_ready.sem, 1)

                def square(s, p, e):
                    act.wait_ge(diff_ready.sem, diff_ready.at((s, p, e)))
                    for b in range(NB):
                        d = diff[:, e % 2, b * SEQ:(b + 1) * SEQ]
                        ins = nc.scalar.activation(d, d, ACT.Square, bias=bd2[:, e:e + 1],
                                                   accum_out=loss_p[:, b, e:e + 1])
                    ins.then_inc(losses_ready.sem, 1)

                def adapter_hidden(s, p):
                    act.wait_ge(small_bank_filled.sem, small_bank_filled.at(("act", s, p)))
                    for b in range(NB):
                        cols = slice(b * SEQ, (b + 1) * SEQ)
                        nc.scalar.activation(aT[0:R, cols], ps_m[0:R, cols], ACT.Relu,
                                             bias=w_sel[0:R, b, R + D:SELW]).then_inc(adapter_hidden_ready.sem, 1)

                do = {"S": exps, "T": move_probs, "OM": move_out, "OT": copy_out, "D": spread_out, "xt": copy_xt,
                      "split1": split1, "split2": split2, "att_late": position_part2, "h": hidden,
                      "square": square, "act": adapter_hidden}
                for kind, *key in plan:
                    if kind in ("q", "k"):
                        copy_qk(kind, *key)
                    elif kind == "att":
                        if key[1] < POS:
                            position_part1(*key)
                    elif kind in do:
                        do[kind](*key)

            @block.vector
            def _(dve):
                def norm1(s, p):
                    src = xn[:, p % 2] if s == "n" else x[:, p]
                    if s in "fn":
                        dve.wait_ge(residual_added.sem, residual_added.at(NUMBER["a" if s == "f" else "b", p, NCH - 1] // HC))
                    elif s == "b":
                        dve.wait_ge(ffn_added.sem, ffn_added.at(("f", p)))
                    elif s == "g":
                        dve.wait_ge(inner_norm_step.sem, inner_norm_step.at((p, 1)))
                    last = before(norms, (s, p))
                    if last:
                        dve.wait_ge(normed.sem, normed.at(last + (NT - 1,)))
                    for k in range(NT):
                        nc.vector.bn_stats(stats[:, k, :], src[:, k, :]).then_inc(stats_done.sem, 1)
                    for k in range(NT):
                        dve.wait_ge(stats_done.sem, stats_done.at((s, p, k)))
                        nc.vector.bn_aggr(mv[:, k, :], stats[:, k, :]).then_inc(stats_done.sem, 1)
                    dve.wait_ge(stats_done.sem, stats_done.at((s, p, 2 * NT - 1)))
                    nc.vector.tensor_scalar(ve[:], mv[:, :, 1], EPS_B if s == "n" else EPS_LN, None,
                                            ALU.add).then_inc(variance_done.sem, 1)

                def norm2(s, p):
                    src = xn[:, p % 2] if s == "n" else x[:, p]
                    dst = ffn_xn if s in "fg" else xn[:, p % 2]
                    dve.wait_ge(root_done.sem, root_done.at((s, p)))
                    if s == "a" and p >= 2:
                        dve.wait_ge(small_bank_filled.sem, small_bank_filled.at(("xt", "a", p - 2)))
                    elif s == "b" and p >= 2:
                        dve.wait_ge(inner_norm_step.sem, inner_norm_step.at((p - 2, 1)))
                    elif s == "b":
                        dve.wait_ge(small_bank_filled.sem, small_bank_filled.at(
                            ("xt", "a", PAIRS - 2 + (PAIRS + p) % 2)))
                    elif s in "fg":
                        if last_front_before[s, p][0] == "b":
                            dve.wait_ge(small_bank_filled.sem, small_bank_filled.at(("att", last_front_before[s, p][1], POS - 1)))
                            dve.wait_ge(qk_ready_b.sem, qk_ready_b.at((last_front_before[s, p][1], 1)))
                        if last_ffn_before[s, p]:
                            dve.wait_ge(small_bank_filled.sem, small_bank_filled.at(("xt",) + last_ffn_before[s, p]))
                    for k in range(NT):
                        nc.vector.tensor_scalar(dst[:, k, :], src[:, k, :], mv[:, k, 0:1], rstd[:, k:k + 1],
                                                ALU.subtract, ALU.mult).then_inc(normed.sem, 1)

                def inner(p):
                    y = xn[:, p % 2]
                    dve.wait_ge(normed.sem, normed.at(("n", p, NT - 1)))
                    nc.vector.tensor_tensor(
                        y, y, ln_s[:].rearrange("p (u n) -> p u n", u=1).to_broadcast([P, NT, D]), ALU.mult).then_inc(inner_norm_step.sem, 1)
                    dve.wait_ge(inner_norm_step.sem, inner_norm_step.at((p, 0)))
                    dve.wait_ge(bias_added.sem, bias_added.at(("n", p)))
                    nc.vector.tensor_tensor(x[:, p], x[:, p], y, ALU.add).then_inc(inner_norm_step.sem, 1)

                def take_v(L, p):
                    dve.wait_ge(small_bank_filled.sem, small_bank_filled.at(("v", L, p)))
                    last = before(fronts, (L, p))
                    if last:
                        dve.wait_ge(v_ready.sem, v_ready.at(last))
                    if L == "b":
                        dve.wait_ge(small_bank_filled.sem, small_bank_filled.at(("att", p, POS // 2 - 1)))
                        dve.wait_ge(qk_ready_b.sem, qk_ready_b.at((p, 0)))
                    nc.vector.tensor_tensor(
                        new_v, ps_m[:].rearrange("p (t h d) -> p t h d", t=NT, h=NH),
                        bv[L][:].rearrange("p (u h d) -> p u h d", u=1, h=NH).to_broadcast([P, NT, NH, DH]),
                        ALU.add).then_inc(new_v_ready.sem, 1)

                def position_rest(p, n):
                    dve.wait_ge(pos_part1_ready.sem, pos_part1_ready.at((p, n)))
                    if n >= 2:
                        dve.wait_ge(pos_part3_ready.sem, pos_part3_ready.at((p, n - 2)))
                        dve.wait_ge(pos_part2_ready.sem, pos_part2_ready.at((p, n - 2)))
                    elif n == 0:
                        last = before(fronts, ("b", p))
                        dve.wait_ge(part3_ready.sem, part3_ready.at(last + (NB - 1,)))
                        dve.wait_ge(part2_ready.sem, part2_ready.at(last + (NB - 1,)))
                        if last_ffn_before["b", p]:
                            dve.wait_ge(losses_ready.sem, losses_ready.at(last_ffn_before["b", p] + (NE - 1,)))
                    nc.vector.tensor_tensor(pos_rest[:, n % 2], ps_m[:].rearrange("p (g t) -> p g t", g=2),
                                            att_parts[:, n % 2, 0], ALU.subtract).then_inc(pos_rest_ready.sem, 1)

                def spread_out(p, qt, c, j):
                    if j % 2 == 0:
                        earlier = chunk_before_half[p, qt]
                        dve.wait_ge(score_slot_filled.sem, score_slot_filled.at(("S",) + earlier))
                        if earlier[0] == "b":
                            dve.wait_ge(scores_summed.sem, scores_summed.at(earlier))
                        dve.wait_ge(score_slot_filled.sem, score_slot_filled.at(("D", p, qt, c, j)))
                        nc.vector.tensor_copy(*spread_views((p, qt, c, j))).then_inc(spread_by_dve.sem, 1)

                def maxima(L, p, i):
                    g = NUMBER[L, p, i]
                    _, _, b, qt = group(g // HC)
                    slot = slot_s(("S", L, p, i)).rearrange("p a (g t) -> p (a g) t", g=2)
                    dve.wait_ge(score_slot_filled.sem, score_slot_filled.at(("S", L, p, i)))
                    if L == "a":
                        nc.vector.tensor_reduce(nmax[:, g % 2, :], slot, AX.X, ALU.max).then_inc(max_ready.sem, 1)
                        dve.wait_ge(max_ready.sem, max_ready.at((L, p, i)))
                    else:
                        if i % (NCH // 2) == 0:
                            dve.wait_ge(spread_by_act.sem, spread_by_act.at((p, qt, "p", DJ - 1)))
                            dve.wait_ge(spread_by_dve.sem, spread_by_dve.at((p, qt, "p", DJ - 2)))
                        dve.wait_ge(probs_turned.sem, probs_turned.at(CHUNKS[g - 2] + (1,)))
                        for k in range(HC):
                            h = (i % HC) * HC + k
                            ins = nc.vector.tensor_tensor_reduce(
                                out=prob[:, g % 2, k, :], in0=slot[:, k, :], in1=p2c[:, b * NH + h, :],
                                scale=1.0, scalar=-3.4e38, op0=ALU.add, op1=ALU.max,
                                accum_out=nmax[:, g % 2, k:k + 1])
                        ins.then_inc(scores_summed.sem, 1)
                        dve.wait_ge(scores_summed.sem, scores_summed.at((L, p, i)))
                    scale = SCALE_A if L == "a" else SCALE_B
                    nc.vector.tensor_scalar(nbias[:, g % 2, :], nmax[:, g % 2, :], -scale, None, ALU.mult).then_inc(exp_bias_ready.sem, 1)

                def move_probs(L, p, i):
                    g = NUMBER[L, p, i]
                    for hh in range(2):
                        if t_engine((L, p, i), hh) == "dve":
                            dve.wait_ge(probs_turned.sem, probs_turned.at((L, p, i, hh)))
                            if g >= 2:
                                dve.wait_ge(values_weighed.sem, values_weighed.at(CHUNKS[g - 2]))
                            nc.vector.tensor_copy(probT[:, g % 2, 2 * hh:2 * hh + 2],
                                                  ps_t[hh][:].rearrange("p (a b c) -> p a b c", a=2, b=2)).then_inc(moved_by["dve"].sem, 1)

                def normalize(n):
                    dve.wait_ge(probs_ready.sem, probs_ready.at(last_chunk_of_group(n)))
                    nc.vector.reciprocal(rinv[:, n % 2, :], rsum[:, n % 2, :]).then_inc(inverse_ready.sem, 1)
                    dve.wait_ge(small_bank_filled.sem, small_bank_filled.at(("OB", n)))
                    dve.wait_ge(inverse_ready.sem, inverse_ready.at(n))
                    if n:
                        dve.wait_ge(small_bank_filled.sem, small_bank_filled.at(("OT", n - 1)))
                    nc.vector.tensor_tensor(
                        o_sb[:], ps_m[:].rearrange("p (h e) -> p h e", e=VC)[:, :, 0:DH],
                        rinv[:, n % 2, :].rearrange("p (h u) -> p h u", u=1).to_broadcast([P, NH, DH]),
                        ALU.mult).then_inc(heads_out_ready.sem, 1)

                def add_out(n):
                    L, p, b, qt = group(n)
                    dst = (x[:, p] if L == "a" else xn[:, p % 2])[:, 2 * b + qt, :]
                    dve.wait_ge(bias_added.sem, bias_added.at((L, p)))
                    dve.wait_ge(small_bank_filled.sem, small_bank_filled.at(("OP", n)))
                    nc.vector.tensor_tensor(dst, ps_m[:, 0:P], dst, ALU.add).then_inc(residual_added.sem, 1)

                def difference(s, p, e):
                    dve.wait_ge(small_bank_filled.sem, small_bank_filled.at(("rec", s, p, e)))
                    if e >= 2:
                        dve.wait_ge(losses_ready.sem, losses_ready.at((s, p, e - 2)))
                    elif e == 0:
                        dve.wait_ge(xnT_ready.sem, xnT_ready.at((s, p)))
                        dve.wait_ge(part3_ready.sem, part3_ready.at(last_front_before[s, p] + (NB - 1,)))
                        dve.wait_ge(part2_ready.sem, part2_ready.at(last_front_before[s, p] + (NB - 1,)))
                        if last_ffn_before[s, p]:
                            dve.wait_ge(losses_ready.sem, losses_ready.at(last_ffn_before[s, p] + (NE - 1,)))
                    nc.vector.tensor_tensor(diff[:, e % 2], ps_m[:], xnT[:], ALU.subtract).then_inc(diff_ready.sem, 1)

                def choose(s, p):
                    loss = ps_m[:, 0:NB * NE].rearrange("p (b e) -> p b e", b=NB)
                    numbers = iota.rearrange("p (u e) -> p u e", u=1).to_broadcast([P, NB, NE])

                    def wide(a):
                        return a[:].rearrange("p (b u) -> p b u", u=1).to_broadcast([P, NB, NE])

                    dve.wait_ge(small_bank_filled.sem, small_bank_filled.at(("loss", s, p)))
                    nc.vector.tensor_reduce(lmin[:], loss, AX.X, ALU.min).then_inc(choice_step.sem, 1)
                    dve.wait_ge(choice_step.sem, choice_step.at((s, p, 0)))
                    nc.vector.tensor_tensor(lkey[:], loss, wide(lmin), ALU.is_gt).then_inc(choice_step.sem, 1)
                    dve.wait_ge(choice_step.sem, choice_step.at((s, p, 1)))
                    nc.vector.scalar_tensor_tensor(out=lkey[:], in0=lkey[:], scalar=float(NE), in1=numbers,
                                                   op0=ALU.mult, op1=ALU.add).then_inc(choice_step.sem, 1)
                    dve.wait_ge(choice_step.sem, choice_step.at((s, p, 2)))
                    nc.vector.tensor_reduce(kmin[:], lkey[:], AX.X, ALU.min).then_inc(choice_step.sem, 1)
                    dve.wait_ge(choice_step.sem, choice_step.at((s, p, 3)))
                    nc.vector.tensor_tensor(onehot[:], numbers, wide(kmin), ALU.is_equal).then_inc(choice_step.sem, 1)

                def pick(s, p, n):
                    dve.wait_ge(choice_step.sem, choice_step.at((s, p, 4)))
                    if n == 0 and last_ffn_before[s, p]:
                        dve.wait_ge(small_bank_filled.sem, small_bank_filled.at(("ffo",) + last_ffn_before[s, p]))
                        dve.wait_ge(adapter_hidden_ready.sem, adapter_hidden_ready.at(last_ffn_before[s, p] + (NB - 1,)))
                    for e in (2 * n, 2 * n + 1):
                        for b in range(NB):
                            if e == 0:
                                nc.vector.tensor_scalar(w_sel[:, b, :], w_all[:, e, :], onehot[:, b, e:e + 1], None,
                                                        ALU.mult).then_inc(expert_added.sem, 1)
                            else:
                                dve.wait_ge(expert_added.sem, expert_added.at((s, p, b, e - 1)))
                                nc.vector.scalar_tensor_tensor(
                                    out=w_sel[:, b, :], in0=w_all[:, e, :], scalar=onehot[:, b, e:e + 1],
                                    in1=w_sel[:, b, :], op0=ALU.mult, op1=ALU.add).then_inc(expert_added.sem, 1)

                def add_ffn(s, p):
                    dve.wait_ge(small_bank_filled.sem, small_bank_filled.at(("ffo", s, p)))
                    nc.vector.tensor_tensor(
                        x[:, p], x[:, p], ps_m[:].rearrange("p (t n) -> p t n", t=NT), ALU.add).then_inc(ffn_added.sem, 1)

                do = {"S": maxima, "T": move_probs, "D": spread_out, "OB": normalize, "OP": add_out,
                      "norm1": norm1, "norm2": norm2, "inner": inner, "v": take_v, "rec": difference,
                      "loss": choose, "pick": pick, "ffo": add_ffn}
                for kind, *key in plan:
                    if kind == "att":
                        if key[1] < POS:
                            position_rest(*key)
                    elif kind in do:
                        do[kind](*key)

            @block.gpsimd
            def _(pool):
                def root(s, p):
                    if s == "n":
                        pool.wait_ge(normed.sem, normed.at(("b", p, NT - 1)))
                        nc.gpsimd.tensor_tensor(
                            x[:, p], x[:, p], ln_b[:].rearrange("p (u n) -> p u n", u=1).to_broadcast([P, NT, D]),
                            ALU.add).then_inc(bias_added.sem, 1)
                    pool.wait_ge(variance_done.sem, variance_done.at((s, p)))
                    nc.gpsimd.tensor_tensor(rstd[:], ve[:], neg_half[:], ALU.pow).then_inc(root_done.sem, 1)

                def add_bias(s, p):
                    if s in "ab":
                        pool.wait_ge(normed.sem, normed.at((s, p, NT - 1)))
                        pool.wait_ge(small_bank_filled.sem, small_bank_filled.at(("xt", s, p)))
                        dst = x[:, p] if s == "a" else xn[:, p % 2]
                        nc.gpsimd.tensor_tensor(
                            dst, dst, bo[s][:].rearrange("p (u n) -> p u n", u=1).to_broadcast([P, NT, D]),
                            ALU.add).then_inc(bias_added.sem, 1)

                def add_centre(which, L, p):
                    if L == "b":
                        n = "qk".index(which)
                        pool.wait_ge(plain_ready.sem, plain_ready.at((p, n)))
                        pool.wait_ge(part1_ready.sem, part1_ready.at(before(fronts, (L, p)) + (NB - 1,)))
                        pool.wait_ge(rest_ready.sem, rest_ready.at(before(fronts, (L, p)) + (NB - 1,)))
                        if last_ffn_before[L, p]:
                            pool.wait_ge(small_bank_filled.sem, small_bank_filled.at(("rec",) + last_ffn_before[L, p] + (NE - 1,)))
                        nc.gpsimd.tensor_scalar(qk[:, n, :], plain[:, n, :], centre[:, n:n + 1], None,
                                                ALU.add).then_inc(qk_ready_b.sem, 1)

                def take_rests(L, p):
                    for b in range(NB):
                        cols = slice(b * SEQ, (b + 1) * SEQ)
                        pool.wait_ge(part1_ready.sem, part1_ready.at((L, p, b)))
                        if b == 0:
                            if before(fronts, (L, p)):
                                pool.wait_ge(part2_ready.sem, part2_ready.at(before(fronts, (L, p)) + (NB - 1,)))
                                pool.wait_ge(part3_ready.sem, part3_ready.at(before(fronts, (L, p)) + (NB - 1,)))
                            if last_ffn_before[L, p]:
                                pool.wait_ge(losses_ready.sem, losses_ready.at(last_ffn_before[L, p] + (NE - 1,)))
                            if L == "b":
                                pool.wait_ge(pos_part2_ready.sem, pos_part2_ready.at((p, POS - 1)))
                                pool.wait_ge(pos_part3_ready.sem, pos_part3_ready.at((p, POS - 1)))
                        nc.gpsimd.tensor_tensor(rest[:, :, cols], qk[:, :, cols], qk_parts[:, 0, :, cols],
                                                ALU.subtract).then_inc(rest_ready.sem, 1)

                def take_part3(L, p):
                    for b in range(NB):
                        cols = slice(b * SEQ, (b + 1) * SEQ)
                        pool.wait_ge(part2_ready.sem, part2_ready.at((L, p, b)))
                        pool.wait_ge(rest_ready.sem, rest_ready.at((L, p, b)))
                        nc.gpsimd.tensor_tensor(qk_parts[:, 2, :, cols], rest[:, :, cols],
                                                qk_parts[:, 1, :, cols], ALU.subtract).then_inc(part3_ready.sem, 1)

                def position_part3(p, n):
                    pool.wait_ge(pos_part2_ready.sem, pos_part2_ready.at((p, n)))
                    pool.wait_ge(pos_rest_ready.sem, pos_rest_ready.at((p, n)))
                    nc.gpsimd.tensor_tensor(att_parts[:, n % 2, 2], pos_rest[:, n % 2], att_parts[:, n % 2, 1],
                                            ALU.subtract).then_inc(pos_part3_ready.sem, 1)

                def copy_v(L, p):
                    pool.wait_ge(new_v_ready.sem, new_v_ready.at((L, p)))
                    g = NUMBER[L, p, 0]
                    if g:
                        pool.wait_ge(values_weighed.sem, values_weighed.at(CHUNKS[g - 1]))
                    nc.gpsimd.tensor_copy(v[:, :, :, 0:DH], new_v).then_inc(v_ready.sem, 1)

                do = {"norm1": root, "xt": add_bias, "split1": take_rests, "split2": take_part3,
                      "att_late": position_part3, "v_copy": copy_v}
                for kind, *key in plan:
                    if kind in ("q", "k"):
                        add_centre(kind, *key)
                    elif kind in do:
                        do[kind](*key)


def kernel(**inputs):
    import numpy as _np
    import concourse.bacc as _bacc
    from concourse import mybir as _mybir
    from concourse.bass_utils import run_bass_kernel_spmd as _run

    nc = _bacc.Bacc("TRN2", target_bir_lowering=False, num_devices=1, dynamic_dma_scratch_size=1024)
    arrays = {name: _np.ascontiguousarray(a) for name, a in inputs.items() if name != "L0_attn_b_attention_mask"}
    arrays["constants"] = constant_table()
    aps = {n: nc.dram_tensor(n, a.shape, _mybir.dt.from_np(a.dtype), kind="ExternalInput").ap()
           for n, a in arrays.items()}
    aps["out"] = nc.dram_tensor("out", inputs["L0_attn_a_x"].shape, _mybir.dt.float32, kind="ExternalOutput").ap()
    build(nc, aps)
    return _run(nc, [arrays], core_ids=[0]).results[0]["out"]
```

```python
from contextlib import ExitStack

import numpy as np

import concourse.bass as bass
from concourse import mybir
from concourse.alu_op_type import AluOpType as ALU

F32 = mybir.dt.float32
BF16 = mybir.dt.bfloat16
ACT = mybir.ActivationFunctionType
AX = mybir.AxisListType

P = 128
D = 128
NH = 16
DH = D // NH
SEQ = 256
NB = 2
NT = NB * SEQ // P
TOK = NB * SEQ
HC = 4
NG = NB * 2
NCH = NG * NH // HC
BH = NB * NH
VC = 32
PARTS = 3
KS = PARTS * PARTS * DH
NE, HE, R = 8, 32, 64
SELW = R + D + 1
SPAN, MAX_REL = 32, 64
NIDX = 32
CEN_C, CEN_P = SPAN + SPAN // 2 - 1, SPAN - SPAN // 2 + 1
EPS_LN, EPS_B = 1e-5, 1e-7
SCALE_A = 1.0 / float(np.sqrt(np.float32(DH)))
SCALE_B = 1.0 / float(np.sqrt(np.float32(3 * DH)))
RELW = 2 * SEQ


def relative_buckets():
    rel = np.arange(-(SEQ - 1), SEQ)
    mid = SPAN // 2
    a = np.where((rel < mid) & (rel > -mid), mid - 1, np.abs(rel)).astype(np.float32)
    steps = np.log(a / np.float32(mid)) / np.log(np.float32((MAX_REL - 1) / mid)) * np.float32(mid - 1)
    log_pos = np.ceil(steps.astype(np.float32)) + mid
    return np.where(a <= mid, a, log_pos * np.sign(rel)).astype(np.int32)


def constant_table():
    bucket = dict(zip(range(-(SEQ - 1), SEQ), relative_buckets()))
    order_c = list(range(0, 16)) + list(range(48, 64))
    order_p = list(range(0, 17)) + list(range(49, 64))
    ohc = np.zeros((P, RELW), np.float32)
    ohp = np.zeros((P, RELW), np.float32)
    for r, _ in bucket.items():
        c = int(np.clip(bucket[r] + SPAN, 0, 2 * SPAN - 1))
        p = int(np.clip(-bucket[-r] + SPAN, 0, 2 * SPAN - 1))
        for part in range(PARTS):
            if c != CEN_C:
                ohc[part * NIDX + order_c.index(c), SEQ - 1 - r] = 1.0
            if p != CEN_P:
                ohp[part * NIDX + order_p.index(p), SEQ - 1 + r] = 1.0
    mask = np.zeros((P, NH), np.float32)
    for p in range(P):
        h = p % NH
        mask[p, (h % 4) * 4 + h // 4] = 1.0
    iota = np.broadcast_to(np.arange(NE, dtype=np.float32), (P, NE))
    return np.ascontiguousarray(np.concatenate([np.eye(P, dtype=np.float32), mask, iota, ohc, ohp], axis=1))


C_ID, C_MASK = 0, P
C_IOTA = C_MASK + NH
CW = C_IOTA + NE


class Signal:

    def __init__(self, sem, keys, step=1):
        self.sem, self.step = sem, step
        self.place = {k: n + 1 for n, k in enumerate(keys)}
        assert len(self.place) == len(keys)

    def at(self, key):
        return self.place[key] * self.step


PAIRS = 8 // NB
CHUNKS = [(L, p, i) for L in "ab" for p in range(PAIRS) for i in range(NCH)]
NUMBER = {c: g for g, c in enumerate(CHUNKS)}
POS_BUFS = 3
POS = 8
DJ = 8


def group(n):
    L, p, i = CHUNKS[HC * n]
    m = i // HC
    return (L, p, m // 2, m % 2) if L == "a" else (L, p, m % 2, m // 2)


def front_steps(L, p):
    slots = [[("norm1", L, p)], [], [("norm2", L, p)], [], [("xt", L, p)], [], [("q", L, p)], [("k", L, p)], []]
    if L == "b":
        for n in range(POS + 1):
            slots.append(([("att", p, n)] if n < POS else []) + ([("att_late", p, n - 1)] if n else []))
        slots += [[("v", L, p)], [], []]
    slots += [[("split1", L, p)], [], []]
    if L == "a":
        slots += [[("v", L, p)]]
    return slots + [[("split2", L, p), ("load_qk", L, p)]]


def ffn_steps(s, p):
    slots = [[("norm1", s, p)], [], [], [("norm2", s, p)], [], [("xt", s, p)], [], [("h", s, p, 0)], [("h", s, p, 1)], []]
    slots += [[("rec", s, p, e)] + ([("square", s, p, e - 1)] if e else []) for e in range(NE)]
    slots += [[("square", s, p, NE - 1)], [], [("loss", s, p)]] + [[("pick", s, p, n)] for n in range(4)]
    slots += [[], [], [("act", s, p)], [], [], [("ffo", s, p)]]
    if s == "g":
        slots.append([("store", p)])
    return slots


def inner_steps(p):
    return [[("norm1", "n", p)], [], [("norm2", "n", p), ("inner", p)], []]


BANK_JOBS = ("xt", "q", "k", "att", "v", "h", "rec", "loss", "act", "ffo", "OB", "OT", "OP")
JOB_GAP = 1
POS_JOB_GAP = {"a": 2, "b": 1}


def make_plan():
    last = PAIRS - 1
    assert PAIRS == 4
    sides = {
        ("a", 0): [(0, front_steps("a", 1))],
        ("a", 1): [(0, front_steps("a", 2)), (16, ffn_steps("f", 0))],
        ("a", 2): [(0, front_steps("a", 3)), (0, ffn_steps("f", 1))],
        ("a", 3): [(0, front_steps("b", 0)), (16, ffn_steps("f", 2))],
        ("b", 0): [(6, front_steps("b", 1)), (0, ffn_steps("f", 3))],
        ("b", 1): [(20, inner_steps(0)), (0, front_steps("b", 2)), (0, ffn_steps("g", 0))],
        ("b", 2): [(20, inner_steps(1)), (0, front_steps("b", 3)), (0, ffn_steps("g", 1))],
        ("b", 3): [(20, inner_steps(2)), (0, ffn_steps("g", 2))],
    }
    plan = [s for slot in front_steps("a", 0) for s in slot] + [("v_copy", "a", 0)]
    due = []
    done = set()
    count = start = last_job = 0
    side = []

    def emit(steps, side):
        nonlocal count, due, last_job
        plan.extend(steps)
        count += 1
        steps_due = [s for when, s in sorted(d for d in due if d[0] <= count)]
        plan.extend(steps_due)
        due = [d for d in due if d[0] > count]
        for s in steps:
            if s[0] == "PV" and s[3] % HC == HC - 1:
                n = NUMBER[s[1:]] // HC
                plan.append(("OM", n))
                due += [(count + 3, ("OB", n)), (count + 6, ("OT", n)), (count + 9, ("OP", n))]
        for step in steps_due:
            if step[0] in BANK_JOBS:
                last_job = count
        if side:
            jobs = [s[0] for s in side[0][1] if s[0] in BANK_JOBS]
            gap = POS_JOB_GAP[L] if jobs == ["att"] else JOB_GAP
            if count - start >= side[0][0] and (not jobs or count - last_job >= gap):
                plan.extend(side.pop(0)[1])
                if jobs:
                    last_job = count

    def weigh(g):
        if g < 0 or g in done:
            return []
        done.add(g)
        nxt = [("v_copy",) + CHUNKS[g + 1][:2]] if g % NCH == NCH - 1 and g + 1 < len(CHUNKS) else []
        return [("PV",) + CHUNKS[g]] + nxt

    turned = set()

    def turn(g):
        if g < 0 or g in turned:
            return []
        turned.add(g)
        return [("T",) + CHUNKS[g]]

    for L in "ab":
        for p in range(PAIRS):
            start = count
            side = [(0, slot) for _, slot in side]
            side += [(first, slot) for first, slots in sides[L, p] for slot in slots]
            for i in range(NCH):
                g = NUMBER[L, p, i]
                if L == "b" and i % (NCH // 2) == 0:
                    jobs = [(p, i * 2 // NCH, c, j) for c in "cp" for j in range(DJ)]
                    for m, key in enumerate(jobs):
                        emit([("D",) + key], side)
                        if m == 1:
                            emit(turn(g - 1), side)
                        if m == 3:
                            emit(weigh(g - 2), side)
                        if m == 6:
                            emit(weigh(g - 1), side)
                emit([("S", L, p, i)], side)
                for steps in (turn(g - 1), weigh(g - 2)):
                    if steps:
                        emit(steps, side)
    emit(turn(len(CHUNKS) - 1), side)
    emit(weigh(len(CHUNKS) - 2), side)
    emit(weigh(len(CHUNKS) - 1), side)
    while due:
        emit([], side)
    for _, slot in side:
        plan.extend(slot)
    for slot in inner_steps(last) + ffn_steps("g", last):
        plan.extend(slot)
    return plan


def build(nc, t):
    with ExitStack() as ctx:
        def sb(name, shape, dt=F32):
            return ctx.enter_context(nc.sbuf_tensor(name, shape, dt))

        def sem(name):
            return ctx.enter_context(nc.semaphore(name))

        cst = sb("cst", [P, CW])
        ident = cst[:, C_ID:C_ID + P]
        iota = cst[:, C_IOTA:C_IOTA + NE]
        oh_c = sb("oh_c", [P, RELW], BF16)
        oh_p = sb("oh_p", [P, RELW], BF16)
        ones = sb("ones", [P, P])
        neg_half = sb("neg_half", [P, NT])
        wq, wk, wv, wo = ({L: sb(f"{n}_{L}", [P, D]) for L in "ab"} for n in ("wq", "wk", "wv", "wo"))
        bq, bk = ({L: sb(f"{n}_{L}", [P, 1]) for L in "ab"} for n in ("bq", "bk"))
        bv, bo = ({L: sb(f"{n}_{L}", [P, D]) for L in "ab"} for n in ("bv", "bo"))
        centre = sb("centre", [P, 2])
        ln_s, ln_b = sb("ln_s", [P, D]), sb("ln_b", [P, D])
        pos_w = {y: sb(f"pos_w_{y}", [P, 4, NIDX, 4]) for y in "cp"}
        w_base = sb("w_base", [P, D])
        wd1 = sb("wd1", [P, NE, HE])
        bd1 = sb("bd1", [P, 2])
        wd2 = sb("wd2", [P, NE // 4, D])
        bd2 = sb("bd2", [P, NE])
        w_all = sb("w_all", [P, NE, SELW])

        x = sb("x", [P, PAIRS, NT, D])
        xn = sb("xn", [P, 2, NT, D])
        xnT = sb("xnT", [P, TOK])
        stats = sb("stats", [P, NT, 6])
        mv = sb("mv", [P, NT, 2])
        ve = sb("ve", [P, NT])
        rstd = sb("rstd", [P, NT])
        parts = sb("parts", [P, PARTS * POS_BUFS * TOK], BF16)
        qk_parts = parts[:, 0:PARTS * 2 * TOK].rearrange("p (s n t) -> p s n t", s=PARTS, n=2)
        att_parts = parts[:].rearrange("p (n s g t) -> p n s g t", n=POS_BUFS, s=PARTS, g=2)
        v = sb("v", [P, NT, NH, VC])
        stack_0 = sb("stack_0", [KS, 2, NB, NH, SEQ], BF16)
        prob = sb("prob", [P, 2, HC, SEQ])
        probT = sb("probT", [P, 2, HC, 2, P])
        qk = sb("qk", [P, 2, TOK])
        rest = sb("rest", [P, 2, TOK])
        pos_rest = rest[:].rearrange("p n (g t) -> p n g t", g=2)
        hT, diff = qk, rest
        nmax = sb("nmax", [P, 2, HC])
        nbias = sb("nbias", [P, 2, HC])
        rsum = sb("rsum", [P, 2, NH])
        rinv = sb("rinv", [P, 2, NH])
        o_sb = sb("o_sb", [P, NH, DH])
        oT = sb("oT", [P, P])
        o_turned = sb("o_turned", [P, HC, P])
        plain = sb("plain", [P, 2, TOK])
        new_v = plain[:, 0, :].rearrange("p (t h d) -> p t h d", t=NT, h=NH)
        ffn_xn = plain[:, 1, :].rearrange("p (t n) -> p t n", t=NT)
        att = {y: sb(f"att_{y}", [PARTS * NIDX, NB, NH, SEQ], BF16) for y in "cp"}
        c2p = sb("c2p", [P, 2, BH, P])
        p2c = sb("p2c", [P, BH, SEQ])
        stack_1 = c2p[:].rearrange("p a b c -> p (a b c)").bitcast(BF16).rearrange(
            "p (n b h t) -> p n b h t", n=2, b=NB, h=NH)[0:KS]
        stacks = [stack_0[:], stack_1]
        tables = c2p[:].rearrange("p a b c -> p (a b c)")[:, 0:2 * RELW]
        aT = sb("aT", [R + 1, TOK])
        w_sel = sb("w_sel", [P, NB, SELW])
        loss_p = sb("loss_p", [P, NB, NE])
        lmin, lkey, kmin, onehot = (sb(n, s) for n, s in (
            ("lmin", [P, NB]), ("lkey", [P, NB, NE]), ("kmin", [P, NB]), ("onehot", [P, NB, NE])))
        spare = p2c[:].rearrange("p a b -> p (a b)")
        rel_sb = spare[0:2 * SPAN, 0:D]
        relT = spare[:, D:D + 2 * SPAN]
        posT = spare[:, 2 * D:2 * D + 2 * SPAN]
        dpos = {c: spare[:, (3 + k) * D:(3 + k) * D + NIDX] for k, c in enumerate("cp")}
        rows = {n: spare[:, (5 + k) * D:(6 + k) * D] for k, n in enumerate(("q", "k", "v", "o"))}
        raw = {n: spare[:, (9 + k) * D:(10 + k) * D] for k, n in enumerate("qk")}

        ps_s = [ctx.enter_context(nc.psum_tensor(f"ps_s{n}", [P, 512], F32)) for n in range(3)]
        ps_t = [ctx.enter_context(nc.psum_tensor(f"ps_t{n}", [P, 512], F32)) for n in range(2)]
        ps_o = ctx.enter_context(nc.psum_tensor("ps_o", [P, 512], F32))
        ps_m = [ctx.enter_context(nc.psum_tensor(f"ps_m{n}", [P, 512], F32)) for n in range(2)]

        q_dram = nc.dram_tensor("q_scratch", (NB, PARTS, PARTS, P, SEQ), BF16, kind="Internal").ap()
        k_dram = nc.dram_tensor("k_scratch", (NB, PARTS, P, SEQ), BF16, kind="Internal").ap()
        att_dram = nc.dram_tensor("att_scratch", (2, NB, PARTS, P, 4 * SEQ), BF16, kind="Internal").ap()

        s_cst, s_x, s_load, s_rows, s_wd2 = sem("s_cst"), sem("s_x"), sem("s_load"), sem("s_rows"), sem("s_wd2")
        s_zero, s_tr, s_trc, s_pos, s_perm, s_bb = (
            sem(n) for n in ("s_zero", "s_tr", "s_trc", "s_pos", "s_perm", "s_bb"))
        qkv_c = t["L0_attn_a_W_qkv"].rearrange("(h c) i -> c h i", c=3 * DH)
        qkv_h = t["L0_attn_a_W_qkv"].rearrange("(h c) i -> h c i", c=3 * DH)
        bqkv_c = t["L0_attn_a_b_qkv"].rearrange("(h c u) -> c h u", c=3 * DH, u=1)
        bqkv_h = t["L0_attn_a_b_qkv"].rearrange("(h c) -> h c", c=3 * DH)

        def column(name):
            return t[name].rearrange("(h d u) -> d h u", d=DH, u=1)

        def everywhere(name):
            return t[name].rearrange("(u n) -> u n", u=1).to_broadcast([P, D])

        loads = [
            (w_base[:], t["L0_ffn_W_base"]),
            (wv["b"][:], t["L0_attn_b_Wv"]), (wo["b"][:], t["L0_attn_b_Wo"]),
            (raw["q"], t["L0_attn_b_Wq"]), (raw["k"], t["L0_attn_b_Wk"]),
            (rel_sb, t["L0_attn_b_rel_embeddings"]),
            (bq["a"][:], bqkv_c[0:DH]), (bk["a"][:], bqkv_c[DH:2 * DH]),
            (bv["a"][:].rearrange("p (h d) -> p h d", d=DH),
             bqkv_h[:, 2 * DH:].rearrange("(u h) d -> u h d", u=1).to_broadcast([P, NH, DH])),
            (bo["a"][:], everywhere("L0_attn_a_b_out")),
            (bq["b"][:], column("L0_attn_b_bq")), (bk["b"][:], column("L0_attn_b_bk")),
            (bv["b"][:], everywhere("L0_attn_b_bv")), (bo["b"][:], everywhere("L0_attn_b_bo")),
            (ln_s[:], everywhere("L0_attn_b_ln_scale")), (ln_b[:], everywhere("L0_attn_b_ln_bias")),
            (wd1[:], t["L0_ffn_Wd1"].rearrange("e d h -> d e h")),
            (bd1[:], t["L0_ffn_bd1"].rearrange("(j e) h -> (e h) j", j=2)),
            (bd2[:], t["L0_ffn_bd2"].rearrange("e d -> d e")),
        ]
        loads_zeroed = [
            (w_all[:, :, 0:R], t["L0_ffn_Wa_down"].rearrange("e d r -> d e r")),
            (w_all[0:R, :, R:R + D], t["L0_ffn_Wa_up"].rearrange("e r o -> r e o")),
            (w_all[R:R + 1, :, R:R + D], t["L0_ffn_ba_up"].rearrange("(u e) o -> u e o", u=1)),
            (w_all[0:R, :, R + D:SELW], t["L0_ffn_ba_down"].rearrange("e (r u) -> r e u", u=1)),
            (aT[R:R + 1, 0:D], t["L0_ffn_b_base"].rearrange("(u n) -> u n", u=1)),
        ] + [(wd2[:], t["L0_ffn_Wd2"].rearrange("(j e) h d -> (e h) j d", j=2))]

        ctx.enter_context(nc.allow_non_contiguous_dma(reason="bias vectors laid out one element per partition"))
        with nc.Block() as block:
            @block.sync
            def _(sp):
                sp.dma_start(cst[:], t["constants"][:, 0:CW]).then_inc(s_cst, 16)
                sp.dma_start(tables, t["constants"][:, CW:]).then_inc(s_cst, 16)
                sp.dma_start(rows["q"], qkv_c[0:DH]).then_inc(s_rows, 16)
                sp.dma_start(rows["k"], qkv_c[DH:2 * DH]).then_inc(s_rows, 16)
                sp.dma_start(rows["v"], qkv_h[:, 2 * DH:]).then_inc(s_rows, 16)
                sp.dma_start(rows["o"], t["L0_attn_a_W_out"]).then_inc(s_rows, 16)
                sp.dma_start(x[:].rearrange("p a t d -> p (a t) d"),
                             t["L0_attn_a_x"].rearrange("b (t p) d -> p (b t) d", p=P)).then_inc(s_x, 16)
                for dst, src in loads:
                    sp.dma_start(dst, src).then_inc(s_load, 16)
                sp.wait_ge(s_zero, 2)
                for dst, src in loads_zeroed:
                    sp.dma_start(dst, src).then_inc(s_wd2, 16)
                sp.wait_ge(s_x, 16)
                sp.wait_ge(s_load, 16 * len(loads))
                sp.wait_ge(s_wd2, 16 * len(loads_zeroed))

            @block.gpsimd
            def _(pool):
                nc.gpsimd.memset(w_all[:], 0.0).then_inc(s_zero, 1)
                nc.gpsimd.memset(neg_half[:], -0.5).then_inc(s_zero, 1)
                nc.gpsimd.memset(ones[:], 1.0).then_inc(s_zero, 1)
                nc.gpsimd.memset(v[:], 0.0).then_inc(s_zero, 1)
                pool.wait_ge(s_zero, 4)
                pool.wait_ge(s_wd2, 16 * len(loads_zeroed))
                nc.gpsimd.tensor_tensor(
                    w_all[R:R + 1, :, R:R + D], w_all[R:R + 1, :, R:R + D],
                    aT[R:R + 1, 0:D].rearrange("u (e n) -> u e n", e=1).to_broadcast([1, NE, D]),
                    ALU.add).then_inc(s_bb, 1)
                pool.wait_ge(s_bb, 1)
                nc.gpsimd.memset(aT[R:R + 1, :], 1.0).then_inc(s_bb, 1)
                pool.wait_ge(s_bb, 2)

            @block.tensor
            def _(pe):
                pe.wait_ge(s_cst, 32)
                pe.wait_ge(s_rows, 16 * 4)
                for k, n in enumerate("qkvo"):
                    ins = nc.tensor.transpose(ps_m[0][:, k * P:(k + 1) * P], rows[n], ident)
                ins.then_inc(s_tr, 1)
                pe.wait_ge(s_load, 16 * len(loads))
                nc.tensor.transpose(ps_o[:, 0:2 * SPAN], rel_sb, ident[0:2 * SPAN, 0:2 * SPAN]).then_inc(s_tr, 1)
                pe.wait_ge(s_trc, 5)
                pe.wait_ge(s_perm, 2)
                nc.tensor.matmul(ps_t[0][:, 0:2 * SPAN], wk["b"][:], relT, start=True, stop=True).then_inc(s_tr, 1)

            @block.vector
            def _(dve):
                dve.wait_ge(s_cst, 32)
                nc.vector.tensor_copy(oh_c[:], tables[:, 0:RELW])
                nc.vector.tensor_copy(oh_p[:], tables[:, RELW:])
                dve.wait_ge(s_tr, 1)
                for k, w in enumerate((wq["a"], wk["a"], wv["a"], wo["a"])):
                    nc.vector.tensor_copy(w[:], ps_m[0][:, k * P:(k + 1) * P]).then_inc(s_trc, 1)
                dve.wait_ge(s_load, 16 * len(loads))
                for n, w in (("q", wq["b"]), ("k", wk["b"])):
                    nc.vector.tensor_copy(w[:].rearrange("p (d h) -> p d h", d=DH),
                                          raw[n].rearrange("p (h d) -> p d h", d=DH)).then_inc(s_perm, 1)
                dve.wait_ge(s_tr, 2)
                nc.vector.tensor_copy(relT, ps_o[:, 0:2 * SPAN]).then_inc(s_trc, 1)
                dve.wait_ge(s_tr, 3)
                nc.vector.tensor_scalar(posT, ps_t[0][:, 0:2 * SPAN], bk["b"][:], None, ALU.add).then_inc(s_pos, 1)
                dve.wait_ge(s_pos, 1)
                nc.vector.tensor_copy(centre[:, 0:1], posT[:, CEN_P:CEN_P + 1])
                nc.vector.tensor_copy(centre[:, 1:2], posT[:, CEN_C:CEN_C + 1])
                for c, cen, cut, nxt in (("c", CEN_C, 16, 48), ("p", CEN_P, 17, 49)):
                    nc.vector.tensor_scalar(dpos[c][:, 0:cut], posT[:, 0:cut], posT[:, cen:cen + 1], None,
                                            ALU.subtract).then_inc(s_pos, 1)
                    nc.vector.tensor_scalar(dpos[c][:, cut:], posT[:, nxt:], posT[:, cen:cen + 1], None,
                                            ALU.subtract).then_inc(s_pos, 1)
                dve.wait_ge(s_pos, 5)
                for c in "cp":
                    for g in range(4):
                        m = cst[:, C_MASK + 4 * g:C_MASK + 4 * g + 4].rearrange("p (u h) -> p u h", u=1)
                        nc.vector.tensor_tensor(
                            pos_w[c][:, g], dpos[c].rearrange("p (i u) -> p i u", u=1).to_broadcast([P, NIDX, 4]),
                            m.to_broadcast([P, NIDX, 4]), ALU.mult)

        nc.all_engine_barrier()

        plan = make_plan()

        def order(*kinds):
            return [s[1:] for s in plan if s[0] in kinds]

        def signal(name, keys, step=1):
            return Signal(sem(name), list(keys), step)

        s_jobs = [s + (half,) for s in plan if s[0] in ("S", "D") for half in range(2)]
        score_keys = [s[1:] for s in s_jobs if s[0] == "S"]
        m_jobs = [s for s in plan if s[0] in ("xt", "q", "k", "att", "v", "h", "rec", "loss", "act", "ffo", "OB", "OT", "OP")
                  and not (s[0] == "att" and s[2] >= POS)]
        s_place = {s: n for n, s in enumerate(s_jobs)}
        m_place = {s: n for n, s in enumerate(m_jobs)}
        fronts = order("q")
        norms, turns = order("norm2"), order("xt")
        ffns = order("loss")
        n_groups = len(CHUNKS) // HC

        parts_stored = {b: signal(f"parts_stored{b}", [k + (n,) for k in fronts for n in range(1 + PARTS)], 16) for b in range(NB)}
        stack_loaded = {b: signal(f"stack_loaded{b}", [k + (n,) for k in fronts for n in range(1 + PARTS)], 16) for b in range(NB)}
        pos_parts_stored = {m: signal(f"pos_parts_stored{m}", [k for k in order("att_late") if k[1] % POS_BUFS == m], 16) for m in range(POS_BUFS)}
        pos_stack_loaded = {c: signal(f"pos_stack_loaded_{c}", [(p, b) for p in range(PAIRS) for b in range(NB)], 16) for c in "cp"}
        out_stored = signal("out_stored", order("store"), 16)

        score_bank_filled = signal("score_bank_filled", s_jobs)
        small_bank_filled = signal("small_bank_filled", m_jobs)
        probs_turned = signal("probs_turned", [c + (hh,) for c in CHUNKS for hh in range(2)])
        values_weighed = signal("values_weighed", CHUNKS)

        stats_done = signal("stats_done", [k + (n,) for k in order("norm1") for n in range(2 * NT)])
        variance_done = signal("variance_done", order("norm1"))
        root_done = signal("root_done", order("norm1"))
        normed = signal("normed", [k + (n,) for k in norms for n in range(NT)])
        bias_added = signal("bias_added", [s[1:] for s in plan if (s[0] == "xt" and s[1] in "ab") or (s[0] == "norm1" and s[1] == "n")])
        xnT_ready = signal("xnT_ready", turns)
        plain_ready = signal("plain_ready", [(p, n) for L, p in fronts if L == "b" for n in range(2)])
        qk_ready_a = signal("qk_ready_a", [(p, n) for L, p in fronts if L == "a" for n in range(2)])
        qk_ready_b = signal("qk_ready_b", [(p, n) for L, p in fronts if L == "b" for n in range(2)])
        new_v_ready = signal("new_v_ready", order("v"))
        v_ready = signal("v_ready", order("v_copy"))
        split_keys = [k + (b,) for k in fronts for b in range(NB)]
        part1_ready, part2_ready = signal("part1_ready", split_keys), signal("part2_ready", split_keys)
        rest_ready, part3_ready = signal("rest_ready", split_keys), signal("part3_ready", split_keys)
        pos_keys = order("att_late")
        pos_part1_ready, pos_part2_ready = signal("pos_part1_ready", pos_keys), signal("pos_part2_ready", pos_keys)
        pos_rest_ready, pos_part3_ready = signal("pos_rest_ready", pos_keys), signal("pos_part3_ready", pos_keys)
        spread_by_act = signal("spread_by_act", order("D"))
        spread_by_dve = signal("spread_by_dve", order("D"))
        scores_summed = signal("scores_summed", [c for c in score_keys if c[0] == "b"])
        max_ready = signal("max_ready", [c for c in score_keys if c[0] == "a"])
        exp_bias_ready = signal("exp_bias_ready", score_keys)
        probs_ready = signal("probs_ready", score_keys)

        def t_engine(chunk, hh):
            if hh == 0:
                return "dve"
            return "act" if chunk[0] == "b" or chunk[2] % 2 == 0 else "dve"

        halves = [(c, hh) for c in CHUNKS for hh in range(2)]
        moved_by = {e: signal(f"probT_by_{e}", [k for k in halves if t_engine(*k) == e]) for e in ("act", "dve")}
        inverse_ready = signal("inverse_ready", range(n_groups))
        out_moved = signal("out_moved", range(n_groups))
        heads_out_ready = signal("heads_out_ready", range(n_groups))
        outT_ready = signal("outT_ready", range(n_groups))
        residual_added = signal("residual_added", range(n_groups))
        hidden_ready = signal("hidden_ready", order("h"))
        diff_ready = signal("diff_ready", order("rec"))
        losses_ready = signal("losses_ready", order("square"))
        choice_step = signal("choice_step", [k + (n,) for k in ffns for n in range(5)])
        expert_added = signal("expert_added", [k + (b, e) for k in ffns for e in range(NE) for b in range(NB)])
        adapter_hidden_ready = signal("adapter_hidden_ready", [k + (b,) for k in ffns for b in range(NB)])
        ffn_added = signal("ffn_added", ffns)
        inner_norm_step = signal("inner_norm_step", [(p, n) for p in range(PAIRS) for n in range(2)])

        def before(keys, key):
            n = keys.index(key)
            return keys[n - 1] if n else None

        last_ffn_before, last_front_before = {}, {}
        seen_ffn = seen_front = None
        for kind, *key in plan:
            if kind == "norm1" and key[0] != "n":
                last_ffn_before[tuple(key)], last_front_before[tuple(key)] = seen_ffn, seen_front
                if key[0] in "fg":
                    seen_ffn = tuple(key)
                else:
                    seen_front = tuple(key)

        def last_chunk_of_group(n):
            return CHUNKS[HC * n + HC - 1]

        def take_s(pe, job):
            n = s_place[job]
            if n >= 3:
                kind, *key = s_jobs[n - 3]
                key = tuple(key)
                if kind == "S":
                    read_out = probs_ready if key[0] == "a" else scores_summed
                else:
                    read_out, key = (spread_by_act if key[4] else spread_by_dve), key[:4]
                pe.wait_ge(read_out.sem, read_out.at(key))
            return ps_s[n % 3]

        def score_bank(job):
            return ps_s[s_place[job] % 3]

        def small_bank(*job):
            return ps_m[m_place[job] % 2]

        def take_m(pe, job):
            n = m_place[job]
            if n >= 2:
                kind, *key = m_jobs[n - 2]
                key = tuple(key)
                if kind in ("q", "k"):
                    read_out = qk_ready_a if key[0] == "a" else plain_ready
                    key = (key[1], "qk".index(kind))
                elif kind == "loss":
                    read_out, key = choice_step, key + (1,)
                elif kind == "act":
                    read_out, key = adapter_hidden_ready, key + (NB - 1,)
                elif kind in ("OB", "OT", "OP"):
                    read_out = {"OB": heads_out_ready, "OT": outT_ready, "OP": residual_added}[kind]
                    key = key[0]
                else:
                    read_out = {"xt": xnT_ready, "att": pos_rest_ready, "v": new_v_ready, "h": hidden_ready,
                                "rec": diff_ready, "ffo": ffn_added}[kind]
                pe.wait_ge(read_out.sem, read_out.at(key))
            return ps_m[n % 2]

        def spread_views(k, half):
            p, qt, c, j = k
            src = score_bank(("D",) + k + (half,))[:].rearrange("p (n b) -> p b n", b=BH)
            first = j * 32 + half * 16
            if c == "c":
                return c2p[:, j // 4, :, first % P:first % P + 16], src
            return p2c[:, :, first:first + 16], src

        def stack(L, p):
            return stacks[p % 2 if L == "a" else 0]

        def last_reader_of_stack(L, p):
            if L == "a":
                return ("a", p - 2, NCH - 1) if p >= 2 else None
            return ("b", p - 1, NCH - 1) if p else ("a", PAIRS - 2 + PAIRS % 2, NCH - 1)

        x_rows = t["L0_attn_a_x"].rearrange("b (t p) d -> (b t) p d", p=P)
        out_rows = t["out"].rearrange("b (t p) d -> (b t) p d", p=P)
        chunk_before_half = {}
        for p in range(PAIRS):
            for qt in range(2):
                chunk_before_half[p, qt] = CHUNKS[NUMBER["b", p, qt * NCH // 2] - 1]

        with nc.Block() as block:

            @block.sync
            def _(sp):
                def store_qk(L, p, b):
                    sp.wait_ge(part3_ready.sem, part3_ready.at((L, p, b)))
                    sp.wait_ge(part2_ready.sem, part2_ready.at((L, p, b)))
                    if before(fronts, (L, p)):
                        sp.wait_ge(stack_loaded[b].sem, stack_loaded[b].at(before(fronts, (L, p)) + (PARTS,)))
                    parts_of = [qk_parts[:, :, n, b * SEQ:(b + 1) * SEQ] for n in range(2)]
                    sp.dma_start(k_dram[b].rearrange("j p t -> p j t"), parts_of[1]).then_inc(parts_stored[b].sem, 16)
                    for j in range(PARTS):
                        sp.dma_start(q_dram[b, :, j].rearrange("i p t -> p i t"), parts_of[0]).then_inc(parts_stored[b].sem, 16)

                def load_qk(L, p, b):
                    q_stack, k_stack = (stack(L, p)[:, n] for n in range(2))
                    sp.wait_ge(parts_stored[b].sem, parts_stored[b].at((L, p, PARTS)))
                    if b == 0 and last_reader_of_stack(L, p):
                        sp.wait_ge(score_bank_filled.sem, score_bank_filled.at(("S",) + last_reader_of_stack(L, p) + (1,)))
                    for i in range(PARTS):
                        sp.dma_start(
                            k_stack[i * PARTS * DH:(i + 1) * PARTS * DH, b].rearrange("r h t -> r (h t)"),
                            k_dram[b].rearrange("j (d h) t -> (j d) (h t)", d=DH)).then_inc(stack_loaded[b].sem, 16)
                    sp.dma_start(
                        q_stack[:, b].rearrange("r h t -> r (h t)"),
                        q_dram[b].rearrange("i j (d h) t -> (i j d) (h t)", d=DH)).then_inc(stack_loaded[b].sem, 16)

                def store_positions(p, n):
                    c, b, half = n // 4, n // 2 % 2, n % 2
                    sp.wait_ge(pos_part3_ready.sem, pos_part3_ready.at((p, n)))
                    sp.wait_ge(pos_part2_ready.sem, pos_part2_ready.at((p, n)))
                    if p and n == 0:
                        sp.wait_ge(pos_stack_loaded["c"].sem, pos_stack_loaded["c"].at((p - 1, NB - 1)))
                        sp.wait_ge(pos_stack_loaded["p"].sem, pos_stack_loaded["p"].at((p - 1, NB - 1)))
                    sp.dma_start(att_dram[c, b].rearrange("s p t -> p s t")[:, :, half * 2 * SEQ:(half + 1) * 2 * SEQ],
                                 att_parts[:, n % POS_BUFS].rearrange("p s g t -> p s (g t)")).then_inc(
                                     pos_parts_stored[n % POS_BUFS].sem, 16)

                def load_positions(p, c, b):
                    if p:
                        sp.wait_ge(score_bank_filled.sem, score_bank_filled.at(("D", p - 1, 1, "p", DJ - 1, 1)))
                    n = 4 * c + 2 * b
                    for part in (n, n + 1):
                        stored = pos_parts_stored[part % POS_BUFS]
                        sp.wait_ge(stored.sem, stored.at((p, part)))
                    sp.dma_start(att["cp"[c]][:, b].rearrange("r h t -> r (h t)"),
                                 att_dram[c, b].rearrange("s (i a) t -> (s i) (a t)", a=4)).then_inc(
                                     pos_stack_loaded["cp"[c]].sem, 16)

                for kind, *key in plan:
                    if kind == "att_late":
                        p, n = key
                        store_positions(p, n)
                        if p == 0 and n >= 3 and n % 2:
                            load_positions(p, (n - 3) // 4, (n - 3) // 2 % 2)
                    elif kind == "split2":
                        if key == ["b", 0]:
                            load_positions(0, 1, 1)
                        for b in range(NB):
                            store_qk(*key, b)
                        if key[0] == "b" and key[1]:
                            for c in range(2):
                                for b in range(NB):
                                    load_positions(key[1], c, b)
                    elif kind == "load_qk":
                        for b in range(NB):
                            load_qk(*key, b)
                    elif kind == "store":
                        (p,) = key
                        sp.wait_ge(ffn_added.sem, ffn_added.at(("g", p)))
                        sp.dma_start(out_rows[p * NT:(p + 1) * NT].rearrange("t p d -> p t d"), x[:, p]).then_inc(out_stored.sem, 16)
                sp.wait_ge(out_stored.sem, out_stored.at((PAIRS - 1,)))

            @block.tensor
            def _(pe):
                def turn_xn(s, p):
                    src = ffn_xn if s in "fg" else xn[:, p % 2]
                    pe.wait_ge(normed.sem, normed.at((s, p, NT - 1)))
                    bank = take_m(pe, ("xt", s, p))
                    for k in range(NT):
                        ins = nc.tensor.transpose(bank[:, k * P:(k + 1) * P], src[:, k, :], ident)
                    ins.then_inc(small_bank_filled.sem, 1)

                def project(which, L, p):
                    pe.wait_ge(xnT_ready.sem, xnT_ready.at((L, p)))
                    bank = take_m(pe, (which, L, p))
                    w = wq[L] if which == "q" else wk[L]
                    nc.tensor.matmul(bank[:], w[:], xnT[:], start=True, stop=True).then_inc(small_bank_filled.sem, 1)

                def project_v(L, p):
                    bank = take_m(pe, ("v", L, p))
                    for k in range(NT):
                        ins = nc.tensor.matmul(bank[:, k * P:(k + 1) * P], xnT[:, k * P:(k + 1) * P],
                                               wv[L][:], start=True, stop=True)
                    ins.then_inc(small_bank_filled.sem, 1)

                def position_terms(p, n):
                    c, b, half = n // 4, n // 2 % 2, n % 2
                    pe.wait_ge(plain_ready.sem, plain_ready.at((p, c)))
                    bank = take_m(pe, ("att", p, n))
                    for g in range(2):
                        ins = nc.tensor.matmul(bank[:, g * SEQ:(g + 1) * SEQ],
                                               pos_w["cp"[c]][:, 2 * half + g].rearrange("p i h -> p (i h)"),
                                               plain[:, c, b * SEQ:(b + 1) * SEQ], start=True, stop=True)
                    ins.then_inc(small_bank_filled.sem, 1)

                def spread_positions(p, qt, c, j):
                    if j == 0:
                        pe.wait_ge(pos_stack_loaded[c].sem, pos_stack_loaded[c].at((p, NB - 1)))
                    for half in range(2):
                        bank = take_s(pe, ("D", p, qt, c, j, half))[:].rearrange("p (n b) -> p n b", b=BH)
                        for u in range(16 * half, 16 * half + 16):
                            if c == "c":
                                fixed = qt * P + (j % 4) * 32 + u
                                start = SEQ - 1 - fixed + j // 4 * P
                                table = oh_c
                            else:
                                fixed = j * 32 + u
                                start = SEQ - 1 - fixed + qt * P
                                table = oh_p
                            ins = nc.tensor.matmul(
                                bank[:, u % 16, :], table[0:PARTS * NIDX, start:start + P],
                                att[c][:, :, :, fixed:fixed + 1].rearrange("r b h u -> r (b h u)"),
                                start=True, stop=True)
                        ins.then_inc(score_bank_filled.sem, 1)

                def scores(L, p, i):
                    _, _, b, qt = group(NUMBER[L, p, i] // HC)
                    q_stack, k_stack = (stack(L, p)[:, n] for n in range(2))
                    if i % HC == 0:
                        pe.wait_ge(stack_loaded[b].sem, stack_loaded[b].at((L, p, PARTS)))
                    if L == "b" and i % (NCH // 2) == 0:
                        pe.wait_ge(spread_by_act.sem, spread_by_act.at((p, qt, "c", DJ - 1)))
                        pe.wait_ge(spread_by_dve.sem, spread_by_dve.at((p, qt, "c", DJ - 1)))
                    for half in range(2):
                        bank = take_s(pe, ("S", L, p, i, half))[:].rearrange("p (k t) -> p k t", k=2)
                        for k in range(2):
                            h = (i % HC) * HC + 2 * half + k
                            if L == "b":
                                for kt in range(2):
                                    nc.tensor.matmul(bank[:, k, kt * P:(kt + 1) * P], c2p[:, kt, b * NH + h, :], ident,
                                                     start=(k == 0 and kt == 0), stop=False, is_transpose=True,
                                                     skip_group_check=True)
                            ins = nc.tensor.matmul(bank[:, k, :], q_stack[:, b, h, qt * P:(qt + 1) * P],
                                                   k_stack[:, b, h, :], start=(L == "a"), stop=True,
                                                   skip_group_check=True)
                        ins.then_inc(score_bank_filled.sem, 1)

                def turn_probs(L, p, i):
                    g = NUMBER[L, p, i]
                    for hh in range(2):
                        pe.wait_ge(probs_ready.sem, probs_ready.at((L, p, i, hh)))
                        if g:
                            key = (CHUNKS[g - 1], hh)
                            moved = moved_by[t_engine(*key)]
                            pe.wait_ge(moved.sem, moved.at(key))
                        for k in range(2):
                            for kt in range(2):
                                ins = nc.tensor.transpose(
                                    ps_t[hh][:, (2 * k + kt) * P:(2 * k + kt + 1) * P],
                                    prob[:, g % 2, 2 * hh + k, kt * P:(kt + 1) * P], ident)
                        ins.then_inc(probs_turned.sem, 1)

                def weigh_values(L, p, i):
                    g = NUMBER[L, p, i]
                    b = group(g // HC)[2]
                    if i == 0:
                        pe.wait_ge(v_ready.sem, v_ready.at((L, p)))
                    if i % HC == 0 and g:
                        pe.wait_ge(out_moved.sem, out_moved.at(g // HC - 1))
                    for hh in range(2):
                        key = ((L, p, i), hh)
                        moved = moved_by[t_engine(*key)]
                        pe.wait_ge(moved.sem, moved.at(key))
                    c = i % HC
                    for kt in range(2):
                        for k in range(HC):
                            ins = nc.tensor.matmul(ps_o[VC * k:VC * (k + 1), c * P:(c + 1) * P],
                                                   v[:, 2 * b + kt, c * HC + k, :], probT[:, g % 2, k, kt, :],
                                                   start=(kt == 0), stop=(kt == 1), skip_group_check=True)
                    ins.then_inc(values_weighed.sem, 1)

                def turn_back(n):
                    pe.wait_ge(out_moved.sem, out_moved.at(n))
                    bank = take_m(pe, ("OB", n))
                    for c in range(HC):
                        ins = nc.tensor.transpose(bank[:, c * P:(c + 1) * P], o_turned[:, c, :], ident)
                    ins.then_inc(small_bank_filled.sem, 1)

                def turn_out(n):
                    pe.wait_ge(heads_out_ready.sem, heads_out_ready.at(n))
                    bank = take_m(pe, ("OT", n))
                    nc.tensor.transpose(bank[:, 0:P], o_sb[:].rearrange("p h d -> p (h d)"),
                                        ident).then_inc(small_bank_filled.sem, 1)

                def project_out(n):
                    pe.wait_ge(outT_ready.sem, outT_ready.at(n))
                    bank = take_m(pe, ("OP", n))
                    nc.tensor.matmul(bank[:, 0:P], oT[:], wo[group(n)[0]][:], start=True, stop=True).then_inc(small_bank_filled.sem, 1)

                def hidden(s, p, j):
                    pe.wait_ge(xnT_ready.sem, xnT_ready.at((s, p)))
                    bank = take_m(pe, ("h", s, p, j))
                    nc.tensor.matmul(bank[:], wd1[:, 4 * j:4 * j + 4, :].rearrange("p e h -> p (e h)"),
                                     xnT[:], start=True, stop=True).then_inc(small_bank_filled.sem, 1)

                def reconstruct(s, p, e):
                    pe.wait_ge(hidden_ready.sem, hidden_ready.at((s, p, e // 4)))
                    bank = take_m(pe, ("rec", s, p, e))
                    rows = slice(HE * (e % 4), HE * (e % 4 + 1))
                    nc.tensor.matmul(bank[:], wd2[rows, e // 4, :], hT[rows, e // 4, :],
                                     start=True, stop=True).then_inc(small_bank_filled.sem, 1)

                def sum_losses(s, p):
                    pe.wait_ge(losses_ready.sem, losses_ready.at((s, p, NE - 1)))
                    bank = take_m(pe, ("loss", s, p))
                    nc.tensor.matmul(bank[:, 0:NB * NE], ones[:], loss_p[:].rearrange("p b e -> p (b e)"),
                                     start=True, stop=True).then_inc(small_bank_filled.sem, 1)

                def adapter_down(s, p):
                    bank = take_m(pe, ("act", s, p))
                    for b in range(NB):
                        pe.wait_ge(expert_added.sem, expert_added.at((s, p, b, NE - 1)))
                        ins = nc.tensor.matmul(bank[0:R, b * SEQ:(b + 1) * SEQ], w_sel[:, b, 0:R],
                                               xnT[:, b * SEQ:(b + 1) * SEQ], start=True, stop=True)
                    ins.then_inc(small_bank_filled.sem, 1)

                def ffn_out(s, p):
                    bank = take_m(pe, ("ffo", s, p))
                    pe.wait_ge(adapter_hidden_ready.sem, adapter_hidden_ready.at((s, p, NB - 1)))
                    for k in range(NT):
                        nc.tensor.matmul(bank[:, k * P:(k + 1) * P], xnT[:, k * P:(k + 1) * P], w_base[:],
                                         start=True, stop=False)
                        ins = nc.tensor.matmul(bank[:, k * P:(k + 1) * P], aT[:, k * P:(k + 1) * P],
                                               w_sel[0:R + 1, k // 2, R:R + D], start=False, stop=True)
                    ins.then_inc(small_bank_filled.sem, 1)

                do = {"S": scores, "T": turn_probs, "PV": weigh_values, "D": spread_positions, "OB": turn_back,
                      "OT": turn_out, "OP": project_out, "xt": turn_xn, "v": project_v, "h": hidden,
                      "rec": reconstruct, "loss": sum_losses, "act": adapter_down, "ffo": ffn_out}
                for kind, *key in plan:
                    if kind in ("q", "k"):
                        project(kind, *key)
                    elif kind == "att":
                        if key[1] < POS:
                            position_terms(*key)
                    elif kind in do:
                        do[kind](*key)

            @block.scalar
            def _(act):
                def copy_xt(s, p):
                    bank = small_bank("xt", s, p)
                    act.wait_ge(small_bank_filled.sem, small_bank_filled.at(("xt", s, p)))
                    last = before(turns, (s, p))
                    if last:
                        job = ("v",) + last if last[0] in "ab" else ("ffo",) + last
                        act.wait_ge(small_bank_filled.sem, small_bank_filled.at(job))
                    nc.scalar.copy(xnT[:], bank[:]).then_inc(xnT_ready.sem, 1)

                def copy_qk(which, L, p):
                    bank = small_bank(which, L, p)
                    n = "qk".index(which)
                    act.wait_ge(small_bank_filled.sem, small_bank_filled.at((which, L, p)))
                    last = before(fronts, (L, p))
                    if L == "a":
                        if last:
                            act.wait_ge(rest_ready.sem, rest_ready.at(last + (NB - 1,)))
                        if last_ffn_before[L, p]:
                            act.wait_ge(small_bank_filled.sem, small_bank_filled.at(("rec",) + last_ffn_before[L, p] + (NE - 1,)))
                        nc.scalar.activation(qk[:, n, :], bank[:], ACT.Identity,
                                             bias=(bq, bk)[n]["a"][:]).then_inc(qk_ready_a.sem, 1)
                    else:
                        if n == 0:
                            act.wait_ge(v_ready.sem, v_ready.at(last))
                        elif last_ffn_before[L, p]:
                            act.wait_ge(small_bank_filled.sem, small_bank_filled.at(("xt",) + last_ffn_before[L, p]))
                        nc.scalar.activation(plain[:, n, :], bank[:], ACT.Identity,
                                             bias=(bq, bk)[n]["b"][:]).then_inc(plain_ready.sem, 1)

                def split1(L, p):
                    for b in range(NB):
                        cols = slice(b * SEQ, (b + 1) * SEQ)
                        ready = qk_ready_a if L == "a" else qk_ready_b
                        act.wait_ge(ready.sem, ready.at((p, 1)))
                        if before(fronts, (L, p)):
                            act.wait_ge(parts_stored[b].sem, parts_stored[b].at(before(fronts, (L, p)) + (PARTS,)))
                        if L == "b" and b == 0:
                            for n in range(POS - POS_BUFS, POS):
                                stored = pos_parts_stored[n % POS_BUFS]
                                act.wait_ge(stored.sem, stored.at((p, n)))
                        nc.scalar.copy(qk_parts[:, 0, :, cols], qk[:, :, cols]).then_inc(part1_ready.sem, 1)

                def split2(L, p):
                    for b in range(NB):
                        cols = slice(b * SEQ, (b + 1) * SEQ)
                        act.wait_ge(rest_ready.sem, rest_ready.at((L, p, b)))
                        nc.scalar.copy(qk_parts[:, 1, :, cols], rest[:, :, cols]).then_inc(part2_ready.sem, 1)

                def position_part1(p, n):
                    bank = small_bank("att", p, n)
                    act.wait_ge(small_bank_filled.sem, small_bank_filled.at(("att", p, n)))
                    if n >= POS_BUFS:
                        act.wait_ge(pos_parts_stored[n % POS_BUFS].sem, pos_parts_stored[n % POS_BUFS].at((p, n - POS_BUFS)))
                    elif n == 0:
                        for b in range(NB):
                            act.wait_ge(parts_stored[b].sem, parts_stored[b].at(before(fronts, ("b", p)) + (PARTS,)))
                    nc.scalar.copy(att_parts[:, n % POS_BUFS, 0], bank[:].rearrange("p (g t) -> p g t", g=2)).then_inc(pos_part1_ready.sem, 1)

                def position_part2(p, n):
                    act.wait_ge(pos_rest_ready.sem, pos_rest_ready.at((p, n)))
                    nc.scalar.copy(att_parts[:, n % POS_BUFS, 1], pos_rest[:, n % 2]).then_inc(pos_part2_ready.sem, 1)

                def spread_out(p, qt, c, j):
                    earlier = chunk_before_half[p, qt] + (1,)
                    act.wait_ge(score_bank_filled.sem, score_bank_filled.at(("S",) + earlier))
                    if earlier[0] == "b":
                        act.wait_ge(scores_summed.sem, scores_summed.at(earlier))
                    act.wait_ge(score_bank_filled.sem, score_bank_filled.at(("D", p, qt, c, j, 1)))
                    nc.scalar.copy(*spread_views((p, qt, c, j), 1)).then_inc(spread_by_act.sem, 1)

                def exps(L, p, i):
                    g = NUMBER[L, p, i]
                    n = g // HC
                    scale = SCALE_A if L == "a" else SCALE_B
                    if i % HC == 0 and n >= 2:
                        act.wait_ge(inverse_ready.sem, inverse_ready.at(n - 2))
                    for half in range(2):
                        bank = score_bank(("S", L, p, i, half))[:].rearrange("p (k t) -> p k t", k=2)
                        act.wait_ge(exp_bias_ready.sem, exp_bias_ready.at((L, p, i, half)))
                        if L == "a" and g >= 2:
                            act.wait_ge(probs_turned.sem, probs_turned.at(CHUNKS[g - 2] + (half,)))
                        for k in (2 * half, 2 * half + 1):
                            h = (i % HC) * HC + k
                            ins = nc.scalar.activation(prob[:, g % 2, k, :],
                                                       bank[:, k % 2, :] if L == "a" else prob[:, g % 2, k, :], ACT.Exp,
                                                       bias=nbias[:, g % 2, k:k + 1], scale=scale,
                                                       accum_out=rsum[:, n % 2, h:h + 1])
                        ins.then_inc(probs_ready.sem, 1)

                def move_probs(L, p, i):
                    g = NUMBER[L, p, i]
                    for hh in range(2):
                        if t_engine((L, p, i), hh) == "act":
                            act.wait_ge(probs_turned.sem, probs_turned.at((L, p, i, hh)))
                            if g >= 2:
                                act.wait_ge(values_weighed.sem, values_weighed.at(CHUNKS[g - 2]))
                            nc.scalar.copy(probT[:, g % 2, 2 * hh:2 * hh + 2],
                                           ps_t[hh][:].rearrange("p (a b c) -> p a b c", a=2, b=2)).then_inc(moved_by["act"].sem, 1)

                def move_out(n):
                    act.wait_ge(values_weighed.sem, values_weighed.at(last_chunk_of_group(n)))
                    if n:
                        act.wait_ge(small_bank_filled.sem, small_bank_filled.at(("OB", n - 1)))
                    nc.scalar.copy(o_turned[:].rearrange("p c t -> p (c t)"), ps_o[:]).then_inc(out_moved.sem, 1)

                def copy_out(n):
                    bank = small_bank("OT", n)
                    act.wait_ge(small_bank_filled.sem, small_bank_filled.at(("OT", n)))
                    if n:
                        act.wait_ge(small_bank_filled.sem, small_bank_filled.at(("OP", n - 1)))
                    nc.scalar.copy(oT[:], bank[:, 0:P]).then_inc(outT_ready.sem, 1)

                def hidden(s, p, j):
                    bank = small_bank("h", s, p, j)
                    if j == 0:
                        act.wait_ge(rest_ready.sem, rest_ready.at(last_front_before[s, p] + (NB - 1,)))
                        if last_ffn_before[s, p]:
                            act.wait_ge(small_bank_filled.sem, small_bank_filled.at(("rec",) + last_ffn_before[s, p] + (NE - 1,)))
                    act.wait_ge(small_bank_filled.sem, small_bank_filled.at(("h", s, p, j)))
                    nc.scalar.activation(hT[:, j, :], bank[:], ACT.Relu, bias=bd1[:, j:j + 1]).then_inc(hidden_ready.sem, 1)

                def square(s, p, e):
                    act.wait_ge(diff_ready.sem, diff_ready.at((s, p, e)))
                    for b in range(NB):
                        d = diff[:, e % 2, b * SEQ:(b + 1) * SEQ]
                        ins = nc.scalar.activation(d, d, ACT.Square, bias=bd2[:, e:e + 1],
                                                   accum_out=loss_p[:, b, e:e + 1])
                    ins.then_inc(losses_ready.sem, 1)

                def adapter_hidden(s, p):
                    bank = small_bank("act", s, p)
                    act.wait_ge(small_bank_filled.sem, small_bank_filled.at(("act", s, p)))
                    for b in range(NB):
                        cols = slice(b * SEQ, (b + 1) * SEQ)
                        nc.scalar.activation(aT[0:R, cols], bank[0:R, cols], ACT.Relu,
                                             bias=w_sel[0:R, b, R + D:SELW]).then_inc(adapter_hidden_ready.sem, 1)

                do = {"S": exps, "T": move_probs, "OM": move_out, "OT": copy_out, "D": spread_out, "xt": copy_xt,
                      "split1": split1, "split2": split2, "att_late": position_part2, "h": hidden,
                      "square": square, "act": adapter_hidden}
                for kind, *key in plan:
                    if kind in ("q", "k"):
                        copy_qk(kind, *key)
                    elif kind == "att":
                        if key[1] < POS:
                            position_part1(*key)
                    elif kind in do:
                        do[kind](*key)

            @block.vector
            def _(dve):
                def norm1(s, p):
                    src = xn[:, p % 2] if s == "n" else x[:, p]
                    if s in "fn":
                        dve.wait_ge(residual_added.sem, residual_added.at(NUMBER["a" if s == "f" else "b", p, NCH - 1] // HC))
                    elif s == "b":
                        dve.wait_ge(ffn_added.sem, ffn_added.at(("f", p)))
                    elif s == "g":
                        dve.wait_ge(inner_norm_step.sem, inner_norm_step.at((p, 1)))
                    last = before(norms, (s, p))
                    if last:
                        dve.wait_ge(normed.sem, normed.at(last + (NT - 1,)))
                    for k in range(NT):
                        nc.vector.bn_stats(stats[:, k, :], src[:, k, :]).then_inc(stats_done.sem, 1)
                    for k in range(NT):
                        dve.wait_ge(stats_done.sem, stats_done.at((s, p, k)))
                        nc.vector.bn_aggr(mv[:, k, :], stats[:, k, :]).then_inc(stats_done.sem, 1)
                    dve.wait_ge(stats_done.sem, stats_done.at((s, p, 2 * NT - 1)))
                    nc.vector.tensor_scalar(ve[:], mv[:, :, 1], EPS_B if s == "n" else EPS_LN, None,
                                            ALU.add).then_inc(variance_done.sem, 1)

                def norm2(s, p):
                    src = xn[:, p % 2] if s == "n" else x[:, p]
                    dst = ffn_xn if s in "fg" else xn[:, p % 2]
                    dve.wait_ge(root_done.sem, root_done.at((s, p)))
                    if s == "a" and p >= 2:
                        dve.wait_ge(small_bank_filled.sem, small_bank_filled.at(("xt", "a", p - 2)))
                    elif s == "b" and p >= 2:
                        dve.wait_ge(inner_norm_step.sem, inner_norm_step.at((p - 2, 1)))
                    elif s == "b":
                        dve.wait_ge(small_bank_filled.sem, small_bank_filled.at(
                            ("xt", "a", PAIRS - 2 + (PAIRS + p) % 2)))
                    elif s in "fg":
                        if last_front_before[s, p][0] == "b":
                            dve.wait_ge(small_bank_filled.sem, small_bank_filled.at(("att", last_front_before[s, p][1], POS - 1)))
                            dve.wait_ge(qk_ready_b.sem, qk_ready_b.at((last_front_before[s, p][1], 1)))
                        if last_ffn_before[s, p]:
                            dve.wait_ge(small_bank_filled.sem, small_bank_filled.at(("xt",) + last_ffn_before[s, p]))
                    for k in range(NT):
                        nc.vector.tensor_scalar(dst[:, k, :], src[:, k, :], mv[:, k, 0:1], rstd[:, k:k + 1],
                                                ALU.subtract, ALU.mult).then_inc(normed.sem, 1)

                def inner(p):
                    y = xn[:, p % 2]
                    dve.wait_ge(normed.sem, normed.at(("n", p, NT - 1)))
                    nc.vector.tensor_tensor(
                        y, y, ln_s[:].rearrange("p (u n) -> p u n", u=1).to_broadcast([P, NT, D]), ALU.mult).then_inc(inner_norm_step.sem, 1)
                    dve.wait_ge(inner_norm_step.sem, inner_norm_step.at((p, 0)))
                    dve.wait_ge(bias_added.sem, bias_added.at(("n", p)))
                    nc.vector.tensor_tensor(x[:, p], x[:, p], y, ALU.add).then_inc(inner_norm_step.sem, 1)

                def take_v(L, p):
                    bank = small_bank("v", L, p)
                    dve.wait_ge(small_bank_filled.sem, small_bank_filled.at(("v", L, p)))
                    last = before(fronts, (L, p))
                    if last:
                        dve.wait_ge(v_ready.sem, v_ready.at(last))
                    if L == "b":
                        dve.wait_ge(small_bank_filled.sem, small_bank_filled.at(("att", p, POS // 2 - 1)))
                        dve.wait_ge(qk_ready_b.sem, qk_ready_b.at((p, 0)))
                    nc.vector.tensor_tensor(
                        new_v, bank[:].rearrange("p (t h d) -> p t h d", t=NT, h=NH),
                        bv[L][:].rearrange("p (u h d) -> p u h d", u=1, h=NH).to_broadcast([P, NT, NH, DH]),
                        ALU.add).then_inc(new_v_ready.sem, 1)

                def position_rest(p, n):
                    bank = small_bank("att", p, n)
                    dve.wait_ge(pos_part1_ready.sem, pos_part1_ready.at((p, n)))
                    if n >= 2:
                        dve.wait_ge(pos_part3_ready.sem, pos_part3_ready.at((p, n - 2)))
                        dve.wait_ge(pos_part2_ready.sem, pos_part2_ready.at((p, n - 2)))
                    elif n == 0:
                        last = before(fronts, ("b", p))
                        dve.wait_ge(part3_ready.sem, part3_ready.at(last + (NB - 1,)))
                        dve.wait_ge(part2_ready.sem, part2_ready.at(last + (NB - 1,)))
                        if last_ffn_before["b", p]:
                            dve.wait_ge(losses_ready.sem, losses_ready.at(last_ffn_before["b", p] + (NE - 1,)))
                    nc.vector.tensor_tensor(pos_rest[:, n % 2], bank[:].rearrange("p (g t) -> p g t", g=2),
                                            att_parts[:, n % POS_BUFS, 0], ALU.subtract).then_inc(pos_rest_ready.sem, 1)

                def spread_out(p, qt, c, j):
                    earlier = chunk_before_half[p, qt] + (1,)
                    dve.wait_ge(score_bank_filled.sem, score_bank_filled.at(("S",) + earlier))
                    if earlier[0] == "b":
                        dve.wait_ge(scores_summed.sem, scores_summed.at(earlier))
                    dve.wait_ge(score_bank_filled.sem, score_bank_filled.at(("D", p, qt, c, j, 0)))
                    nc.vector.tensor_copy(*spread_views((p, qt, c, j), 0)).then_inc(spread_by_dve.sem, 1)

                def maxima(L, p, i):
                    g = NUMBER[L, p, i]
                    _, _, b, qt = group(g // HC)
                    if L == "b" and i % (NCH // 2) == 0:
                        dve.wait_ge(spread_by_act.sem, spread_by_act.at((p, qt, "p", DJ - 1)))
                        dve.wait_ge(spread_by_dve.sem, spread_by_dve.at((p, qt, "p", DJ - 1)))
                    for half in range(2):
                        key, heads = (L, p, i, half), slice(2 * half, 2 * half + 2)
                        bank = score_bank(("S",) + key)[:].rearrange("p (k t) -> p k t", k=2)
                        dve.wait_ge(score_bank_filled.sem, score_bank_filled.at(("S",) + key))
                        if L == "a":
                            nc.vector.tensor_reduce(nmax[:, g % 2, heads], bank, AX.X, ALU.max).then_inc(max_ready.sem, 1)
                            dve.wait_ge(max_ready.sem, max_ready.at(key))
                        else:
                            dve.wait_ge(probs_turned.sem, probs_turned.at(CHUNKS[g - 2] + (half,)))
                            for k in range(2):
                                h = (i % HC) * HC + 2 * half + k
                                ins = nc.vector.tensor_tensor_reduce(
                                    out=prob[:, g % 2, 2 * half + k, :], in0=bank[:, k, :], in1=p2c[:, b * NH + h, :],
                                    scale=1.0, scalar=-3.4e38, op0=ALU.add, op1=ALU.max,
                                    accum_out=nmax[:, g % 2, 2 * half + k:2 * half + k + 1])
                            ins.then_inc(scores_summed.sem, 1)
                            dve.wait_ge(scores_summed.sem, scores_summed.at(key))
                        scale = SCALE_A if L == "a" else SCALE_B
                        nc.vector.tensor_scalar(nbias[:, g % 2, heads], nmax[:, g % 2, heads], -scale, None,
                                                ALU.mult).then_inc(exp_bias_ready.sem, 1)

                def move_probs(L, p, i):
                    g = NUMBER[L, p, i]
                    for hh in range(2):
                        if t_engine((L, p, i), hh) == "dve":
                            dve.wait_ge(probs_turned.sem, probs_turned.at((L, p, i, hh)))
                            if g >= 2:
                                dve.wait_ge(values_weighed.sem, values_weighed.at(CHUNKS[g - 2]))
                            nc.vector.tensor_copy(probT[:, g % 2, 2 * hh:2 * hh + 2],
                                                  ps_t[hh][:].rearrange("p (a b c) -> p a b c", a=2, b=2)).then_inc(moved_by["dve"].sem, 1)

                def normalize(n):
                    bank = small_bank("OB", n)
                    dve.wait_ge(probs_ready.sem, probs_ready.at(last_chunk_of_group(n) + (1,)))
                    nc.vector.reciprocal(rinv[:, n % 2, :], rsum[:, n % 2, :]).then_inc(inverse_ready.sem, 1)
                    dve.wait_ge(small_bank_filled.sem, small_bank_filled.at(("OB", n)))
                    dve.wait_ge(inverse_ready.sem, inverse_ready.at(n))
                    if n:
                        dve.wait_ge(small_bank_filled.sem, small_bank_filled.at(("OT", n - 1)))
                    nc.vector.tensor_tensor(
                        o_sb[:], bank[:].rearrange("p (h e) -> p h e", e=VC)[:, :, 0:DH],
                        rinv[:, n % 2, :].rearrange("p (h u) -> p h u", u=1).to_broadcast([P, NH, DH]),
                        ALU.mult).then_inc(heads_out_ready.sem, 1)

                def add_out(n):
                    bank = small_bank("OP", n)
                    L, p, b, qt = group(n)
                    dst = (x[:, p] if L == "a" else xn[:, p % 2])[:, 2 * b + qt, :]
                    dve.wait_ge(bias_added.sem, bias_added.at((L, p)))
                    dve.wait_ge(small_bank_filled.sem, small_bank_filled.at(("OP", n)))
                    nc.vector.tensor_tensor(dst, bank[:, 0:P], dst, ALU.add).then_inc(residual_added.sem, 1)

                def difference(s, p, e):
                    bank = small_bank("rec", s, p, e)
                    dve.wait_ge(small_bank_filled.sem, small_bank_filled.at(("rec", s, p, e)))
                    if e >= 2:
                        dve.wait_ge(losses_ready.sem, losses_ready.at((s, p, e - 2)))
                    elif e == 0:
                        dve.wait_ge(xnT_ready.sem, xnT_ready.at((s, p)))
                        dve.wait_ge(part3_ready.sem, part3_ready.at(last_front_before[s, p] + (NB - 1,)))
                        dve.wait_ge(part2_ready.sem, part2_ready.at(last_front_before[s, p] + (NB - 1,)))
                        if last_ffn_before[s, p]:
                            dve.wait_ge(losses_ready.sem, losses_ready.at(last_ffn_before[s, p] + (NE - 1,)))
                    nc.vector.tensor_tensor(diff[:, e % 2], bank[:], xnT[:], ALU.subtract).then_inc(diff_ready.sem, 1)

                def choose(s, p):
                    bank = small_bank("loss", s, p)
                    loss = bank[:, 0:NB * NE].rearrange("p (b e) -> p b e", b=NB)
                    numbers = iota.rearrange("p (u e) -> p u e", u=1).to_broadcast([P, NB, NE])

                    def wide(a):
                        return a[:].rearrange("p (b u) -> p b u", u=1).to_broadcast([P, NB, NE])

                    dve.wait_ge(small_bank_filled.sem, small_bank_filled.at(("loss", s, p)))
                    nc.vector.tensor_reduce(lmin[:], loss, AX.X, ALU.min).then_inc(choice_step.sem, 1)
                    dve.wait_ge(choice_step.sem, choice_step.at((s, p, 0)))
                    nc.vector.tensor_tensor(lkey[:], loss, wide(lmin), ALU.is_gt).then_inc(choice_step.sem, 1)
                    dve.wait_ge(choice_step.sem, choice_step.at((s, p, 1)))
                    nc.vector.scalar_tensor_tensor(out=lkey[:], in0=lkey[:], scalar=float(NE), in1=numbers,
                                                   op0=ALU.mult, op1=ALU.add).then_inc(choice_step.sem, 1)
                    dve.wait_ge(choice_step.sem, choice_step.at((s, p, 2)))
                    nc.vector.tensor_reduce(kmin[:], lkey[:], AX.X, ALU.min).then_inc(choice_step.sem, 1)
                    dve.wait_ge(choice_step.sem, choice_step.at((s, p, 3)))
                    nc.vector.tensor_tensor(onehot[:], numbers, wide(kmin), ALU.is_equal).then_inc(choice_step.sem, 1)

                def pick(s, p, n):
                    dve.wait_ge(choice_step.sem, choice_step.at((s, p, 4)))
                    if n == 0 and last_ffn_before[s, p]:
                        dve.wait_ge(small_bank_filled.sem, small_bank_filled.at(("ffo",) + last_ffn_before[s, p]))
                        dve.wait_ge(adapter_hidden_ready.sem, adapter_hidden_ready.at(last_ffn_before[s, p] + (NB - 1,)))
                    for e in (2 * n, 2 * n + 1):
                        for b in range(NB):
                            if e == 0:
                                nc.vector.tensor_scalar(w_sel[:, b, :], w_all[:, e, :], onehot[:, b, e:e + 1], None,
                                                        ALU.mult).then_inc(expert_added.sem, 1)
                            else:
                                dve.wait_ge(expert_added.sem, expert_added.at((s, p, b, e - 1)))
                                nc.vector.scalar_tensor_tensor(
                                    out=w_sel[:, b, :], in0=w_all[:, e, :], scalar=onehot[:, b, e:e + 1],
                                    in1=w_sel[:, b, :], op0=ALU.mult, op1=ALU.add).then_inc(expert_added.sem, 1)

                def add_ffn(s, p):
                    bank = small_bank("ffo", s, p)
                    dve.wait_ge(small_bank_filled.sem, small_bank_filled.at(("ffo", s, p)))
                    nc.vector.tensor_tensor(
                        x[:, p], x[:, p], bank[:].rearrange("p (t n) -> p t n", t=NT), ALU.add).then_inc(ffn_added.sem, 1)

                do = {"S": maxima, "T": move_probs, "D": spread_out, "OB": normalize, "OP": add_out,
                      "norm1": norm1, "norm2": norm2, "inner": inner, "v": take_v, "rec": difference,
                      "loss": choose, "pick": pick, "ffo": add_ffn}
                for kind, *key in plan:
                    if kind == "att":
                        if key[1] < POS:
                            position_rest(*key)
                    elif kind in do:
                        do[kind](*key)

            @block.gpsimd
            def _(pool):
                def root(s, p):
                    if s == "n":
                        pool.wait_ge(normed.sem, normed.at(("b", p, NT - 1)))
                        nc.gpsimd.tensor_tensor(
                            x[:, p], x[:, p], ln_b[:].rearrange("p (u n) -> p u n", u=1).to_broadcast([P, NT, D]),
                            ALU.add).then_inc(bias_added.sem, 1)
                    pool.wait_ge(variance_done.sem, variance_done.at((s, p)))
                    nc.gpsimd.tensor_tensor(rstd[:], ve[:], neg_half[:], ALU.pow).then_inc(root_done.sem, 1)

                def add_bias(s, p):
                    if s in "ab":
                        pool.wait_ge(normed.sem, normed.at((s, p, NT - 1)))
                        pool.wait_ge(small_bank_filled.sem, small_bank_filled.at(("xt", s, p)))
                        dst = x[:, p] if s == "a" else xn[:, p % 2]
                        nc.gpsimd.tensor_tensor(
                            dst, dst, bo[s][:].rearrange("p (u n) -> p u n", u=1).to_broadcast([P, NT, D]),
                            ALU.add).then_inc(bias_added.sem, 1)

                def add_centre(which, L, p):
                    if L == "b":
                        n = "qk".index(which)
                        pool.wait_ge(plain_ready.sem, plain_ready.at((p, n)))
                        pool.wait_ge(part1_ready.sem, part1_ready.at(before(fronts, (L, p)) + (NB - 1,)))
                        pool.wait_ge(rest_ready.sem, rest_ready.at(before(fronts, (L, p)) + (NB - 1,)))
                        if last_ffn_before[L, p]:
                            pool.wait_ge(small_bank_filled.sem, small_bank_filled.at(("rec",) + last_ffn_before[L, p] + (NE - 1,)))
                        nc.gpsimd.tensor_scalar(qk[:, n, :], plain[:, n, :], centre[:, n:n + 1], None,
                                                ALU.add).then_inc(qk_ready_b.sem, 1)

                def take_rests(L, p):
                    for b in range(NB):
                        cols = slice(b * SEQ, (b + 1) * SEQ)
                        pool.wait_ge(part1_ready.sem, part1_ready.at((L, p, b)))
                        if b == 0:
                            if before(fronts, (L, p)):
                                pool.wait_ge(part2_ready.sem, part2_ready.at(before(fronts, (L, p)) + (NB - 1,)))
                                pool.wait_ge(part3_ready.sem, part3_ready.at(before(fronts, (L, p)) + (NB - 1,)))
                            if last_ffn_before[L, p]:
                                pool.wait_ge(losses_ready.sem, losses_ready.at(last_ffn_before[L, p] + (NE - 1,)))
                            if L == "b":
                                pool.wait_ge(pos_part2_ready.sem, pos_part2_ready.at((p, POS - 1)))
                                pool.wait_ge(pos_part3_ready.sem, pos_part3_ready.at((p, POS - 1)))
                        nc.gpsimd.tensor_tensor(rest[:, :, cols], qk[:, :, cols], qk_parts[:, 0, :, cols],
                                                ALU.subtract).then_inc(rest_ready.sem, 1)

                def take_part3(L, p):
                    for b in range(NB):
                        cols = slice(b * SEQ, (b + 1) * SEQ)
                        pool.wait_ge(part2_ready.sem, part2_ready.at((L, p, b)))
                        pool.wait_ge(rest_ready.sem, rest_ready.at((L, p, b)))
                        nc.gpsimd.tensor_tensor(qk_parts[:, 2, :, cols], rest[:, :, cols],
                                                qk_parts[:, 1, :, cols], ALU.subtract).then_inc(part3_ready.sem, 1)

                def position_part3(p, n):
                    pool.wait_ge(pos_part2_ready.sem, pos_part2_ready.at((p, n)))
                    pool.wait_ge(pos_rest_ready.sem, pos_rest_ready.at((p, n)))
                    nc.gpsimd.tensor_tensor(att_parts[:, n % POS_BUFS, 2], pos_rest[:, n % 2], att_parts[:, n % POS_BUFS, 1],
                                            ALU.subtract).then_inc(pos_part3_ready.sem, 1)

                def copy_v(L, p):
                    pool.wait_ge(new_v_ready.sem, new_v_ready.at((L, p)))
                    g = NUMBER[L, p, 0]
                    if g:
                        pool.wait_ge(values_weighed.sem, values_weighed.at(CHUNKS[g - 1]))
                    nc.gpsimd.tensor_copy(v[:, :, :, 0:DH], new_v).then_inc(v_ready.sem, 1)

                do = {"norm1": root, "xt": add_bias, "split1": take_rests, "split2": take_part3,
                      "att_late": position_part3, "v_copy": copy_v}
                for kind, *key in plan:
                    if kind in ("q", "k"):
                        add_centre(kind, *key)
                    elif kind in do:
                        do[kind](*key)


def kernel(**inputs):
    import numpy as _np
    import concourse.bacc as _bacc
    from concourse import mybir as _mybir
    from concourse.bass_utils import run_bass_kernel_spmd as _run

    nc = _bacc.Bacc("TRN2", target_bir_lowering=False, num_devices=1, dynamic_dma_scratch_size=1024)
    arrays = {name: _np.ascontiguousarray(a) for name, a in inputs.items() if name != "L0_attn_b_attention_mask"}
    arrays["constants"] = constant_table()
    aps = {n: nc.dram_tensor(n, a.shape, _mybir.dt.from_np(a.dtype), kind="ExternalInput").ap()
           for n, a in arrays.items()}
    aps["out"] = nc.dram_tensor("out", inputs["L0_attn_a_x"].shape, _mybir.dt.float32, kind="ExternalOutput").ap()
    build(nc, aps)
    return _run(nc, [arrays], core_ids=[0]).results[0]["out"]
```
